# Optimizing a Trainium2 kernel written in Bass

```python
import numpy as np
import jax
import jax.numpy as jnp

def _softmax(x, axis=-1):
    return jax.nn.softmax(x, axis=axis)

def _gelu(x):
    return jax.nn.gelu(x, approximate=True)

def _silu(x):
    return jax.nn.silu(x)

def _sigmoid(x):
    return jax.nn.sigmoid(x)

def _layernorm(x, axis=-1, eps=1e-05):
    m = jnp.mean(x, axis=axis, keepdims=True)
    v = jnp.var(x, axis=axis, keepdims=True)
    return (x - m) / jnp.sqrt(v + eps)

def _scatter_add(tgt, idx, src, axis=0):
    return tgt.at[idx].add(src)

def _segment_sum(src, seg, n):
    return jax.ops.segment_sum(src, seg, n)
kernel_name = 'mk_audio_tower_d1_tok_audfeat768_r4_4d8de6'

def setup_inputs(seed: int=0):
    np.random.seed(seed)
    _w = jnp.asarray

    def _rec_inputs():
        import jax
        import jax.numpy as jnp
        _rk = jax.random.key(seed)
        x = -4.65018e-05 + 0.999886 * jax.random.normal(jax.random.fold_in(_rk, 1), (64, 125, 192), jnp.float32)
        return x
    x = _rec_inputs()

    def _L0_tok_setup():
        import jax, jax.numpy as jnp
        import numpy as np
        POOL_SIZE = 2
        STRIDE = 2
        CHANNELS = 192
        key = jax.random.key(seed)
        k1, = jax.random.split(key, 1)
        x = jax.random.normal(k1, (8, 2048, CHANNELS), dtype=jnp.float32)
        w = jnp.eye(CHANNELS, dtype=jnp.float32) * 2.0
        return {'x': x, 'w': w}
    _L0_tok_all = _L0_tok_setup()
    _L0_tok_in = {k: v for k, v in _L0_tok_all.items() if k in ('w',)}
    del _L0_tok_all

    def _L0_attn_setup():
        import jax, jax.numpy as jnp
        import numpy as np
        B, N, C, H = (8, 256, 192, 12)
        D = C // H
        SCALE = D ** (-0.5)
        key = jax.random.key(seed)
        ks = jax.random.split(key, 5)
        s = lambda k, sh, fan: jax.random.normal(k, sh, jnp.float32) * fan ** (-0.5)
        return {'x': jax.random.normal(ks[0], (B, N, C), jnp.float32), 'w_qkv': s(ks[1], (C, 3 * C), C), 'b_qkv': jnp.zeros((3 * C,), jnp.float32), 'w_l': s(ks[2], (H, H), H), 'b_l': jnp.zeros((H,), jnp.float32), 'w_w': s(ks[3], (H, H), H), 'b_w': jnp.zeros((H,), jnp.float32), 'w_proj': s(ks[4], (C, C), C), 'b_proj': jnp.zeros((C,), jnp.float32)}
    _L0_attn_all = _L0_attn_setup()
    _L0_attn_in = {k: v for k, v in _L0_attn_all.items() if k in ('w_qkv', 'b_qkv', 'w_l', 'b_l', 'w_w', 'b_w', 'w_proj', 'b_proj')}
    del _L0_attn_all

    def _L0_ffn_setup():
        import math
        import jax, jax.numpy as jnp
        import numpy as np
        B, L, D = (8, 1024, 192)
        E = 16
        TOP_K = 2
        F_EXP = 4 * D
        F_SH = F_EXP * 2 // 4
        key = jax.random.key(seed)
        ks = jax.random.split(key, 8)
        s = lambda fan_in: 1.0 / math.sqrt(fan_in)
        return {'hidden_states': jax.random.normal(ks[0], (B, L, D), jnp.float32), 'gate_weight': jax.random.uniform(ks[1], (E, D), jnp.float32, -s(D), s(D)), 'Wg': jax.random.uniform(ks[2], (E, F_EXP, D), jnp.float32, -s(D), s(D)), 'Wu': jax.random.uniform(ks[3], (E, F_EXP, D), jnp.float32, -s(D), s(D)), 'Wd': jax.random.uniform(ks[4], (E, D, F_EXP), jnp.float32, -s(F_EXP), s(F_EXP)), 'Ws_g': jax.random.uniform(ks[5], (F_SH, D), jnp.float32, -s(D), s(D)), 'Ws_u': jax.random.uniform(ks[6], (F_SH, D), jnp.float32, -s(D), s(D)), 'Ws_d': jax.random.uniform(ks[7], (D, F_SH), jnp.float32, -s(F_SH), s(F_SH))}
    _L0_ffn_all = _L0_ffn_setup()
    _L0_ffn_in = {k: v for k, v in _L0_ffn_all.items() if k in ('gate_weight', 'Wg', 'Wu', 'Wd', 'Ws_g', 'Ws_u', 'Ws_d')}
    del _L0_ffn_all
    return {'x': x, 'L0_tok_w': _L0_tok_in['w'], 'L0_attn_w_qkv': _L0_attn_in['w_qkv'], 'L0_attn_b_qkv': _L0_attn_in['b_qkv'], 'L0_attn_w_l': _L0_attn_in['w_l'], 'L0_attn_b_l': _L0_attn_in['b_l'], 'L0_attn_w_w': _L0_attn_in['w_w'], 'L0_attn_b_w': _L0_attn_in['b_w'], 'L0_attn_w_proj': _L0_attn_in['w_proj'], 'L0_attn_b_proj': _L0_attn_in['b_proj'], 'L0_ffn_gate_weight': _L0_ffn_in['gate_weight'], 'L0_ffn_Wg': _L0_ffn_in['Wg'], 'L0_ffn_Wu': _L0_ffn_in['Wu'], 'L0_ffn_Wd': _L0_ffn_in['Wd'], 'L0_ffn_Ws_g': _L0_ffn_in['Ws_g'], 'L0_ffn_Ws_u': _L0_ffn_in['Ws_u'], 'L0_ffn_Ws_d': _L0_ffn_in['Ws_d']}

def reference(x, L0_tok_w, L0_attn_w_qkv, L0_attn_b_qkv, L0_attn_w_l, L0_attn_b_l, L0_attn_w_w, L0_attn_b_w, L0_attn_w_proj, L0_attn_b_proj, L0_ffn_gate_weight, L0_ffn_Wg, L0_ffn_Wu, L0_ffn_Wd, L0_ffn_Ws_g, L0_ffn_Ws_u, L0_ffn_Ws_d):
    import jax
    import jax.numpy as jnp

    def _L0_tok_ref(x, w):
        import jax, jax.numpy as jnp
        import numpy as np
        POOL_SIZE = 2
        STRIDE = 2
        CHANNELS = 192
        B, S, C = x.shape
        n_windows = (S - POOL_SIZE) // STRIDE + 1
        window = jnp.stack([x[:, i::STRIDE, :][:, :n_windows, :] for i in range(POOL_SIZE)], axis=2)
        scores = jnp.einsum('bnpc,cd->bnpd', window, w)
        weights = jax.nn.softmax(scores, axis=2)
        return jnp.sum(weights * window, axis=2)

    def _L0_attn_ref(x, w_qkv, b_qkv, w_l, b_l, w_w, b_w, w_proj, b_proj):
        import jax, jax.numpy as jnp
        import numpy as np
        B, N, C, H = (8, 256, 192, 12)
        D = C // H
        SCALE = D ** (-0.5)
        Bq, Nq, Cq = x.shape
        qkv = (x @ w_qkv + b_qkv).reshape(Bq, Nq, 3, H, D).transpose(2, 0, 3, 1, 4)
        q, k, v = (qkv[0] * SCALE, qkv[1], qkv[2])
        attn = jnp.einsum('bhnd,bhmd->bhnm', q, k)
        attn = jnp.einsum('bhnm,hg->bgnm', attn, w_l) + b_l[None, :, None, None]
        attn = jax.nn.softmax(attn, axis=-1)
        attn = jnp.einsum('bhnm,hg->bgnm', attn, w_w) + b_w[None, :, None, None]
        out = jnp.einsum('bhnm,bhmd->bnhd', attn, v).reshape(Bq, Nq, Cq)
        return out @ w_proj + b_proj

    def _L0_ffn_ref(hidden_states, gate_weight, Wg, Wu, Wd, Ws_g, Ws_u, Ws_d):
        import math
        import jax, jax.numpy as jnp
        import numpy as np
        B, L, D = (8, 1024, 192)
        E = 16
        TOP_K = 2
        F_EXP = 4 * D
        F_SH = F_EXP * 2 // 4
        b, l, d = hidden_states.shape
        n = b * l
        x = hidden_states.reshape(n, d)
        scores = jax.nn.sigmoid(x @ gate_weight.T)
        capacity = math.ceil(n / E * TOP_K)
        topk_score, topk_ids = jax.lax.top_k(scores.T, capacity)
        xg = x[topk_ids]
        gate = jax.nn.silu(jnp.einsum('ecd,efd->ecf', xg, Wg))
        up = jnp.einsum('ecd,efd->ecf', xg, Wu)
        out = jnp.einsum('ecf,edf->ecd', gate * up, Wd)
        out = out * topk_score[..., None]
        y = jnp.zeros((n, d), x.dtype).at[topk_ids.reshape(-1)].add(out.reshape(-1, d))
        y = y.reshape(b, l, d)
        shared = jax.nn.silu(hidden_states @ Ws_g.T) * (hidden_states @ Ws_u.T) @ Ws_d.T
        return y + shared
    h = _L0_tok_ref(x, L0_tok_w)
    h = h + _L0_attn_ref(_layernorm(h, axis=-1), L0_attn_w_qkv, L0_attn_b_qkv, L0_attn_w_l, L0_attn_b_l, L0_attn_w_w, L0_attn_b_w, L0_attn_w_proj, L0_attn_b_proj)
    h = h + _L0_ffn_ref(_layernorm(h, axis=-1), L0_ffn_gate_weight, L0_ffn_Wg, L0_ffn_Wu, L0_ffn_Wd, L0_ffn_Ws_g, L0_ffn_Ws_u, L0_ffn_Ws_d)
    return h

_drawn_inputs = setup_inputs


def setup_inputs(seed=0):
    import zlib

    import numpy as np

    out = dict(_drawn_inputs(seed))
    spreads = {'L0_attn_b_qkv': (0.0, 0.1),
     'L0_attn_b_l': (0.0, 0.1),
     'L0_attn_b_w': (0.0, 0.1),
     'L0_attn_b_proj': (0.0, 0.1)}
    factors = {}
    for name, (base, spread) in spreads.items():
        noise = np.random.default_rng([zlib.crc32(name.encode()), seed]).standard_normal(out[name].shape)
        drawn = base * np.exp(spread * noise) if base else spread * noise
        out[name] = jnp.asarray(drawn.astype(out[name].dtype))
    for name, factor in factors.items():
        out[name] = (out[name] * factor).astype(out[name].dtype)
    return out
```

```python
from contextlib import ExitStack, contextmanager

import concourse.bass as bass
from concourse import mybir

ALU = mybir.AluOpType
ACT = mybir.ActivationFunctionType
AX = mybir.AxisListType
F32 = mybir.dt.float32
BF16 = mybir.dt.bfloat16
I32 = mybir.dt.int32
U32 = mybir.dt.uint32

BATCH, FRAMES, C = 64, 125, 192
POOL = 2
WIN = (FRAMES - POOL) // POOL + 1
HEADS = 12
HD = C // HEADS
EXPERTS = 16
F_EXP = 4 * C
F_SH = F_EXP // 2
TOKENS = BATCH * WIN
TOP_K = 2
CAP = -(-TOKENS * TOP_K // EXPERTS)
LN_EPS = 1e-5

KC = 2
HC = C // KC
SEQS = 2
TT = SEQS * WIN
TILES = TOKENS // TT
HALF = HEADS // 2
PAIRS = HEADS // 2
SECOND = 64
SP_ = SECOND + WIN
ROW = C + EXPERTS
GROUP = 4
GT = GROUP * TT
GROUPS = TILES // GROUP
FC_SH = F_SH // 128
FC_EXP = F_EXP // 128
SLOTS = CAP // GROUP
HI = CAP // 16
LO = 16
SEARCH_BITS = 32
SPREAD = GROUPS

LEAD, LOOP_FROM, LOOP_TO, LAST = -3, 4, 28, TILES + 3


def count_ge(eng, sem, value):
    if isinstance(value, int) and value <= 0:
        return
    eng.wait_ge(sem, value)


def live(i, off):
    return not isinstance(i, int) or 0 <= i + off < TILES


def upto(t, off):
    if isinstance(t, int):
        return min(t + off + 1, TILES)
    return t + (off + 1)


@contextmanager
def by_two(eng, start, end):
    with eng.Fori(0, (end - start) // 2) as half:
        yield half * 2 + start


def pipeline(eng, body):
    for i in range(LEAD, LOOP_FROM):
        body(i, i % 2)
    with by_two(eng, LOOP_FROM, LOOP_TO) as r:
        body(r, 0)
        body(r + 1, 1)
    for i in range(LOOP_TO, LAST):
        body(i, i % 2)


def audio_tower(nc, xT, xp, w_tok, w_qkv, b_qkv, w_l, b_l, w_w, b_w, w_proj, b_proj,
                w_gate, wg, wu, wd, wsg, wsu, wsd, out):
    out_rows = out.rearrange("b n c -> (b n) c")
    rows_dram = nc.dram_tensor("rows_scratch", (TOKENS, ROW), F32, kind="Internal").ap()
    score_dram = nc.dram_tensor("score_scratch", (EXPERTS, TOKENS), F32, kind="Internal").ap()
    ids_dram = nc.dram_tensor("ids_scratch", (EXPERTS, CAP), I32, kind="Internal").ap()

    with ExitStack() as ctx:
        ctx.enter_context(nc.allow_non_contiguous_dma(reason="layout of small tables"))

        def sb(name, shape, dt=F32, scope=ctx):
            return scope.enter_context(nc.sbuf_tensor(name, shape, dt))

        def sem(name):
            return ctx.enter_context(nc.semaphore(name))

        def sems(name, n=2):
            return [sem(f"{name}{i}") for i in range(n)]

        bank = [ctx.enter_context(nc.psum_tensor(f"bank{i}", [128, 512], F32)) for i in range(8)]

        ident = sb("ident", [128, 128])
        h_all = sb("h_all", [TT, TILES, C])
        hn2T = sb("hn2T", [HC, KC, TOKENS])
        w_gate_sb = sb("w_gate_sb", [HC, KC, EXPERTS])
        wsg_sb = sb("wsg_sb", [HC, KC, F_SH])
        wsu_sb = sb("wsu_sb", [HC, KC, F_SH])
        wsd_sb = sb("wsd_sb", [128, FC_SH, C])
        wg_sb = [sb(f"wg_sb{p}", [HC, KC, F_EXP]) for p in range(2)]
        wu_sb = [sb(f"wu_sb{p}", [HC, KC, F_EXP]) for p in range(2)]
        wd_sb = [sb(f"wd_sb{p}", [128, FC_EXP, C]) for p in range(2)]
        idx_all = sb("idx_all", [SLOTS, EXPERTS, GROUP], I32)

        att = ExitStack()
        w_tok_sb = sb("w_tok_sb", [HC, KC, C], scope=att)
        w_qkv_sb = sb("w_qkv_sb", [HC + 1, KC, 3 * C], scope=att)
        w_proj_sb = sb("w_proj_sb", [HC + 1, KC, C], scope=att)
        mix_in = sb("mix_in", [HC, KC, HEADS], scope=att)
        mix_out = sb("mix_out", [2 * WIN, PAIRS, HEADS], scope=att)
        mix_bias = sb("mix_bias", [WIN, HEADS], scope=att)
        ones_win = sb("ones_win", [WIN, WIN], scope=att)
        bl_row = sb("bl_row", [HC + 1, HEADS], scope=att)
        minus_half = sb("minus_half", [TT, 1], scope=att)
        xT_in = [sb(f"xT_in{p}", [HC, KC, POOL, TT], scope=att) for p in range(2)]
        xp_in = [sb(f"xp_in{p}", [TT, POOL, C], scope=att) for p in range(2)]
        dT = [sb(f"dT{p}", [HC, KC, TT], scope=att) for p in range(2)]
        tanh_d = [sb(f"tanh_d{p}", [TT, C], scope=att) for p in range(2)]
        diff = sb("diff", [TT, C], scope=att)
        stats1 = sb("stats1", [TT, 12], scope=att)
        stats2 = sb("stats2", [TT, 12], scope=att)
        rstd1 = [sb(f"rstd1_{p}", [TT, 1], scope=att) for p in range(2)]
        rstd2 = [sb(f"rstd2_{p}", [TT, 1], scope=att) for p in range(2)]
        hn = [sb(f"hn{p}", [TT, C], scope=att) for p in range(2)]
        hnT = [sb(f"hnT{p}", [HC + 1, KC, SEQS, 2, WIN], scope=att) for p in range(2)]
        qT = [sb(f"qT{p}", [HC + 1, KC, TT], scope=att) for p in range(2)]
        kT = [sb(f"kT{p}", [HC, KC, TT], scope=att) for p in range(2)]
        ks = [sb(f"ks{p}", [HC + 1, KC, HEADS, TT], scope=att) for p in range(2)]
        v_sb = [sb(f"v_sb{p}", [2 * WIN, SEQS, C], scope=att) for p in range(2)]
        vs = [sb(f"vs{p}", [2 * WIN, SEQS, PAIRS + 1, C], scope=att) for p in range(2)]
        smax = sb("smax", [SP_, HEADS], scope=att)
        ssum = sb("ssum", [SP_, HEADS], scope=att)
        prob = [sb(f"prob{p}", [SP_, HEADS, WIN], scope=att) for p in range(2)]
        probT = [sb(f"probT{p}", [2 * WIN, PAIRS, SP_], scope=att) for p in range(2)]
        oT = [sb(f"oT{p}", [HC + 1, KC, TT], scope=att) for p in range(2)]
        row = [sb(f"row{p}", [TT, ROW], scope=att) for p in range(2)]
        scoreT = [sb(f"scoreT{p}", [EXPERTS, TT], scope=att) for p in range(2)]
        att.close()

        score = sb("score", [128, CAP])
        onehot_sum = sb("onehot_sum", [128, 128])
        before = sb("before", [128, 128])
        cand = sb("cand", [128, 1], U32)
        thr = sb("thr", [128, 1], U32)
        bit = sb("bit", [128, 1], U32)
        enough = sb("enough", [128, 1], U32)
        count = sb("count", [128, 1])
        above = sb("above", [128, CAP])
        equal = sb("equal", [128, CAP])
        scan = sb("scan", [128, CAP])
        zeros = sb("zeros", [128, CAP])
        picked = sb("picked", [128, CAP])
        totals = sb("totals", [128, 2])
        room = sb("room", [128, 3])
        act_sh = [sb(f"act_sh{p}", [128, FC_SH, GT]) for p in range(2)]
        silu = [sb(f"silu{p}", [128, GT]) for p in range(2)]
        base = [sb(f"base{p}", [TT, GROUP, C]) for p in range(2)]
        iota_p = sb("iota_p", [TT, 1])
        iota_t = sb("iota_t", [TT, TILES], BF16)
        iota_hi = sb("iota_hi", [TT, HI])
        hot = ExitStack()
        pos_i = sb("pos_i", [TT, TILES * EXPERTS], I32, hot)
        pos_hi = sb("pos_hi", [TT, TILES * EXPERTS], I32, hot)
        pos_lo = sb("pos_lo", [TT, TILES * EXPERTS], I32, hot)
        hot_hi = sb("hot_hi", [TT, TILES * EXPERTS, HI], BF16, hot)
        hot_id = sb("hot_id", [TT, TILES * EXPERTS, 2, LO], BF16, hot)
        id_part = sb("id_part", [HI, EXPERTS, LO], F32, hot)
        ids = sb("ids", [HI, EXPERTS, LO], I32, hot)
        hot.close()
        idx = [sb(f"idx{p}", [SLOTS, GROUP], I32) for p in range(2)]
        xg = [sb(f"xg{p}", [SLOTS, GROUP, ROW]) for p in range(2)]
        top = [sb(f"top{p}", [SLOTS, GROUP]) for p in range(2)]
        xgT = [sb(f"xgT{p}", [HC, KC, CAP]) for p in range(2)]
        act_ex = [sb(f"act_ex{p}", [128, FC_EXP, CAP]) for p in range(2)]
        yo = [sb(f"yo{p}", [SLOTS, GROUP, C]) for p in range(2)]

        ps_s = [bank[0], bank[1]]
        ps_gate = bank[0][0:EXPERTS, 372:372 + TT]
        ps_pt = [bank[2], bank[3]]
        ps_qk = bank[4][0:HC, 0:4 * TT].rearrange("p (a n) -> p a n", a=4)
        ps_v = bank[5][0:2 * WIN, 0:SEQS * C].rearrange("p (s c) -> p s c", s=SEQS)
        ps_sct = bank[5][0:TT, 384:384 + EXPERTS]
        ps_hT = bank[6][0:HC, 0:KC * TT].rearrange("p (k n) -> p k n", k=KC)
        ps_pool = bank[6][0:TT, 256:256 + C]
        ps_o = bank[7][0:HC, 0:KC * TT].rearrange("p (k n) -> p k n", k=KC)
        ps_r = bank[7][0:TT, 256:256 + C]
        ps_g, ps_u, ps_y, ps_x = bank[0:2], bank[2:4], bank[4:6], bank[6:8]

        tok_loaded = sem("tok_loaded")
        qkv_loaded = sem("qkv_loaded")
        mix_in_loaded = sem("mix_in_loaded")
        mix_out_loaded = sem("mix_out_loaded")
        proj_loaded = sem("proj_loaded")
        ffn_loaded = sem("ffn_loaded")
        const_pool = sem("const_pool")
        const_dve = sem("const_dve")
        x_loaded = sems("x_loaded")
        dT_ready = sem("dT_ready")
        pool_mm = sem("pool_mm")
        pool_tanh = sem("pool_tanh")
        pool_seq = sem("pool_seq")
        var1_ready = sem("var1_ready")
        rstd1_ready = sem("rstd1_ready")
        hn_ready = sem("hn_ready")
        hnT_mm = sem("hnT_mm")
        hnT_ready = sem("hnT_ready")
        qk_mm = sem("qk_mm")
        v_mm = sem("v_mm")
        q_ready = sem("q_ready")
        k_ready = sem("k_ready")
        v_ready = sem("v_ready")
        ks0_ready = sem("ks0_ready")
        ks1_ready = sem("ks1_ready")
        vs0_ready = sem("vs0_ready")
        vs1_ready = sem("vs1_ready")
        s_mm = sem("s_mm")
        soft_seq = sem("soft_seq")
        shifted = sem("shifted")
        exp_done = sem("exp_done")
        prob_ready = sem("prob_ready")
        pt_mm = sem("pt_mm")
        probT_ready = sem("probT_ready")
        o_mm = sem("o_mm")
        oT_ready = sem("oT_ready")
        r_mm = sem("r_mm")
        res_seq = sem("res_seq")
        var2_ready = sem("var2_ready")
        rstd2_ready = sem("rstd2_ready")
        hn2_ready = sem("hn2_ready")
        hn2T_mm = sem("hn2T_mm")
        hn2T_ready = sem("hn2T_ready")
        gate_mm = sem("gate_mm")
        gate_tanh = sem("gate_tanh")
        score_ready = sem("score_ready")
        sct_mm = sem("sct_mm")
        row_ready = sem("row_ready")
        row_stored = sems("row_stored")
        w_loaded = sems("w_loaded")
        score_loaded = sem("score_loaded")
        counted = sem("counted")
        count_sum = sem("count_sum")
        find_seq = sem("find_seq")
        sh_g_mm = sem("sh_g_mm")
        sh_u_mm = sem("sh_u_mm")
        sh_silu = sem("sh_silu")
        sh_act = sem("sh_act")
        sh_y_mm = sem("sh_y_mm")
        sh_base = sem("sh_base")
        base_stored = sems("base_stored")
        route_seq = sem("route_seq")
        totals_ready = sem("totals_ready")
        eq_mm = sem("eq_mm")
        sel_total = sem("sel_total")
        sel_mm = sem("sel_mm")
        pos_ready = sem("pos_ready")
        posT_mm = sem("posT_mm")
        hot_ready = sem("hot_ready")
        ids_mm = sem("ids_mm")
        ids_ready = sem("ids_ready")
        ids_stored = sem("ids_stored")
        idx_loaded = sem("idx_loaded")
        idx_ready = sem("idx_ready")
        gathered = sems("gathered")
        scattered = sem("scattered")
        top_ready = sem("top_ready")
        xgT_mm = sem("xgT_mm")
        xgT_ready = sem("xgT_ready")
        g_mm = sem("g_mm")
        u_mm = sem("u_mm")
        silu_ready = sem("silu_ready")
        act_ready = sem("act_ready")
        y_mm = sem("y_mm")
        yo_ready = sem("yo_ready")

        own_waits = {e.engine: sem(f"own_waits_{n}") for n, e in
                     (("sp", nc.sync), ("pool", nc.gpsimd), ("pe", nc.tensor), ("dve", nc.vector))}

        def attention_over(eng):
            for s in (hn2T_ready, row_ready, gate_tanh, score_ready, prob_ready, hn2_ready, oT_ready,
                      o_mm, r_mm, sct_mm, gate_mm, pt_mm, v_mm, s_mm, vs0_ready, vs1_ready, ks0_ready,
                      ks1_ready, probT_ready, rstd2_ready, exp_done, hn2T_mm):
                eng.wait_ge(s, TILES)
            for s in row_stored:
                eng.wait_ge(s, 32 * (TILES // 2))

        def scale_values(eng, p, s):
            shape = [2 * WIN, PAIRS, HEADS, HD]
            return eng.tensor_tensor(
                vs[p][:, s, 0:PAIRS, :].rearrange("p j (g d) -> p j g d", d=HD),
                v_sb[p][:, s, :].rearrange("p (g d) -> p g d", d=HD).unsqueeze(1).to_broadcast(shape),
                mix_out[:].unsqueeze(3).to_broadcast(shape), ALU.mult)

        def stored_of(t, p, off):
            if isinstance(t, int):
                return 32 * ((t + off - p) // 2 + 1)
            return 16 * t + 16 * (off - p + 2)

        def apart(eng):
            eng.sem_inc(own_waits[eng.engine], 1)

        block = ctx.enter_context(nc.Block())

        @block.sync
        def _(sp):
            def load_x(t, p):
                count_ge(sp, dT_ready, upto(t, -2))
                apart(sp)
                count_ge(sp, pool_seq, 5 * upto(t, -2))
                apart(sp)
                sp.dma_start(xT_in[p][:], xT[t]).then_inc(x_loaded[p], 16)
                sp.dma_start(xp_in[p][:], xp[t]).then_inc(x_loaded[p], 16)

            halves = "(k p) n -> p k n"
            load_x(0, 0)
            sp.dma_start(w_tok_sb[:], w_tok.rearrange(halves, k=KC)).then_inc(tok_loaded, 16)
            sp.dma_start(w_qkv_sb[0:HC], w_qkv.rearrange(halves, k=KC)).then_inc(qkv_loaded, 16)
            sp.dma_start(w_qkv_sb[HC:HC + 1, 0, :], b_qkv).then_inc(qkv_loaded, 16)
            load_x(1, 1)
            for half in range(2):
                for j in range(PAIRS):
                    h = 2 * j + half
                    sp.dma_start(mix_out[half * WIN:(half + 1) * WIN, j, :],
                                 w_w[h:h + 1, :].to_broadcast([WIN, HEADS])).then_inc(mix_out_loaded, 16)
            sp.dma_start(mix_bias[:], b_w.to_broadcast([WIN, HEADS])).then_inc(mix_out_loaded, 16)
            sp.dma_start(w_proj_sb[0:HC], w_proj.rearrange(halves, k=KC)).then_inc(proj_loaded, 16)
            sp.dma_start(w_proj_sb[HC:HC + 1, 0, :], b_proj).then_inc(proj_loaded, 16)
            sp.dma_start(w_gate_sb[:], w_gate.rearrange(halves, k=KC)).then_inc(ffn_loaded, 16)
            sp.dma_start(wsg_sb[:], wsg.rearrange(halves, k=KC)).then_inc(ffn_loaded, 16)
            sp.dma_start(wsu_sb[:], wsu.rearrange(halves, k=KC)).then_inc(ffn_loaded, 16)
            sp.dma_start(wsd_sb[:], wsd.rearrange("(f p) n -> p f n", p=128)).then_inc(ffn_loaded, 16)

            def load_expert(e, p):
                sp.dma_start(wg_sb[p][:], wg[e]).then_inc(w_loaded[p], 16)
                sp.dma_start(wu_sb[p][:], wu[e]).then_inc(w_loaded[p], 16)
                sp.dma_start(wd_sb[p][:], wd[e]).then_inc(w_loaded[p], 16)

            load_expert(0, 0)
            load_expert(1, 1)

            def step(i, par):
                if live(i, 4) and not (isinstance(i, int) and i + 4 < 2):
                    load_x(i + 4, par)
                if live(i, -3):
                    t, p = i - 3, (par + 1) % 2
                    sp.wait_ge(row_ready, upto(t, 0))
                    apart(sp)
                    sp.dma_start(rows_dram[bass.ds(t * TT, TT), :], row[p][:]).then_inc(row_stored[p], 16)
                    sp.dma_start(score_dram[:, bass.ds(t * TT, TT)], scoreT[p][:]).then_inc(row_stored[p], 16)

            pipeline(sp, step)

            attention_over(sp)
            for c in range(SPREAD):
                sp.dma_start(score[c * EXPERTS:(c + 1) * EXPERTS, :],
                             score_dram[:, c * CAP:(c + 1) * CAP]).then_inc(score_loaded, 16)

            def store_base(g, p):
                sp.wait_ge(sh_base, 2 * g + 2)
                apart(sp)
                sp.dma_start(out_rows[bass.ds(g * GT, GT), :].rearrange("(j p) c -> p j c", p=TT),
                             base[p][:]).then_inc(base_stored[p], 16)

            with by_two(sp, 0, GROUPS) as g:
                store_base(g, 0)
                store_base(g + 1, 1)
            sp.wait_ge(ids_ready, 1)
            sp.dma_start(ids_dram.rearrange("e (h l) -> h e l", l=LO), ids[:]).then_inc(ids_stored, 16)
            sp.wait_ge(ids_stored, 16)
            sp.dma_start(idx_all[:], ids_dram.rearrange("e (p j) -> p e j", j=GROUP)).then_inc(idx_loaded, 16)

            def next_expert(e, p):
                sp.wait_ge(y_mm, 2 * e - 2)
                apart(sp)
                load_expert(e, p)

            with by_two(sp, 2, EXPERTS) as e:
                next_expert(e, 0)
                next_expert(e + 1, 1)
            for s in base_stored:
                sp.wait_ge(s, 16 * (GROUPS // 2))
            sp.wait_ge(scattered, 64 * EXPERTS)

        @block.gpsimd
        def _(pool):
            pool.memset(ident[:], 0.0).then_inc(const_pool, 1)
            pool.memset(minus_half[:], -0.5).then_inc(const_pool, 1)
            pool.memset(ones_win[:], 1.0).then_inc(const_pool, 1)
            pool.wait_ge(const_pool, 3)
            pool.affine_select(out=ident[:], in_=ident[:], compare_op=ALU.not_equal, fill=1.0,
                               base=0, pattern=[[-1, 128]], channel_multiplier=1).then_inc(const_pool, 1)
            pool.wait_ge(mix_in_loaded, 16 * (HEADS + 1))
            pool.wait_ge(mix_out_loaded, 16 * (HEADS + 1))

            def step(i, par):
                if live(i, 1):
                    t, p = i + 1, (par + 1) % 2
                    pool.wait_ge(k_ready, upto(t, 0))
                    count_ge(pool, s_mm, upto(t, -2))
                    pool.tensor_tensor(ks[p][0:HC, 1], kT[p][:, 1, :].unsqueeze(1).to_broadcast([HC, HEADS, TT]),
                                       mix_in[:, 1, :].unsqueeze(2).to_broadcast([HC, HEADS, TT]),
                                       ALU.mult).then_inc(ks1_ready, 1)
                if live(i, 2):
                    t, p = i + 2, par
                    pool.wait_ge(var1_ready, upto(t, 0))
                    count_ge(pool, hn_ready, upto(t, -2))
                    pool.tensor_tensor(rstd1[p][:], stats1[:, 8:9], minus_half[:], ALU.pow).then_inc(rstd1_ready, 1)
                if live(i, -1):
                    t, p = i - 1, (par + 1) % 2
                    pool.wait_ge(var2_ready, upto(t, 0))
                    count_ge(pool, hn2_ready, upto(t, -2))
                    pool.tensor_tensor(rstd2[p][:], stats2[:, 8:9], minus_half[:], ALU.pow).then_inc(rstd2_ready, 1)
                if live(i, 1):
                    t, p = i + 1, (par + 1) % 2
                    pool.wait_ge(v_ready, upto(t, 0))
                    count_ge(pool, o_mm, upto(t, -2))
                    scale_values(pool, p, 0).then_inc(vs0_ready, 1)

            pipeline(pool, step)

            attention_over(pool)
            pool.memset(onehot_sum[:], 0.0).then_inc(const_pool, 1)
            pool.memset(before[:], 0.0).then_inc(const_pool, 1)
            pool.wait_ge(const_pool, 6)
            for d in range(-(SPREAD - 1), SPREAD):
                pool.affine_select(out=onehot_sum[:], in_=onehot_sum[:], compare_op=ALU.not_equal, fill=1.0,
                                   base=d * EXPERTS, pattern=[[-1, 128]],
                                   channel_multiplier=1).then_inc(const_pool, 1)
                pool.wait_ge(const_pool, 6 + d + SPREAD)
            for d in range(1, SPREAD):
                pool.affine_select(out=before[:], in_=before[:], compare_op=ALU.not_equal, fill=1.0,
                                   base=d * EXPERTS, pattern=[[-1, 128]],
                                   channel_multiplier=1).then_inc(const_pool, 1)
                pool.wait_ge(const_pool, 5 + 2 * SPREAD + d)
            pool.memset(zeros[:], 0.0).then_inc(const_pool, 1)
            pool.iota(iota_p[:], [[0, 1]], base=0, channel_multiplier=1,
                      allow_small_or_imprecise_dtypes=True).then_inc(const_pool, 1)
            pool.iota(iota_t[:], [[1, TILES]], base=0, channel_multiplier=0,
                      allow_small_or_imprecise_dtypes=True).then_inc(const_pool, 1)
            pool.iota(iota_hi[:], [[1, HI]], base=0, channel_multiplier=0,
                      allow_small_or_imprecise_dtypes=True).then_inc(const_pool, 1)

            pool.wait_ge(idx_loaded, 16)

            def gather(e, p, first=False):
                if not first:
                    pool.wait_ge(scattered, 64 * (e - 1))
                pool.tensor_copy(idx[p][:], idx_all[:, bass.ds(e, 1), :].rearrange("p a j -> p (a j)")
                                 ).then_inc(idx_ready, 1)
                pool.wait_ge(idx_ready, e + 1)
                if not first:
                    pool.wait_ge(xgT_mm, e - 1)
                    pool.wait_ge(top_ready, e - 1)
                apart(pool)
                for j in range(GROUP):
                    pool.indirect_dma_start(out=xg[p][:, j, :], out_offset=None, in_=rows_dram,
                                            in_offset=bass.IndirectOffsetOnAxis(
                                                ap=idx[p][:, j:j + 1].bitcast(U32), axis=0)
                                            ).then_inc(gathered[p], 16)

            def scatter(e, p, first=False):
                pool.wait_ge(yo_ready, 2 * e + 2)
                if not first:
                    pool.wait_ge(scattered, 64 * e)
                apart(pool)
                for j in range(GROUP):
                    pool.indirect_dma_start(out=out_rows, out_offset=bass.IndirectOffsetOnAxis(
                        ap=idx[p][:, j:j + 1].bitcast(U32), axis=0),
                        in_=yo[p][:, j, :], in_offset=None, compute_op=ALU.add).then_inc(scattered, 16)

            gather(0, 0, first=True)
            gather(1, 1, first=True)
            for s in base_stored:
                pool.wait_ge(s, 16 * (GROUPS // 2))
            scatter(0, 0, first=True)
            gather(2, 0)
            with by_two(pool, 1, EXPERTS - 3) as e:
                scatter(e, 1)
                gather(e + 2, 1)
                scatter(e + 1, 0)
                gather(e + 3, 0)
            scatter(EXPERTS - 3, 1)
            gather(EXPERTS - 1, 1)
            scatter(EXPERTS - 2, 0)
            scatter(EXPERTS - 1, 1)

        @block.scalar
        def _(act):
            for h in range(HEADS):
                k, r = divmod(h * HD, HC)
                act.dma_start(mix_in[r:r + HD, k, :],
                              w_l[h:h + 1, :].to_broadcast([HD, HEADS])).then_inc(mix_in_loaded, 16)
            act.dma_start(bl_row[HC:HC + 1, :], b_l).then_inc(mix_in_loaded, 16)

            def step(i, par):
                if live(i, -3):
                    t, p = i - 3, (par + 1) % 2
                    act.wait_ge(sct_mm, upto(t, 0))
                    nc.scalar.copy(row[p][:, C:ROW], ps_sct).then_inc(row_ready, 1)
                if live(i, -2):
                    t = i - 2
                    act.wait_ge(hn2T_mm, upto(t, 0))
                    nc.scalar.copy(hn2T[:, :, bass.ds(t * TT, TT)], ps_hT).then_inc(hn2T_ready, 1)
                if live(i, 1):
                    t, p = i + 1, (par + 1) % 2
                    act.wait_ge(qk_mm, upto(t, 0))
                    count_ge(act, ks0_ready, upto(t, -2))
                    count_ge(act, ks1_ready, upto(t, -2))
                    nc.scalar.copy(kT[p][:], ps_qk[:, 2:4, :]).then_inc(k_ready, 1)
                    count_ge(act, s_mm, upto(t, -2))
                    nc.scalar.mul(qT[p][0:HC], ps_qk[:, 0:2, :], float(HD) ** -0.5).then_inc(q_ready, 1)
                if live(i, 0):
                    t, p = i, par
                    act.wait_ge(shifted, upto(t, 0))
                    nc.scalar.activation(prob[p][:], prob[p][:], ACT.Exp).then_inc(exp_done, 1)
                if live(i, 1):
                    t, p = i + 1, (par + 1) % 2
                    act.wait_ge(v_mm, upto(t, 0))
                    count_ge(act, vs0_ready, upto(t, -2))
                    count_ge(act, vs1_ready, upto(t, -2))
                    nc.scalar.copy(v_sb[p][:], ps_v).then_inc(v_ready, 1)
                if live(i, 2):
                    t, p = i + 2, par
                    act.wait_ge(pool_mm, upto(t, 0))
                    count_ge(act, pool_seq, 5 * upto(t, -2))
                    nc.scalar.activation(tanh_d[p][:], ps_pool, ACT.Tanh, scale=0.5).then_inc(pool_tanh, 1)
                if live(i, -1):
                    t, p = i - 1, (par + 1) % 2
                    act.wait_ge(o_mm, upto(t, 0))
                    count_ge(act, r_mm, upto(t, -2))
                    nc.scalar.copy(oT[p][0:HC], ps_o).then_inc(oT_ready, 1)
                if live(i, -2):
                    t, p = i - 2, par
                    act.wait_ge(gate_mm, upto(t, 0))
                    count_ge(act, sct_mm, upto(t, -2))
                    if not (isinstance(t, int) and t < 2):
                        act.wait_ge(row_stored[p], stored_of(t, p, -2))
                    nc.scalar.activation(scoreT[p][:], ps_gate, ACT.Tanh, scale=0.5).then_inc(gate_tanh, 1)
                if live(i, 0):
                    t, p = i, par
                    act.wait_ge(pt_mm, upto(t, 0))
                    count_ge(act, o_mm, upto(t, -2))
                    for b in range(2):
                        ins = nc.scalar.copy(probT[p][:, 3 * b:3 * b + 3, :],
                                             ps_pt[b][0:2 * WIN, 0:3 * SP_].rearrange("p (a n) -> p a n", a=3))
                    ins.then_inc(probT_ready, 1)
                if live(i, 2):
                    t, p = i + 2, par
                    act.wait_ge(hnT_mm, upto(t, 0))
                    count_ge(act, v_mm, upto(t, -2))
                    for k in range(KC):
                        ins = nc.scalar.copy(hnT[p][0:HC, k], ps_hT[:, k, :].rearrange("p (s m) -> p s m", s=SEQS)
                                             .unsqueeze(2).to_broadcast([HC, SEQS, 2, WIN]))
                    ins.then_inc(hnT_ready, 1)

            pipeline(act, step)
            attention_over(act)

            def shared_silu(n, b):
                act.wait_ge(sh_g_mm, n + 1)
                count_ge(act, sh_act, n - 1)
                nc.scalar.activation(silu[b][:], ps_g[b][:, 0:GT], ACT.Silu).then_inc(sh_silu, 1)

            for n in range(2):
                shared_silu(n, n)
            with by_two(act, 2, FC_SH * GROUPS) as n:
                shared_silu(n, 0)
                shared_silu(n + 1, 1)

            def turn_in(e, p, first=False):
                act.wait_ge(xgT_mm, e + 1)
                if not first:
                    act.wait_ge(u_mm, FC_EXP * (e - 1))
                for k in range(KC):
                    ins = nc.scalar.copy(xgT[p][:, k, :], ps_x[k][0:HC, 0:CAP])
                ins.then_inc(xgT_ready, 1)

            def expert_silu(e, first=False):
                for f in range(FC_EXP):
                    act.wait_ge(g_mm, FC_EXP * e + (f + 1))
                    if first and f < 2:
                        act.wait_ge(sh_act, FC_SH * GROUPS)
                    else:
                        act.wait_ge(act_ready, FC_EXP * e + (f - 1))
                    nc.scalar.activation(silu[f % 2][:], ps_g[f % 2][:, 0:CAP], ACT.Silu).then_inc(silu_ready, 1)

            turn_in(0, 0, first=True)
            expert_silu(0, first=True)
            turn_in(1, 1, first=True)
            expert_silu(1)
            turn_in(2, 0)
            with by_two(act, 2, EXPERTS - 2) as e:
                expert_silu(e)
                turn_in(e + 1, 1)
                expert_silu(e + 1)
                turn_in(e + 2, 0)
            expert_silu(EXPERTS - 2)
            turn_in(EXPERTS - 1, 1)
            expert_silu(EXPERTS - 1)

        @block.vector
        def _(dve):
            def loaded_of(t, p):
                return 32 * ((t - p) // 2 + 1) if isinstance(t, int) else 16 * t + 16 * (2 - p)

            def difference(t, p):
                dve.wait_ge(x_loaded[p], loaded_of(t, p))
                count_ge(dve, pool_mm, upto(t, -2))
                dve.tensor_tensor(dT[p][:], xT_in[p][:, :, 0, :], xT_in[p][:, :, 1, :],
                                  ALU.subtract).then_inc(dT_ready, 1)

            def normalise(t, p, src, dst, stats, var_ready, rstd, rstd_ready, seq, n, done):
                apart(dve)
                dve.bn_stats(stats[:, 0:6], src).then_inc(seq, 1)
                dve.wait_ge(seq, n + 1)
                apart(dve)
                dve.bn_aggr(stats[:, 6:8], stats[:, 0:6]).then_inc(seq, 1)
                dve.wait_ge(seq, n + 2)
                dve.tensor_scalar(stats[:, 8:9], stats[:, 7:8], LN_EPS, None, ALU.add).then_inc(var_ready, 1)
                dve.wait_ge(rstd_ready, upto(t, 0))
                return dve.tensor_scalar(dst, src, stats[:, 6:7], rstd[:, 0:1], ALU.subtract, ALU.mult)

            def scaled_keys(t, p):
                dve.wait_ge(k_ready, upto(t, 0))
                count_ge(dve, s_mm, upto(t, -2))
                dve.tensor_tensor(ks[p][0:HC, 0], kT[p][:, 0, :].unsqueeze(1).to_broadcast([HC, HEADS, TT]),
                                  mix_in[:, 0, :].unsqueeze(2).to_broadcast([HC, HEADS, TT]),
                                  ALU.mult).then_inc(ks0_ready, 1)

            for p in range(2):
                for buf in (hnT, qT, oT):
                    dve.memset(buf[p][HC:HC + 1, 0], 1.0).then_inc(const_dve, 1)
                dve.wait_ge(mix_in_loaded, 16 * (HEADS + 1))
                dve.tensor_copy(ks[p][HC:HC + 1, 0], bl_row[HC:HC + 1, :].unsqueeze(2)
                                .to_broadcast([1, HEADS, TT])).then_inc(const_dve, 1)

            dve.wait_ge(mix_out_loaded, 16 * (HEADS + 1))

            def step(i, par):
                if live(i, 0):
                    t, p = i, par
                    s_view = [ps_s[b][0:SP_, 0:HALF * WIN].rearrange("p (g m) -> p g m", m=WIN) for b in range(2)]
                    dve.wait_ge(s_mm, upto(t, 0))
                    for b in range(2):
                        dve.tensor_reduce(smax[:, HALF * b:HALF * (b + 1)], s_view[b], AX.X,
                                          ALU.max).then_inc(soft_seq, 1)
                    dve.wait_ge(soft_seq, 4 * upto(t, -1) + 2)
                    count_ge(dve, pt_mm, upto(t, -2))
                    for b in range(2):
                        ins = dve.tensor_tensor(
                            prob[p][:, HALF * b:HALF * (b + 1), :], s_view[b],
                            smax[:, HALF * b:HALF * (b + 1)].unsqueeze(2).to_broadcast([SP_, HALF, WIN]),
                            ALU.subtract)
                    ins.then_inc(shifted, 1)
                if live(i, 1):
                    scaled_keys(i + 1, (par + 1) % 2)
                if live(i, 0):
                    t, p = i, par
                    dve.wait_ge(exp_done, upto(t, 0))
                    dve.tensor_reduce(ssum[:], prob[p][:], AX.X, ALU.add).then_inc(soft_seq, 1)
                    dve.wait_ge(soft_seq, 4 * upto(t, -1) + 3)
                    dve.reciprocal(ssum[:], ssum[:]).then_inc(soft_seq, 1)
                    dve.wait_ge(soft_seq, 4 * upto(t, 0))
                    dve.tensor_tensor(prob[p][:], prob[p][:], ssum[:].unsqueeze(2).to_broadcast([SP_, HEADS, WIN]),
                                      ALU.mult).then_inc(prob_ready, 1)
                if live(i, 2):
                    t, p = i + 2, par
                    n = 5 * upto(t, -1)
                    h_t = h_all[:, bass.ds(t, 1), :].rearrange("p a c -> p (a c)")
                    dve.wait_ge(x_loaded[p], loaded_of(t, p))
                    dve.tensor_tensor(diff[:], xp_in[p][:, 0, :], xp_in[p][:, 1, :],
                                      ALU.subtract).then_inc(pool_seq, 1)
                    dve.wait_ge(pool_seq, n + 1)
                    dve.wait_ge(pool_tanh, upto(t, 0))
                    dve.scalar_tensor_tensor(out=diff[:], in0=tanh_d[p][:], scalar=1.0, in1=diff[:],
                                             op0=ALU.add, op1=ALU.mult).then_inc(pool_seq, 1)
                    dve.wait_ge(pool_seq, n + 2)
                    dve.scalar_tensor_tensor(out=h_t, in0=diff[:], scalar=0.5, in1=xp_in[p][:, 1, :],
                                             op0=ALU.mult, op1=ALU.add).then_inc(pool_seq, 1)
                    dve.wait_ge(pool_seq, n + 3)
                    count_ge(dve, hnT_mm, upto(t, -2))
                    normalise(t, p, h_t, hn[p][:], stats1, var1_ready, rstd1[p], rstd1_ready,
                              pool_seq, n + 3, None).then_inc(hn_ready, 1)
                if live(i, -1):
                    t, p = i - 1, (par + 1) % 2
                    n = 3 * upto(t, -1)
                    h_t = h_all[:, bass.ds(t, 1), :].rearrange("p a c -> p (a c)")
                    dve.wait_ge(r_mm, upto(t, 0))
                    dve.tensor_tensor(h_t, h_t, ps_r, ALU.add).then_inc(res_seq, 1)
                    dve.wait_ge(res_seq, n + 1)
                    count_ge(dve, hn2T_mm, upto(t, -2))
                    if not (isinstance(t, int) and t < 2):
                        dve.wait_ge(row_stored[p], stored_of(t, p, -2))
                    normalise(t, p, h_t, row[p][:, 0:C], stats2, var2_ready, rstd2[p], rstd2_ready,
                              res_seq, n + 1, None).then_inc(hn2_ready, 1)
                if live(i, 1):
                    t, p = i + 1, (par + 1) % 2
                    dve.wait_ge(v_ready, upto(t, 0))
                    count_ge(dve, o_mm, upto(t, -2))
                    scale_values(dve, p, 1)
                    dve.tensor_tensor(
                        vs[p][0:WIN, :, PAIRS, :].rearrange("p s (g d) -> p s g d", d=HD),
                        v_sb[p][0:WIN].rearrange("p s (g d) -> p s g d", d=HD),
                        mix_bias[:].unsqueeze(1).unsqueeze(3).to_broadcast([WIN, SEQS, HEADS, HD]),
                        ALU.mult).then_inc(vs1_ready, 1)
                if live(i, -2):
                    t, p = i - 2, par
                    dve.wait_ge(gate_tanh, upto(t, 0))
                    dve.tensor_scalar(scoreT[p][:], scoreT[p][:], 0.5, 0.5, ALU.mult, ALU.add
                                      ).then_inc(score_ready, 1)
                if live(i, 3):
                    difference(i + 3, (par + 1) % 2)

            pipeline(dve, step)
            attention_over(dve)

            dve.memset(thr[:], 0).then_inc(find_seq, 1)
            dve.memset(bit[:], 1 << 30).then_inc(find_seq, 1)
            dve.wait_ge(find_seq, 2)
            dve.wait_ge(score_loaded, 16 * SPREAD)

            def try_bit(s):
                dve.tensor_tensor(cand[:], thr[:], bit[:], ALU.bitwise_or).then_inc(find_seq, 1)
                dve.wait_ge(find_seq, 5 * s + 3)
                dve.tensor_scalar(above[:], score[:], cand[:].bitcast(F32), 0.0, ALU.is_ge, ALU.add,
                                  accum_out=count[:]).then_inc(counted, 1)

            def keep_bit(s):
                dve.wait_ge(count_sum, s + 1)
                dve.tensor_scalar(enough[:], ps_x[0][:, 0:1], float(CAP), None, ALU.is_ge).then_inc(find_seq, 1)
                dve.wait_ge(find_seq, 5 * s + 4)
                dve.copy_predicated(thr[:], enough[:], cand[:]).then_inc(find_seq, 1)
                dve.tensor_scalar(bit[:], bit[:], 1, None, ALU.logical_shift_right).then_inc(find_seq, 1)
                dve.wait_ge(find_seq, 5 * s + 6)
                dve.engine_nop().then_inc(find_seq, 1)
                dve.wait_ge(find_seq, 5 * s + 7)

            def shared_act(n, b, p, f):
                dve.wait_ge(sh_silu, n + 1)
                dve.wait_ge(sh_u_mm, n + 1)
                dve.tensor_tensor(act_sh[p][:, f, :], silu[b][:], ps_u[b][:, 0:GT], ALU.mult).then_inc(sh_act, 1)

            def shared_out(g, p, half):
                dve.wait_ge(sh_y_mm, 2 * g + half + 1)
                dve.tensor_tensor(base[p][:, 2 * half:2 * half + 2, :],
                                  h_all[:, bass.ds(GROUP * g + 2 * half, 2), :],
                                  ps_y[half][0:TT, 0:2 * C].rearrange("p (j c) -> p j c", c=C),
                                  ALU.add).then_inc(sh_base, 1)

            def free_base(g, p):
                if g >= 2:
                    dve.wait_ge(base_stored[p], 16 * (g // 2))

            def shared_group(g, p, search, first=False):
                def slot(k):
                    if search:
                        try_bit(8 * g + k)
                        keep_bit(8 * g + k)
                n, b = FC_SH * g, (FC_SH * p) % 2
                if g >= 2:
                    dve.wait_ge(sh_y_mm, 2 * g - 2)
                slot(0)
                slot(1)
                shared_act(n, b, p, 0)
                slot(2)
                slot(3)
                if not first:
                    free_base(g - 1, 1 - p)
                    shared_out(g - 1, 1 - p, 0)
                    shared_out(g - 1, 1 - p, 1)
                slot(4)
                slot(5)
                shared_act(n + 1, 1 - b, p, 1)
                slot(6)
                slot(7)
                shared_act(n + 2, b, p, 2)

            for g in range(GROUPS // 2):
                shared_group(g, g % 2, True, first=(g == 0))

            dve.wait_ge(const_pool, 8 + 3 * SPREAD)
            thr_f = thr[:].bitcast(F32)
            dve.tensor_scalar(above[:], score[:], thr_f, 0.0, ALU.is_gt, ALU.add,
                              accum_out=totals[:, 0:1]).then_inc(route_seq, 1)
            dve.tensor_scalar(equal[:], score[:], thr_f, 0.0, ALU.is_equal, ALU.add,
                              accum_out=totals[:, 1:2]).then_inc(totals_ready, 1)
            dve.wait_ge(totals_ready, 1)
            dve.tensor_tensor_scan(scan[:], equal[:], zeros[:], 0.0, ALU.add, ALU.add).then_inc(route_seq, 1)
            shared_group(4, 0, False)
            dve.wait_ge(eq_mm, 1)
            dve.tensor_scalar(room[:, 0:1], ps_x[0][:, 1:2], -1.0, float(CAP), ALU.mult, ALU.add
                              ).then_inc(route_seq, 1)
            dve.wait_ge(route_seq, 3)
            dve.tensor_tensor(room[:, 1:2], room[:, 0:1], ps_x[0][:, 3:4], ALU.subtract).then_inc(route_seq, 1)
            dve.wait_ge(route_seq, 4)
            dve.scalar_tensor_tensor(out=equal[:], in0=scan[:], scalar=room[:, 1:2], in1=equal[:],
                                     op0=ALU.is_le, op1=ALU.mult).then_inc(route_seq, 1)
            dve.wait_ge(route_seq, 5)
            dve.tensor_tensor(picked[:], above[:], equal[:], ALU.add).then_inc(route_seq, 1)
            dve.wait_ge(route_seq, 6)
            dve.tensor_tensor_scan(scan[:], picked[:], zeros[:], 0.0, ALU.add, ALU.add).then_inc(route_seq, 1)
            dve.wait_ge(route_seq, 7)
            dve.tensor_copy(room[:, 2:3], scan[:, CAP - 1:CAP]).then_inc(sel_total, 1)
            shared_group(5, 1, False)
            dve.wait_ge(sel_mm, 1)
            dve.scalar_tensor_tensor(out=above[:], in0=scan[:], scalar=ps_x[0][:, 4:5], in1=picked[:],
                                     op0=ALU.add, op1=ALU.mult).then_inc(pos_ready, 1)
            shared_group(6, 0, False)
            dve.wait_ge(posT_mm, 1)
            dve.tensor_scalar(pos_i[:].rearrange("p (c j e) -> p j c e", j=GROUP, e=EXPERTS),
                              ps_x[1][0:TT, :].rearrange("p (j c e) -> p j c e", j=GROUP, e=EXPERTS),
                              -1.0, None, ALU.add).then_inc(route_seq, 1)
            dve.wait_ge(route_seq, 8)
            dve.tensor_scalar(pos_hi[:], pos_i[:], 4, None, ALU.arith_shift_right).then_inc(route_seq, 1)
            dve.tensor_scalar(pos_lo[:], pos_i[:], LO - 1, None, ALU.bitwise_and).then_inc(route_seq, 1)
            dve.wait_ge(route_seq, 10)
            n_te = TILES * EXPERTS
            shape = [TT, n_te, LO]
            dve.tensor_tensor(hot_id[:, :, 0, :], pos_lo[:].unsqueeze(2).to_broadcast(shape),
                              iota_hi[:, 0:LO].unsqueeze(1).to_broadcast(shape),
                              ALU.is_equal).then_inc(route_seq, 1)
            dve.tensor_tensor(hot_hi[:], pos_hi[:].unsqueeze(2).to_broadcast([TT, n_te, HI]),
                              iota_hi[:].unsqueeze(1).to_broadcast([TT, n_te, HI]),
                              ALU.is_equal).then_inc(route_seq, 1)
            dve.wait_ge(route_seq, 12)
            dve.tensor_scalar(hot_id[:, :, 1, :], hot_id[:, :, 0, :], iota_p[:, 0:1], None,
                              ALU.mult).then_inc(route_seq, 1)
            dve.wait_ge(route_seq, 13)
            by_tile = hot_id[:].rearrange("p (t e) a l -> p t e a l", e=EXPERTS)[:, :, :, 0, :]
            dve.tensor_tensor(by_tile, by_tile,
                              iota_t[:].unsqueeze(2).unsqueeze(3).to_broadcast([TT, TILES, EXPERTS, LO]),
                              ALU.mult).then_inc(hot_ready, 1)
            shared_group(7, 1, False)
            free_base(7, 1)
            shared_out(7, 1, 0)
            shared_out(7, 1, 1)
            dve.wait_ge(ids_mm, 1)
            ids_view = ps_x[0][0:HI, :].rearrange("p (e a l) -> p e a l", a=2, l=LO)
            dve.tensor_scalar(id_part[:], ids_view[:, :, 0, :], float(TT), None, ALU.mult).then_inc(route_seq, 1)
            dve.wait_ge(route_seq, 14)
            dve.tensor_tensor(ids[:], id_part[:], ids_view[:, :, 1, :], ALU.add).then_inc(ids_ready, 1)

            def take_scores(e, p):
                dve.wait_ge(gathered[p], 32 * e - 32 * p + 64)
                dve.tensor_copy(top[p][:], xg[p][:, :, bass.ds(e + C, 1)].rearrange("p j a -> p (j a)")
                                ).then_inc(top_ready, 1)

            def expert_out(e, p, first=False):
                if not first:
                    dve.wait_ge(scattered, 64 * (e - 1))
                dve.wait_ge(top_ready, e + 1)
                for j in range(GROUP):
                    dve.wait_ge(y_mm, 2 * e + 1 + j // 2)
                    ins = dve.tensor_scalar(yo[p][:, j, :], ps_y[j // 2][0:SLOTS, (j % 2) * C:(j % 2 + 1) * C],
                                            top[p][:, j:j + 1], None, ALU.mult)
                    if j % 2 == 1:
                        ins.then_inc(yo_ready, 1)

            def expert_act(e, p, f):
                dve.wait_ge(silu_ready, FC_EXP * e + (f + 1))
                dve.wait_ge(u_mm, FC_EXP * e + (f + 1))
                dve.tensor_tensor(act_ex[p][:, f, :], silu[f % 2][:], ps_u[f % 2][:, 0:CAP],
                                  ALU.mult).then_inc(act_ready, 1)

            def expert(e, p, first=False, second=False):
                if not first:
                    if not second:
                        dve.wait_ge(y_mm, 2 * e - 2)
                expert_act(e, p, 0)
                if not first:
                    expert_out(e - 1, 1 - p, first=second)
                take_scores(e, p)
                for f in range(1, FC_EXP):
                    expert_act(e, p, f)

            expert(0, 0, first=True)
            expert(1, 1, second=True)
            expert(2, 0)
            expert(3, 1)
            with by_two(dve, 4, EXPERTS) as e:
                expert(e, 0)
                expert(e + 1, 1)
            expert_out(EXPERTS - 1, 1)

        @block.tensor
        def _(pe):
            pe.wait_ge(const_pool, 4)
            pe.wait_ge(tok_loaded, 16)
            pe.wait_ge(const_dve, 8)

            def product(out, pairs, sync=None):
                for n, (lhsT, rhs) in enumerate(pairs):
                    ins = nc.tensor.matmul(out, lhsT, rhs, start=(n == 0), stop=(n == len(pairs) - 1))
                return ins

            def step(i, par):
                if live(i, 0):
                    t, p = i, par
                    pe.wait_ge(q_ready, upto(t, 0))
                    pe.wait_ge(ks0_ready, upto(t, 0))
                    pe.wait_ge(ks1_ready, upto(t, 0))
                    count_ge(pe, shifted, upto(t, -1))
                    count_ge(pe, gate_tanh, upto(t, -3))
                    for b in range(2):
                        g0 = HALF * b
                        for s in range(SEQS):
                            rows = slice(0, SECOND) if s == 0 else slice(WIN, TT)
                            keys = slice(s * WIN, (s + 1) * WIN)
                            at = slice(0, SECOND) if s == 0 else slice(SECOND, SP_)
                            ins = product(ps_s[b][at, 0:HALF * WIN].rearrange("p (g m) -> p g m", m=WIN), [
                                (qT[p][0:HC + 1, 0, rows], ks[p][0:HC + 1, 0, g0:g0 + HALF, keys]),
                                (qT[p][0:HC, 1, rows], ks[p][0:HC, 1, g0:g0 + HALF, keys])])
                    ins.then_inc(s_mm, 1)
                if live(i, -3):
                    t, p = i - 3, (par + 1) % 2
                    pe.wait_ge(score_ready, upto(t, 0))
                    count_ge(pe, row_ready, upto(t, -1))
                    count_ge(pe, v_ready, upto(t, 3))
                    apart(pe)
                    nc.tensor.transpose(ps_sct, scoreT[p][:], ident[0:EXPERTS, 0:EXPERTS]).then_inc(sct_mm, 1)
                if live(i, -2):
                    t, p = i - 2, par
                    pe.wait_ge(hn2_ready, upto(t, 0))
                    count_ge(pe, hnT_ready, upto(t, 3))
                    count_ge(pe, hn2T_ready, upto(t, -1))
                    for k in range(KC):
                        ins = nc.tensor.transpose(ps_hT[:, k, :], row[p][:, k * HC:(k + 1) * HC], ident[0:TT, 0:TT])
                    ins.then_inc(hn2T_mm, 1)
                if live(i, 1):
                    t, p = i + 1, (par + 1) % 2
                    pe.wait_ge(hnT_ready, upto(t, 0))
                    if isinstance(t, int) and t == 0:
                        pe.wait_ge(qkv_loaded, 32)
                    count_ge(pe, q_ready, upto(t, -1))
                    count_ge(pe, k_ready, upto(t, -1))
                    for a in range(4):
                        cols = slice(a * HC, (a + 1) * HC)
                        ins = product(ps_qk[:, a, :], [
                            (w_qkv_sb[0:HC + 1, 0, cols], hnT[p][0:HC + 1, 0, :, 0, :]),
                            (w_qkv_sb[0:HC, 1, cols], hnT[p][0:HC, 1, :, 0, :])])
                    ins.then_inc(qk_mm, 1)
                    count_ge(pe, v_ready, upto(t, -1))
                    count_ge(pe, row_ready, upto(t, -4))
                    for s in range(SEQS):
                        cols = slice(2 * C, 3 * C)
                        lhs = [hnT[p][0:n, k, s].rearrange("p a m -> p (a m)")
                               for k, n in ((0, HC + 1), (1, HC))]
                        ins = product(ps_v[:, s, :], [(lhs[0], w_qkv_sb[0:HC + 1, 0, cols]),
                                                      (lhs[1], w_qkv_sb[0:HC, 1, cols])])
                    ins.then_inc(v_mm, 1)
                if live(i, 2):
                    t, p = i + 2, par
                    pe.wait_ge(dT_ready, upto(t, 0))
                    count_ge(pe, pool_tanh, upto(t, -1))
                    count_ge(pe, hnT_ready, upto(t, -1))
                    count_ge(pe, hn2T_ready, upto(t, -4))
                    product(ps_pool, [(dT[p][:, k, :], w_tok_sb[:, k, :]) for k in range(KC)]).then_inc(pool_mm, 1)
                if live(i, -1):
                    t, p = i - 1, (par + 1) % 2
                    pe.wait_ge(probT_ready, upto(t, 0))
                    pe.wait_ge(vs0_ready, upto(t, 0))
                    pe.wait_ge(vs1_ready, upto(t, 0))
                    count_ge(pe, oT_ready, upto(t, -1))
                    count_ge(pe, res_seq, 3 * upto(t, -1))
                    for k in range(KC):
                        c = slice(k * HC, (k + 1) * HC)
                        for s in range(SEQS):
                            at = s * SECOND
                            ins = product(ps_o[:, k, s * WIN:(s + 1) * WIN], [
                                (vs[p][:, s, j, c], probT[p][:, j, at:at + WIN]) for j in range(PAIRS)
                            ] + [(vs[p][0:WIN, s, PAIRS, c], ones_win[:])])
                    ins.then_inc(o_mm, 1)
                if live(i, -2):
                    t = i - 2
                    pe.wait_ge(hn2T_ready, upto(t, 0))
                    if isinstance(t, int) and t == 0:
                        pe.wait_ge(ffn_loaded, 64)
                    count_ge(pe, gate_tanh, upto(t, -1))
                    if live(i, 0):
                        pe.wait_ge(shifted, upto(i, 0))
                    product(ps_gate, [(w_gate_sb[:, k, :], hn2T[:, k, bass.ds(t * TT, TT)])
                                      for k in range(KC)]).then_inc(gate_mm, 1)
                if live(i, -1):
                    t, p = i - 1, (par + 1) % 2
                    pe.wait_ge(oT_ready, upto(t, 0))
                    if isinstance(t, int) and t == 0:
                        pe.wait_ge(proj_loaded, 32)
                    count_ge(pe, res_seq, 3 * upto(t, -1))
                    product(ps_r, [(oT[p][0:HC + 1, 0, :], w_proj_sb[0:HC + 1, 0, :]),
                                   (oT[p][0:HC, 1, :], w_proj_sb[0:HC, 1, :])]).then_inc(r_mm, 1)
                if live(i, 0):
                    t, p = i, par
                    pe.wait_ge(prob_ready, upto(t, 0))
                    count_ge(pe, probT_ready, upto(t, -1))
                    for j in range(PAIRS):
                        ins = nc.tensor.transpose(ps_pt[j // 3][0:2 * WIN, (j % 3) * SP_:(j % 3 + 1) * SP_],
                                                  prob[p][:, 2 * j:2 * j + 2, :].rearrange("p h m -> p (h m)"),
                                                  ident[0:SP_, 0:SP_])
                    ins.then_inc(pt_mm, 1)
                if live(i, 2):
                    t, p = i + 2, par
                    pe.wait_ge(hn_ready, upto(t, 0))
                    pe.wait_ge(pool_tanh, upto(t, 0))
                    for k in range(KC):
                        ins = nc.tensor.transpose(ps_hT[:, k, :], hn[p][:, k * HC:(k + 1) * HC], ident[0:TT, 0:TT])
                    ins.then_inc(hnT_mm, 1)

            pipeline(pe, step)
            attention_over(pe)
            pe.wait_ge(const_pool, 8 + 3 * SPREAD)

            def shared_in(g, n, b, f, w, banks, done):
                cols = slice(f * 128, (f + 1) * 128)
                count_ge(pe, sh_act, n - 1)
                product(banks[b][:, 0:GT], [(w[:, k, cols], hn2T[:, k, bass.ds(g * GT, GT)])
                                            for k in range(KC)]).then_inc(done, 1)

            def shared_down(g, p, half):
                pe.wait_ge(sh_act, FC_SH * g + FC_SH)
                count_ge(pe, sh_base, 2 * g + half - 1)
                for j in range(2 * half, 2 * half + 2):
                    ins = product(ps_y[half][0:TT, (j % 2) * C:(j % 2 + 1) * C],
                                  [(act_sh[p][:, f, j * TT:(j + 1) * TT], wsd_sb[:, f, :]) for f in range(FC_SH)])
                ins.then_inc(sh_y_mm, 1)

            def shared_group(g, p, search, first=False):
                def slot(k):
                    if search:
                        pe.wait_ge(counted, 8 * g + k + 1)
                        nc.tensor.matmul(ps_x[0][:, 0:1], onehot_sum[:], count[:], start=True,
                                         stop=True).then_inc(count_sum, 1)
                n, b = FC_SH * g, (FC_SH * p) % 2
                shared_in(g, n, b, 0, wsg_sb, ps_g, sh_g_mm)
                slot(0)
                shared_in(g, n, b, 0, wsu_sb, ps_u, sh_u_mm)
                slot(1)
                if not first:
                    shared_down(g - 1, 1 - p, 0)
                slot(2)
                if not first:
                    shared_down(g - 1, 1 - p, 1)
                slot(3)
                shared_in(g, n + 1, 1 - b, 1, wsg_sb, ps_g, sh_g_mm)
                slot(4)
                shared_in(g, n + 1, 1 - b, 1, wsu_sb, ps_u, sh_u_mm)
                slot(5)
                shared_in(g, n + 2, b, 2, wsg_sb, ps_g, sh_g_mm)
                slot(6)
                shared_in(g, n + 2, b, 2, wsu_sb, ps_u, sh_u_mm)
                slot(7)

            for g in range(GROUPS // 2):
                shared_group(g, g % 2, True, first=(g == 0))
            pe.wait_ge(totals_ready, 1)
            pe.wait_ge(route_seq, 1)
            nc.tensor.matmul(ps_x[0][:, 1:3], onehot_sum[:], totals[:], start=True, stop=True)
            nc.tensor.matmul(ps_x[0][:, 3:4], before[:], totals[:, 1:2], start=True, stop=True).then_inc(eq_mm, 1)
            shared_group(4, 0, False)
            pe.wait_ge(sel_total, 1)
            nc.tensor.matmul(ps_x[0][:, 4:5], before[:], room[:, 2:3], start=True, stop=True).then_inc(sel_mm, 1)
            shared_group(5, 1, False)
            pe.wait_ge(pos_ready, 1)
            for j in range(GROUP):
                ins = nc.tensor.transpose(ps_x[1][0:TT, j * 128:(j + 1) * 128], above[:, j * TT:(j + 1) * TT], ident[:])
            ins.then_inc(posT_mm, 1)
            shared_group(6, 0, False)
            shared_group(7, 1, False)
            shared_down(7, 1, 0)
            shared_down(7, 1, 1)
            pe.wait_ge(hot_ready, 1)
            pe.wait_ge(route_seq, 13)
            for e in range(EXPERTS):
                for t in range(TILES):
                    ins = nc.tensor.matmul(ps_x[0][0:HI, e * 2 * LO:(e + 1) * 2 * LO],
                                           hot_hi[:, t * EXPERTS + e, :],
                                           hot_id[:, t * EXPERTS + e, :, :].rearrange("p a l -> p (a l)"),
                                           start=(t == 0), stop=(t == TILES - 1))
            ins.then_inc(ids_mm, 1)

            def turn_in(e, p, first=False):
                pe.wait_ge(gathered[p], 32 * e - 32 * p + 64)
                if first:
                    pe.wait_ge(ids_ready, 1)
                else:
                    pe.wait_ge(xgT_ready, e)
                for k in range(KC):
                    for j in range(GROUP):
                        ins = nc.tensor.transpose(ps_x[k][0:HC, j * SLOTS:(j + 1) * SLOTS],
                                                  xg[p][:, j, k * HC:(k + 1) * HC], ident[0:SLOTS, 0:SLOTS])
                ins.then_inc(xgT_mm, 1)

            def expert_in(e, p, f, first=False):
                cols = slice(f * 128, (f + 1) * 128)
                if not (first and f < 2):
                    pe.wait_ge(act_ready, FC_EXP * e + (f - 1))
                product(ps_g[f % 2][:, 0:CAP], [(wg_sb[p][:, k, cols], xgT[p][:, k, :])
                                                for k in range(KC)]).then_inc(g_mm, 1)
                product(ps_u[f % 2][:, 0:CAP], [(wu_sb[p][:, k, cols], xgT[p][:, k, :])
                                                for k in range(KC)]).then_inc(u_mm, 1)

            def expert_down(e, p, first=False):
                pe.wait_ge(act_ready, FC_EXP * e + FC_EXP)
                for j in range(GROUP):
                    if j % 2 == 0 and not first:
                        pe.wait_ge(yo_ready, 2 * e + j // 2 - 1)
                    ins = product(ps_y[j // 2][0:SLOTS, (j % 2) * C:(j % 2 + 1) * C],
                                  [(act_ex[p][:, f, j * SLOTS:(j + 1) * SLOTS], wd_sb[p][:, f, :])
                                   for f in range(FC_EXP)])
                    if j % 2 == 1:
                        ins.then_inc(y_mm, 1)

            def expert(e, p, first=False, second=False, last=False):
                pe.wait_ge(xgT_ready, e + 1)
                pe.wait_ge(w_loaded[p], 24 * e - 24 * p + 48)
                expert_in(e, p, 0, first)
                if not first:
                    expert_down(e - 1, 1 - p, first=second)
                expert_in(e, p, 1, first)
                for f in range(2, FC_EXP):
                    expert_in(e, p, f)
                if not last:
                    turn_in(e + 1, 1 - p)

            turn_in(0, 0, first=True)
            pe.wait_ge(sh_base, 2 * GROUPS)
            pe.wait_ge(sh_act, FC_SH * GROUPS)
            expert(0, 0, first=True)
            expert(1, 1, second=True)
            with by_two(pe, 2, EXPERTS - 2) as e:
                expert(e, 0)
                expert(e + 1, 1)
            expert(EXPERTS - 2, 0)
            expert(EXPERTS - 1, 1, last=True)
            expert_down(EXPERTS - 1, 1)


def kernel(x, L0_tok_w, L0_attn_w_qkv, L0_attn_b_qkv, L0_attn_w_l, L0_attn_b_l, L0_attn_w_w, L0_attn_b_w,
           L0_attn_w_proj, L0_attn_b_proj, L0_ffn_gate_weight, L0_ffn_Wg, L0_ffn_Wu, L0_ffn_Wd,
           L0_ffn_Ws_g, L0_ffn_Ws_u, L0_ffn_Ws_d):
    import numpy as np
    import concourse.bacc as bacc
    from concourse.bass_utils import run_bass_kernel_spmd

    frames = np.asarray(x)[:, :POOL * WIN]
    halves = frames.reshape(TILES, SEQS, WIN, POOL, KC, HC)
    arrays = {
        "xT": halves.transpose(0, 5, 4, 3, 1, 2).reshape(TILES, HC, KC, POOL, TT),
        "xp": frames.reshape(TILES, TT, POOL, C),
        "w_tok": np.asarray(L0_tok_w),
        "w_qkv": np.asarray(L0_attn_w_qkv),
        "b_qkv": np.asarray(L0_attn_b_qkv).reshape(1, -1),
        "w_l": np.asarray(L0_attn_w_l),
        "b_l": np.asarray(L0_attn_b_l).reshape(1, -1),
        "w_w": np.asarray(L0_attn_w_w),
        "b_w": np.asarray(L0_attn_b_w).reshape(1, -1),
        "w_proj": np.asarray(L0_attn_w_proj),
        "b_proj": np.asarray(L0_attn_b_proj).reshape(1, -1),
        "w_gate": np.asarray(L0_ffn_gate_weight).T,
        "wg": np.asarray(L0_ffn_Wg).transpose(0, 2, 1).reshape(EXPERTS, KC, HC, F_EXP).transpose(0, 2, 1, 3),
        "wu": np.asarray(L0_ffn_Wu).transpose(0, 2, 1).reshape(EXPERTS, KC, HC, F_EXP).transpose(0, 2, 1, 3),
        "wd": np.asarray(L0_ffn_Wd).transpose(0, 2, 1).reshape(EXPERTS, FC_EXP, 128, C).transpose(0, 2, 1, 3),
        "wsg": np.asarray(L0_ffn_Ws_g).T,
        "wsu": np.asarray(L0_ffn_Ws_u).T,
        "wsd": np.asarray(L0_ffn_Ws_d).T,
    }
    nc = bacc.Bacc("TRN2", target_bir_lowering=False, num_devices=1)
    feeds, args = {}, []
    for name, a in arrays.items():
        feeds[f"in_{name}"] = np.ascontiguousarray(a)
        args.append(nc.dram_tensor(f"in_{name}", feeds[f"in_{name}"].shape, F32, kind="ExternalInput").ap())
    args.append(nc.dram_tensor("out_h", (BATCH, WIN, C), F32, kind="ExternalOutput").ap())
    audio_tower(nc, *args)
    r = run_bass_kernel_spmd(nc, [feeds], core_ids=[0])
    return r.results[0]["out_h"]
```

```python
from contextlib import ExitStack, contextmanager

import concourse.bass as bass
from concourse import mybir

ALU = mybir.AluOpType
ACT = mybir.ActivationFunctionType
AX = mybir.AxisListType
F32 = mybir.dt.float32
F32R = mybir.dt.float32r
BF16 = mybir.dt.bfloat16
I32 = mybir.dt.int32
U32 = mybir.dt.uint32

BATCH, FRAMES, C = 64, 125, 192
POOL = 2
WIN = (FRAMES - POOL) // POOL + 1
HEADS = 12
HD = C // HEADS
EXPERTS = 16
F_EXP = 4 * C
F_SH = F_EXP // 2
TOKENS = BATCH * WIN
TOP_K = 2
CAP = -(-TOKENS * TOP_K // EXPERTS)
LN_EPS = 1e-5

KC = 2
HC = C // KC
SEQS = 2
TT = SEQS * WIN
TILES = TOKENS // TT
HALF = HEADS // 2
PAIRS = HEADS // 2
SECOND = 64
SP_ = SECOND + WIN
ROW = C + EXPERTS
GROUP = 4
GT = GROUP * TT
GROUPS = TILES // GROUP
FC_SH = F_SH // 128
FC_EXP = F_EXP // 128
MAIN = 128
REM = C - MAIN
SPLIT_GROUP = 6
IN_PIECES, DOWN_PIECES = 4, 2
SLOTS = CAP // GROUP
HI = CAP // 16
LO = 16
SEARCH_BITS = 32
SPREAD = GROUPS

LEAD, LOOP_FROM, LOOP_TO, LAST = -3, 4, 28, TILES + 3


def count_ge(eng, sem, value):
    if isinstance(value, int) and value <= 0:
        return
    eng.wait_ge(sem, value)


def live(i, off):
    return not isinstance(i, int) or 0 <= i + off < TILES


def upto(t, off):
    if isinstance(t, int):
        return min(t + off + 1, TILES)
    return t + (off + 1)


@contextmanager
def by_two(eng, start, end):
    with eng.Fori(0, (end - start) // 2) as half:
        yield half * 2 + start


def pipeline(eng, body):
    for i in range(LEAD, LOOP_FROM):
        body(i, i % 2)
    with by_two(eng, LOOP_FROM, LOOP_TO) as r:
        body(r, 0)
        body(r + 1, 1)
    for i in range(LOOP_TO, LAST):
        body(i, i % 2)


def audio_tower(nc, xT, xp, w_tok, w_qkv, b_qkv, w_l, b_l, w_w, b_w, w_proj, b_proj,
                w_gate, w_main, w_rem, wd, wsg, wsu, wsd, out):
    out_rows = out.rearrange("b n c -> (b n) c")
    rows_dram = nc.dram_tensor("rows_scratch", (TOKENS, ROW), F32, kind="Internal").ap()
    score_dram = nc.dram_tensor("score_scratch", (EXPERTS, TOKENS), F32, kind="Internal").ap()
    ids_dram = nc.dram_tensor("ids_scratch", (EXPERTS, CAP), I32, kind="Internal").ap()

    with ExitStack() as ctx:
        ctx.enter_context(nc.allow_non_contiguous_dma(reason="layout of small tables"))

        def sb(name, shape, dt=F32, scope=ctx):
            return scope.enter_context(nc.sbuf_tensor(name, shape, dt))

        def sem(name):
            return ctx.enter_context(nc.semaphore(name))

        def sems(name, n=2):
            return [sem(f"{name}{i}") for i in range(n)]

        bank = [ctx.enter_context(nc.psum_tensor(f"bank{i}", [128, 512], F32)) for i in range(8)]

        ident = sb("ident", [128, 128])
        ffn_in = ExitStack()
        h_all = sb("h_all", [TT, TILES, C], F32, ffn_in)
        hn2T = sb("hn2T", [HC, KC, TOKENS], F32, ffn_in)
        ffn_in.close()
        x_hi = [sb(f"x_hi{p}", [MAIN, CAP], F32R) for p in range(2)]
        x_lo = [sb(f"x_lo{p}", [MAIN, CAP], F32R) for p in range(2)]
        x_rem = [sb(f"x_rem{p}", [2 * REM, CAP], F32R) for p in range(2)]
        act_hi = [sb(f"act_hi{p}", [128, FC_EXP, CAP], F32R) for p in range(2)]
        act_lo = [sb(f"act_lo{p}", [128, FC_EXP, CAP], F32R) for p in range(2)]
        w_gate_sb = sb("w_gate_sb", [HC, KC, EXPERTS])
        wsg_sb = sb("wsg_sb", [HC, KC, F_SH])
        wsu_sb = sb("wsu_sb", [HC, KC, F_SH])
        wsd_sb = sb("wsd_sb", [128, FC_SH, C])
        raw_in = sb("raw_in", [128, 2, 2, F_EXP])
        raw_down = sb("raw_down", [128, FC_EXP, C])
        idx_all = sb("idx_all", [SLOTS, EXPERTS, GROUP], I32)

        att = ExitStack()
        w_tok_sb = sb("w_tok_sb", [HC, KC, C], scope=att)
        w_qkv_sb = sb("w_qkv_sb", [HC + 1, KC, 3 * C], scope=att)
        w_proj_sb = sb("w_proj_sb", [HC + 1, KC, C], scope=att)
        mix_in = sb("mix_in", [HC, KC, HEADS], scope=att)
        mix_out = sb("mix_out", [2 * WIN, PAIRS, HEADS], scope=att)
        mix_bias = sb("mix_bias", [WIN, HEADS], scope=att)
        ones_win = sb("ones_win", [WIN, WIN], scope=att)
        bl_row = sb("bl_row", [HC + 1, HEADS], scope=att)
        minus_half = sb("minus_half", [TT, 1], scope=att)
        xT_in = [sb(f"xT_in{p}", [HC, KC, POOL, TT], scope=att) for p in range(2)]
        xp_in = [sb(f"xp_in{p}", [TT, POOL, C], scope=att) for p in range(2)]
        dT = [sb(f"dT{p}", [HC, KC, TT], scope=att) for p in range(2)]
        tanh_d = [sb(f"tanh_d{p}", [TT, C], scope=att) for p in range(2)]
        diff = sb("diff", [TT, C], scope=att)
        stats1 = sb("stats1", [TT, 12], scope=att)
        stats2 = sb("stats2", [TT, 12], scope=att)
        rstd1 = [sb(f"rstd1_{p}", [TT, 1], scope=att) for p in range(2)]
        rstd2 = [sb(f"rstd2_{p}", [TT, 1], scope=att) for p in range(2)]
        hn = [sb(f"hn{p}", [TT, C], scope=att) for p in range(2)]
        hnT = [sb(f"hnT{p}", [HC + 1, KC, SEQS, 2, WIN], scope=att) for p in range(2)]
        qT = [sb(f"qT{p}", [HC + 1, KC, TT], scope=att) for p in range(2)]
        kT = [sb(f"kT{p}", [HC, KC, TT], scope=att) for p in range(2)]
        ks = [sb(f"ks{p}", [HC + 1, KC, HEADS, TT], scope=att) for p in range(2)]
        v_sb = [sb(f"v_sb{p}", [2 * WIN, SEQS, C], scope=att) for p in range(2)]
        vs = [sb(f"vs{p}", [2 * WIN, SEQS, PAIRS + 1, C], scope=att) for p in range(2)]
        smax = sb("smax", [SP_, HEADS], scope=att)
        ssum = sb("ssum", [SP_, HEADS], scope=att)
        prob = [sb(f"prob{p}", [SP_, HEADS, WIN], scope=att) for p in range(2)]
        probT = [sb(f"probT{p}", [2 * WIN, PAIRS, SP_], scope=att) for p in range(2)]
        oT = [sb(f"oT{p}", [HC + 1, KC, TT], scope=att) for p in range(2)]
        row = [sb(f"row{p}", [TT, ROW], scope=att) for p in range(2)]
        scoreT = [sb(f"scoreT{p}", [EXPERTS, TT], scope=att) for p in range(2)]
        att.close()

        score = sb("score", [128, CAP])
        onehot_sum = sb("onehot_sum", [128, 128])
        before = sb("before", [128, 128])
        cand = sb("cand", [128, 1], U32)
        thr = sb("thr", [128, 1], U32)
        bit = sb("bit", [128, 1], U32)
        enough = sb("enough", [128, 1], U32)
        count = sb("count", [128, 1])
        above = sb("above", [128, CAP])
        equal = sb("equal", [128, CAP])
        scan = sb("scan", [128, CAP])
        zeros = sb("zeros", [128, CAP])
        picked = sb("picked", [128, CAP])
        totals = sb("totals", [128, 2])
        room = sb("room", [128, 3])
        act_sh = [sb(f"act_sh{p}", [128, FC_SH, GT]) for p in range(2)]
        silu = [sb(f"silu{p}", [128, GT]) for p in range(2)]
        base = [sb(f"base{p}", [TT, GROUP, C]) for p in range(2)]
        iota_p = sb("iota_p", [TT, 1])
        iota_t = sb("iota_t", [TT, TILES, EXPERTS], BF16)
        ids = sb("ids", [HI, EXPERTS, LO], I32)
        id_part = sb("id_part", [HI, EXPERTS, LO])
        idx_g = [sb(f"idx_g{p}", [SLOTS, GROUP], I32) for p in range(2)]
        idx_s = [sb(f"idx_s{p}", [SLOTS, GROUP], I32) for p in range(2)]
        xg = [sb(f"xg{p}", [SLOTS, GROUP, ROW]) for p in range(2)]
        top = [sb(f"top{p}", [SLOTS, GROUP]) for p in range(2)]
        scaled = sb("scaled", [SLOTS, C])
        yo = base
        act_full = [act_sh[p][:, 0, :] for p in range(2)]
        TE = TILES * EXPERTS
        hot = ExitStack()
        pos_i = sb("pos_i", [TT, TE], I32, hot)
        pos_j = sb("pos_j", [TT, TE], I32, hot)
        pos_hi = sb("pos_hi", [TT, TE], BF16, hot)
        pos_lo = sb("pos_lo", [TT, TE], BF16, hot)
        hot_hi = sb("hot_hi", [TT, HI, TE], BF16, hot)
        hot_id = sb("hot_id", [TT, 2, LO, TE], BF16, hot)
        hot.close()
        w_hi = [sb(f"w_hi{p}", [128, 2, 2, F_EXP], F32R) for p in range(2)]
        w_lo = [sb(f"w_lo{p}", [128, 2, 2, F_EXP], F32R) for p in range(2)]
        w_down = [sb(f"w_down{p}", [128, FC_EXP, 2, C], F32R) for p in range(2)]
        ps_s = [bank[0], bank[1]]
        ps_gate = bank[0][0:EXPERTS, 372:372 + TT]
        ps_pt = [bank[2], bank[3]]
        ps_qk = bank[4][0:HC, 0:4 * TT].rearrange("p (a n) -> p a n", a=4)
        ps_v = bank[5][0:2 * WIN, 0:SEQS * C].rearrange("p (s c) -> p s c", s=SEQS)
        ps_sct = bank[5][0:TT, 384:384 + EXPERTS]
        ps_hT = bank[6][0:HC, 0:KC * TT].rearrange("p (k n) -> p k n", k=KC)
        ps_pool = bank[6][0:TT, 256:256 + C]
        ps_o = bank[7][0:HC, 0:KC * TT].rearrange("p (k n) -> p k n", k=KC)
        ps_r = bank[7][0:TT, 256:256 + C]
        ps_g, ps_u, ps_y, ps_x = bank[0:2], bank[2:4], bank[4:6], bank[6:8]

        tok_loaded = sem("tok_loaded")
        qkv_loaded = sem("qkv_loaded")
        mix_in_loaded = sem("mix_in_loaded")
        mix_out_loaded = sem("mix_out_loaded")
        proj_loaded = sem("proj_loaded")
        ffn_loaded = sem("ffn_loaded")
        const_pool = sem("const_pool")
        const_dve = sem("const_dve")
        x_loaded = sems("x_loaded")
        dT_ready = sem("dT_ready")
        pool_mm = sem("pool_mm")
        pool_tanh = sem("pool_tanh")
        pool_seq = sem("pool_seq")
        var1_ready = sem("var1_ready")
        rstd1_ready = sem("rstd1_ready")
        hn_ready = sem("hn_ready")
        hnT_mm = sem("hnT_mm")
        hnT_ready = sem("hnT_ready")
        qk_mm = sem("qk_mm")
        v_mm = sem("v_mm")
        q_ready = sem("q_ready")
        k_ready = sem("k_ready")
        v_ready = sem("v_ready")
        ks0_ready = sem("ks0_ready")
        ks1_ready = sem("ks1_ready")
        vs0_ready = sem("vs0_ready")
        vs1_ready = sem("vs1_ready")
        s_mm = sem("s_mm")
        soft_seq = sem("soft_seq")
        shifted = sem("shifted")
        exp_done = sem("exp_done")
        prob_ready = sem("prob_ready")
        pt_mm = sem("pt_mm")
        probT_ready = sem("probT_ready")
        o_mm = sem("o_mm")
        oT_ready = sem("oT_ready")
        r_mm = sem("r_mm")
        res_seq = sem("res_seq")
        var2_ready = sem("var2_ready")
        rstd2_ready = sem("rstd2_ready")
        hn2_ready = sem("hn2_ready")
        hn2T_mm = sem("hn2T_mm")
        hn2T_ready = sem("hn2T_ready")
        gate_mm = sem("gate_mm")
        gate_tanh = sem("gate_tanh")
        score_ready = sem("score_ready")
        sct_mm = sem("sct_mm")
        row_ready = sem("row_ready")
        row_stored = sems("row_stored")
        in_loaded = sem("in_loaded")
        down_loaded = sem("down_loaded")
        score_loaded = sem("score_loaded")
        counted = sem("counted")
        count_sum = sem("count_sum")
        find_seq = sem("find_seq")
        sh_g_mm = sem("sh_g_mm")
        sh_u_mm = sem("sh_u_mm")
        sh_silu = sem("sh_silu")
        sh_act = sem("sh_act")
        sh_y_mm = sem("sh_y_mm")
        sh_base = sem("sh_base")
        base_stored = sems("base_stored")
        route_seq = sem("route_seq")
        totals_ready = sem("totals_ready")
        eq_mm = sem("eq_mm")
        sel_total = sem("sel_total")
        sel_mm = sem("sel_mm")
        pos_ready = sem("pos_ready")
        posT_mm = sem("posT_mm")
        hot_lo_ready = sem("hot_lo_ready")
        hot_tile_ready = sem("hot_tile_ready")
        hot_ready = sem("hot_ready")
        ids_mm = sem("ids_mm")
        ids_ready = sem("ids_ready")
        ids_stored = sem("ids_stored")
        idx_loaded = sem("idx_loaded")
        idx_g_ready = sem("idx_g_ready")
        idx_s_ready = sem("idx_s_ready")
        gathered = sems("gathered")
        scattered = sem("scattered")
        top_ready = sem("top_ready")
        xgT_mm = sem("xgT_mm")
        x_hi_ready = sem("x_hi_ready")
        x_lo_ready = sem("x_lo_ready")
        w_hi_ready = sem("w_hi_ready")
        down_hi_ready = sem("down_hi_ready")
        w_lo_ready = sem("w_lo_ready")
        down_lo_ready = sem("down_lo_ready")
        g_mm = sem("g_mm")
        u_mm = sem("u_mm")
        silu_ready = sem("silu_ready")
        act_ready = sem("act_ready")
        act_hi_ready = sem("act_hi_ready")
        act_lo_ready = sem("act_lo_ready")
        y_mm = sem("y_mm")
        scaled_ready = sem("scaled_ready")
        yo_ready = sem("yo_ready")
        own_waits = {e.engine: sem(f"own_waits_{n}") for n, e in
                     (("sp", nc.sync), ("pool", nc.gpsimd), ("pe", nc.tensor), ("dve", nc.vector))}

        def attention_over(eng):
            for s in (hn2T_ready, row_ready, gate_tanh, score_ready, prob_ready, hn2_ready, oT_ready,
                      o_mm, r_mm, sct_mm, gate_mm, pt_mm, v_mm, s_mm, vs0_ready, vs1_ready, ks0_ready,
                      ks1_ready, probT_ready, rstd2_ready, exp_done, hn2T_mm):
                eng.wait_ge(s, TILES)
            for s in row_stored:
                eng.wait_ge(s, 32 * (TILES // 2))

        def scale_values(eng, p, s):
            shape = [2 * WIN, PAIRS, HEADS, HD]
            return eng.tensor_tensor(
                vs[p][:, s, 0:PAIRS, :].rearrange("p j (g d) -> p j g d", d=HD),
                v_sb[p][:, s, :].rearrange("p (g d) -> p g d", d=HD).unsqueeze(1).to_broadcast(shape),
                mix_out[:].unsqueeze(3).to_broadcast(shape), ALU.mult)

        def stored_of(t, p, off):
            if isinstance(t, int):
                return 32 * ((t + off - p) // 2 + 1)
            return 16 * t + 16 * (off - p + 2)

        def apart(eng):
            eng.sem_inc(own_waits[eng.engine], 1)

        block = ctx.enter_context(nc.Block())

        @block.sync
        def _(sp):
            def load_x(t, p):
                count_ge(sp, dT_ready, upto(t, -2))
                apart(sp)
                count_ge(sp, pool_seq, 5 * upto(t, -2))
                apart(sp)
                sp.dma_start(xT_in[p][:], xT[t]).then_inc(x_loaded[p], 16)
                sp.dma_start(xp_in[p][:], xp[t]).then_inc(x_loaded[p], 16)

            halves = "(k p) n -> p k n"
            load_x(0, 0)
            sp.dma_start(w_tok_sb[:], w_tok.rearrange(halves, k=KC)).then_inc(tok_loaded, 16)
            sp.dma_start(w_qkv_sb[0:HC], w_qkv.rearrange(halves, k=KC)).then_inc(qkv_loaded, 16)
            sp.dma_start(w_qkv_sb[HC:HC + 1, 0, :], b_qkv).then_inc(qkv_loaded, 16)
            load_x(1, 1)
            for half in range(2):
                for j in range(PAIRS):
                    h = 2 * j + half
                    sp.dma_start(mix_out[half * WIN:(half + 1) * WIN, j, :],
                                 w_w[h:h + 1, :].to_broadcast([WIN, HEADS])).then_inc(mix_out_loaded, 16)
            sp.dma_start(mix_bias[:], b_w.to_broadcast([WIN, HEADS])).then_inc(mix_out_loaded, 16)
            sp.dma_start(w_proj_sb[0:HC], w_proj.rearrange(halves, k=KC)).then_inc(proj_loaded, 16)
            sp.dma_start(w_proj_sb[HC:HC + 1, 0, :], b_proj).then_inc(proj_loaded, 16)
            sp.dma_start(w_gate_sb[:], w_gate.rearrange(halves, k=KC)).then_inc(ffn_loaded, 16)
            sp.dma_start(wsg_sb[:], wsg.rearrange(halves, k=KC)).then_inc(ffn_loaded, 16)
            sp.dma_start(wsu_sb[:], wsu.rearrange(halves, k=KC)).then_inc(ffn_loaded, 16)
            sp.dma_start(wsd_sb[:], wsd.rearrange("(f p) n -> p f n", p=128)).then_inc(ffn_loaded, 16)

            def load_in(e):
                sp.dma_start(raw_in[:, :, 0, :], w_main[e]).then_inc(in_loaded, 16)
                sp.dma_start(raw_in[0:REM, :, 1, :], w_rem[e]).then_inc(in_loaded, 16)
                sp.dma_start(raw_in[REM:2 * REM, :, 1, :], w_rem[e]).then_inc(in_loaded, 16)

            def load_down(e):
                sp.dma_start(raw_down[:], wd[e]).then_inc(down_loaded, 16)

            load_in(0)
            load_down(0)

            def step(i, par):
                if live(i, -3):
                    t, p = i - 3, (par + 1) % 2
                    sp.wait_ge(row_ready, upto(t, 0))
                    apart(sp)
                    sp.dma_start(rows_dram[bass.ds(t * TT, TT), :], row[p][:]).then_inc(row_stored[p], 16)
                    sp.dma_start(score_dram[:, bass.ds(t * TT, TT)], scoreT[p][:]).then_inc(row_stored[p], 16)
                if live(i, 4) and not (isinstance(i, int) and i + 4 < 2):
                    load_x(i + 4, par)

            pipeline(sp, step)

            attention_over(sp)
            for c in range(SPREAD):
                sp.dma_start(score[c * EXPERTS:(c + 1) * EXPERTS, :],
                             score_dram[:, c * CAP:(c + 1) * CAP]).then_inc(score_loaded, 16)

            def store_base(g, p):
                sp.wait_ge(sh_base, 2 * g + 2)
                apart(sp)
                sp.dma_start(out_rows[bass.ds(g * GT, GT), :].rearrange("(j p) c -> p j c", p=TT),
                             base[p][:]).then_inc(base_stored[p], 16)

            with by_two(sp, 0, GROUPS) as g:
                store_base(g, 0)
                store_base(g + 1, 1)
            sp.wait_ge(ids_ready, 1)
            sp.dma_start(ids_dram.rearrange("e (h l) -> h e l", l=LO), ids[:]).then_inc(ids_stored, 16)
            sp.wait_ge(ids_stored, 16)
            sp.dma_start(idx_all[:], ids_dram.rearrange("e (p j) -> p e j", j=GROUP)).then_inc(idx_loaded, 16)

            def next_expert(e):
                sp.wait_ge(w_lo_ready, IN_PIECES * e)
                apart(sp)
                load_in(e)
                sp.wait_ge(down_lo_ready, DOWN_PIECES * e)
                apart(sp)
                load_down(e)

            with sp.Fori(1, EXPERTS) as e:
                next_expert(e)
            for s in base_stored:
                sp.wait_ge(s, 16 * (GROUPS // 2))
            sp.wait_ge(scattered, 64 * EXPERTS)

        @block.gpsimd
        def _(pool):
            pool.memset(ident[:], 0.0).then_inc(const_pool, 1)
            pool.memset(minus_half[:], -0.5).then_inc(const_pool, 1)
            pool.memset(ones_win[:], 1.0).then_inc(const_pool, 1)
            pool.wait_ge(const_pool, 3)
            pool.affine_select(out=ident[:], in_=ident[:], compare_op=ALU.not_equal, fill=1.0,
                               base=0, pattern=[[-1, 128]], channel_multiplier=1).then_inc(const_pool, 1)
            pool.wait_ge(mix_in_loaded, 16 * (HEADS + 1))
            pool.wait_ge(mix_out_loaded, 16 * (HEADS + 1))

            def step(i, par):
                if live(i, 1):
                    t, p = i + 1, (par + 1) % 2
                    pool.wait_ge(k_ready, upto(t, 0))
                    count_ge(pool, s_mm, upto(t, -2))
                    pool.tensor_tensor(ks[p][0:HC, 1], kT[p][:, 1, :].unsqueeze(1).to_broadcast([HC, HEADS, TT]),
                                       mix_in[:, 1, :].unsqueeze(2).to_broadcast([HC, HEADS, TT]),
                                       ALU.mult).then_inc(ks1_ready, 1)
                if live(i, 2):
                    t, p = i + 2, par
                    pool.wait_ge(var1_ready, upto(t, 0))
                    count_ge(pool, hn_ready, upto(t, -2))
                    pool.tensor_tensor(rstd1[p][:], stats1[:, 8:9], minus_half[:], ALU.pow).then_inc(rstd1_ready, 1)
                if live(i, -1):
                    t, p = i - 1, (par + 1) % 2
                    pool.wait_ge(var2_ready, upto(t, 0))
                    count_ge(pool, hn2_ready, upto(t, -2))
                    pool.tensor_tensor(rstd2[p][:], stats2[:, 8:9], minus_half[:], ALU.pow).then_inc(rstd2_ready, 1)
                if live(i, 1):
                    t, p = i + 1, (par + 1) % 2
                    pool.wait_ge(v_ready, upto(t, 0))
                    count_ge(pool, o_mm, upto(t, -2))
                    scale_values(pool, p, 0).then_inc(vs0_ready, 1)

            pipeline(pool, step)

            attention_over(pool)
            pool.memset(onehot_sum[:], 0.0).then_inc(const_pool, 1)
            pool.memset(before[:], 0.0).then_inc(const_pool, 1)
            pool.wait_ge(const_pool, 6)
            for d in range(-(SPREAD - 1), SPREAD):
                pool.affine_select(out=onehot_sum[:], in_=onehot_sum[:], compare_op=ALU.not_equal, fill=1.0,
                                   base=d * EXPERTS, pattern=[[-1, 128]],
                                   channel_multiplier=1).then_inc(const_pool, 1)
                pool.wait_ge(const_pool, 6 + d + SPREAD)
            for d in range(1, SPREAD):
                pool.affine_select(out=before[:], in_=before[:], compare_op=ALU.not_equal, fill=1.0,
                                   base=d * EXPERTS, pattern=[[-1, 128]],
                                   channel_multiplier=1).then_inc(const_pool, 1)
                pool.wait_ge(const_pool, 5 + 2 * SPREAD + d)
            pool.memset(zeros[:], 0.0).then_inc(const_pool, 1)
            pool.iota(iota_p[:], [[0, 1]], base=0, channel_multiplier=1,
                      allow_small_or_imprecise_dtypes=True).then_inc(const_pool, 1)
            pool.iota(iota_t[:], [[1, TILES], [0, EXPERTS]], base=0, channel_multiplier=0,
                      allow_small_or_imprecise_dtypes=True).then_inc(const_pool, 1)
            pool.wait_ge(const_pool, 7 + 3 * SPREAD)
            for l in range(LO):
                pool.wait_ge(hot_lo_ready, l + 1)
                pool.tensor_tensor(hot_id[:, 0, l, :], hot_id[:, 0, l, :], iota_t[:].rearrange("p t e -> p (t e)"),
                                   ALU.mult).then_inc(hot_tile_ready, 1)

            def gather(e, p):
                count_ge(pool, gathered[p], 32 * e - 32 * p)
                apart(pool)
                pool.tensor_copy(idx_g[p][:], idx_all[:, bass.ds(e, 1), :].rearrange("p a j -> p (a j)")
                                 ).then_inc(idx_g_ready, 1)
                count_ge(pool, xgT_mm, e - 1)
                count_ge(pool, top_ready, e - 1)
                pool.wait_ge(idx_g_ready, e + 1)
                apart(pool)
                for j in range(GROUP):
                    pool.indirect_dma_start(out=xg[p][:, j, :], out_offset=None, in_=rows_dram,
                                            in_offset=bass.IndirectOffsetOnAxis(
                                                ap=idx_g[p][:, j:j + 1].bitcast(U32), axis=0)
                                            ).then_inc(gathered[p], 16)

            def scatter(e, p):
                count_ge(pool, scattered, 64 * e)
                apart(pool)
                pool.tensor_copy(idx_s[p][:], idx_all[:, bass.ds(e, 1), :].rearrange("p a j -> p (a j)")
                                 ).then_inc(idx_s_ready, 1)
                pool.wait_ge(yo_ready, GROUP * e + GROUP)
                pool.wait_ge(idx_s_ready, e + 1)
                apart(pool)
                for j in range(GROUP):
                    pool.indirect_dma_start(out=out_rows, out_offset=bass.IndirectOffsetOnAxis(
                        ap=idx_s[p][:, j:j + 1].bitcast(U32), axis=0),
                        in_=yo[p][:, j, :], in_offset=None, compute_op=ALU.add).then_inc(scattered, 16)

            pool.wait_ge(idx_loaded, 16)
            gather(0, 0)
            gather(1, 1)
            for s in base_stored:
                pool.wait_ge(s, 16 * (GROUPS // 2))

            def turn(e, p):
                gather(e + 1, 1 - p)
                scatter(e - 1, 1 - p)

            turn(1, 1)
            with by_two(pool, 2, EXPERTS - 2) as e:
                turn(e, 0)
                turn(e + 1, 1)
            turn(EXPERTS - 2, 0)
            scatter(EXPERTS - 2, 0)
            scatter(EXPERTS - 1, 1)

        @block.scalar
        def _(act):
            for h in range(HEADS):
                k, r = divmod(h * HD, HC)
                act.dma_start(mix_in[r:r + HD, k, :],
                              w_l[h:h + 1, :].to_broadcast([HD, HEADS])).then_inc(mix_in_loaded, 16)
            act.dma_start(bl_row[HC:HC + 1, :], b_l).then_inc(mix_in_loaded, 16)

            def step(i, par):
                if live(i, -2):
                    t = i - 2
                    act.wait_ge(hn2T_mm, upto(t, 0))
                    nc.scalar.copy(hn2T[:, :, bass.ds(t * TT, TT)], ps_hT).then_inc(hn2T_ready, 1)
                if live(i, 1):
                    t, p = i + 1, (par + 1) % 2
                    act.wait_ge(qk_mm, upto(t, 0))
                    count_ge(act, ks0_ready, upto(t, -2))
                    count_ge(act, ks1_ready, upto(t, -2))
                    nc.scalar.copy(kT[p][:], ps_qk[:, 2:4, :]).then_inc(k_ready, 1)
                    count_ge(act, s_mm, upto(t, -2))
                    nc.scalar.mul(qT[p][0:HC], ps_qk[:, 0:2, :], float(HD) ** -0.5).then_inc(q_ready, 1)
                if live(i, -3):
                    t, p = i - 3, (par + 1) % 2
                    act.wait_ge(sct_mm, upto(t, 0))
                    nc.scalar.copy(row[p][:, C:ROW], ps_sct).then_inc(row_ready, 1)
                if live(i, 0):
                    t, p = i, par
                    act.wait_ge(shifted, upto(t, 0))
                    nc.scalar.activation(prob[p][:], prob[p][:], ACT.Exp).then_inc(exp_done, 1)
                if live(i, 1):
                    t, p = i + 1, (par + 1) % 2
                    act.wait_ge(v_mm, upto(t, 0))
                    count_ge(act, vs0_ready, upto(t, -2))
                    count_ge(act, vs1_ready, upto(t, -2))
                    nc.scalar.copy(v_sb[p][:], ps_v).then_inc(v_ready, 1)
                if live(i, 2):
                    t, p = i + 2, par
                    act.wait_ge(pool_mm, upto(t, 0))
                    count_ge(act, pool_seq, 5 * upto(t, -2))
                    nc.scalar.activation(tanh_d[p][:], ps_pool, ACT.Tanh, scale=0.5).then_inc(pool_tanh, 1)
                if live(i, -1):
                    t, p = i - 1, (par + 1) % 2
                    act.wait_ge(o_mm, upto(t, 0))
                    count_ge(act, r_mm, upto(t, -2))
                    nc.scalar.copy(oT[p][0:HC], ps_o).then_inc(oT_ready, 1)
                if live(i, -2):
                    t, p = i - 2, par
                    act.wait_ge(gate_mm, upto(t, 0))
                    count_ge(act, sct_mm, upto(t, -2))
                    if not (isinstance(t, int) and t < 2):
                        act.wait_ge(row_stored[p], stored_of(t, p, -2))
                    nc.scalar.activation(scoreT[p][:], ps_gate, ACT.Tanh, scale=0.5).then_inc(gate_tanh, 1)
                if live(i, 0):
                    t, p = i, par
                    act.wait_ge(pt_mm, upto(t, 0))
                    count_ge(act, o_mm, upto(t, -2))
                    for b in range(2):
                        ins = nc.scalar.copy(probT[p][:, 3 * b:3 * b + 3, :],
                                             ps_pt[b][0:2 * WIN, 0:3 * SP_].rearrange("p (a n) -> p a n", a=3))
                    ins.then_inc(probT_ready, 1)
                if live(i, -2):
                    t, p = i - 2, par
                    act.wait_ge(gate_tanh, upto(t, 0))
                    nc.scalar.activation(scoreT[p][:], scoreT[p][:], ACT.Copy, bias=0.5, scale=0.5
                                         ).then_inc(score_ready, 1)
                if live(i, 2):
                    t, p = i + 2, par
                    act.wait_ge(hnT_mm, upto(t, 0))
                    count_ge(act, v_mm, upto(t, -2))
                    for k in range(KC):
                        ins = nc.scalar.copy(hnT[p][0:HC, k], ps_hT[:, k, :].rearrange("p (s m) -> p s m", s=SEQS)
                                             .unsqueeze(2).to_broadcast([HC, SEQS, 2, WIN]))
                    ins.then_inc(hnT_ready, 1)

            pipeline(act, step)
            attention_over(act)

            def shared_silu(n, b):
                act.wait_ge(sh_g_mm, n + 1)
                count_ge(act, sh_act, n - 1)
                nc.scalar.activation(silu[b][:], ps_g[b][:, 0:GT], ACT.Silu).then_inc(sh_silu, 1)

            for n in range(2):
                shared_silu(n, n)
            with by_two(act, 2, FC_SH * SPLIT_GROUP) as n:
                shared_silu(n, 0)
                shared_silu(n + 1, 1)

            def split_high(e, p, m):
                act.wait_ge(in_loaded, 48 * e + 48)
                count_ge(act, u_mm, FC_EXP * (e - 1))
                nc.scalar.copy(w_hi[p][:, m], raw_in[:, m]).then_inc(w_hi_ready, 1)

            act.wait_ge(ids_mm, 1)
            split_high(0, 0, 0)
            split_high(0, 0, 1)
            with by_two(act, FC_SH * SPLIT_GROUP, FC_SH * GROUPS) as n:
                shared_silu(n, 0)
                shared_silu(n + 1, 1)

            def split_down(e, p):
                act.wait_ge(down_loaded, 16 * e + 16)
                count_ge(act, y_mm, GROUP * (e - 1))
                nc.scalar.copy(w_down[p][:, :, 0, :], raw_down[:]).then_inc(down_hi_ready, 1)

            def x_high(e, p):
                act.wait_ge(xgT_mm, e + 1)
                count_ge(act, u_mm, FC_EXP * (e - 1))
                nc.scalar.copy(x_hi[p][:], ps_x[0][0:MAIN, 0:CAP]).then_inc(x_hi_ready, 1)
                nc.scalar.copy(x_rem[p][0:REM], ps_x[1][0:REM, 0:CAP]).then_inc(x_hi_ready, 1)

            def expert_silu(e, f):
                act.wait_ge(g_mm, FC_EXP * e + (f + 1))
                count_ge(act, act_ready, FC_EXP * e + (f - 1))
                nc.scalar.activation(silu[f % 2][:], ps_g[f % 2][:, 0:CAP], ACT.Silu).then_inc(silu_ready, 1)

            def act_high(e, p, f):
                act.wait_ge(act_ready, FC_EXP * e + (f + 1))
                if f == 0:
                    count_ge(act, y_mm, GROUP * (e - 1))
                nc.scalar.copy(act_hi[p][:, f, :], act_full[f % 2]).then_inc(act_hi_ready, 1)

            def expert(e, p, last=False):
                expert_silu(e, 0)
                expert_silu(e, 1)
                act_high(e, p, 0)
                act_high(e, p, 1)
                if not last:
                    split_high(e + 1, 1 - p, 0)
                    split_high(e + 1, 1 - p, 1)
                expert_silu(e, 2)
                expert_silu(e, 3)
                act_high(e, p, 2)
                if not last:
                    split_down(e + 1, 1 - p)
                    x_high(e + 1, 1 - p)
                expert_silu(e, 4)
                act_high(e, p, 3)
                expert_silu(e, 5)
                act_high(e, p, 4)
                act_high(e, p, 5)

            split_down(0, 0)
            act.wait_ge(sh_base, 2 * GROUPS)
            act.wait_ge(sh_act, FC_SH * GROUPS)
            act.wait_ge(sh_y_mm, 2 * GROUPS)
            x_high(0, 0)
            expert(0, 0)
            expert(1, 1)
            with by_two(act, 2, EXPERTS - 2) as e:
                expert(e, 0)
                expert(e + 1, 1)
            expert(EXPERTS - 2, 0)
            expert(EXPERTS - 1, 1, last=True)

        @block.vector
        def _(dve):
            def loaded_of(t, p):
                return 32 * ((t - p) // 2 + 1) if isinstance(t, int) else 16 * t + 16 * (2 - p)

            def difference(t, p):
                dve.wait_ge(x_loaded[p], loaded_of(t, p))
                count_ge(dve, pool_mm, upto(t, -2))
                dve.tensor_tensor(dT[p][:], xT_in[p][:, :, 0, :], xT_in[p][:, :, 1, :],
                                  ALU.subtract).then_inc(dT_ready, 1)

            def normalise(t, p, src, dst, stats, var_ready, rstd, rstd_ready, seq, n, done):
                apart(dve)
                dve.bn_stats(stats[:, 0:6], src).then_inc(seq, 1)
                dve.wait_ge(seq, n + 1)
                apart(dve)
                dve.bn_aggr(stats[:, 6:8], stats[:, 0:6]).then_inc(seq, 1)
                dve.wait_ge(seq, n + 2)
                dve.tensor_scalar(stats[:, 8:9], stats[:, 7:8], LN_EPS, None, ALU.add).then_inc(var_ready, 1)
                dve.wait_ge(rstd_ready, upto(t, 0))
                return dve.tensor_scalar(dst, src, stats[:, 6:7], rstd[:, 0:1], ALU.subtract, ALU.mult)

            def scaled_keys(t, p):
                dve.wait_ge(k_ready, upto(t, 0))
                count_ge(dve, s_mm, upto(t, -2))
                dve.tensor_tensor(ks[p][0:HC, 0], kT[p][:, 0, :].unsqueeze(1).to_broadcast([HC, HEADS, TT]),
                                  mix_in[:, 0, :].unsqueeze(2).to_broadcast([HC, HEADS, TT]),
                                  ALU.mult).then_inc(ks0_ready, 1)

            for p in range(2):
                for buf in (hnT, qT, oT):
                    dve.memset(buf[p][HC:HC + 1, 0], 1.0).then_inc(const_dve, 1)
                dve.wait_ge(mix_in_loaded, 16 * (HEADS + 1))
                dve.tensor_copy(ks[p][HC:HC + 1, 0], bl_row[HC:HC + 1, :].unsqueeze(2)
                                .to_broadcast([1, HEADS, TT])).then_inc(const_dve, 1)

            dve.wait_ge(mix_out_loaded, 16 * (HEADS + 1))

            def step(i, par):
                if live(i, 0):
                    t, p = i, par
                    s_view = [ps_s[b][0:SP_, 0:HALF * WIN].rearrange("p (g m) -> p g m", m=WIN) for b in range(2)]
                    dve.wait_ge(s_mm, upto(t, 0))
                    for b in range(2):
                        dve.tensor_reduce(smax[:, HALF * b:HALF * (b + 1)], s_view[b], AX.X,
                                          ALU.max).then_inc(soft_seq, 1)
                    dve.wait_ge(soft_seq, 4 * upto(t, -1) + 2)
                    count_ge(dve, pt_mm, upto(t, -2))
                    for b in range(2):
                        ins = dve.tensor_tensor(
                            prob[p][:, HALF * b:HALF * (b + 1), :], s_view[b],
                            smax[:, HALF * b:HALF * (b + 1)].unsqueeze(2).to_broadcast([SP_, HALF, WIN]),
                            ALU.subtract)
                    ins.then_inc(shifted, 1)
                if live(i, 1):
                    scaled_keys(i + 1, (par + 1) % 2)
                if live(i, 0):
                    t, p = i, par
                    dve.wait_ge(exp_done, upto(t, 0))
                    dve.tensor_reduce(ssum[:], prob[p][:], AX.X, ALU.add).then_inc(soft_seq, 1)
                    dve.wait_ge(soft_seq, 4 * upto(t, -1) + 3)
                    dve.reciprocal(ssum[:], ssum[:]).then_inc(soft_seq, 1)
                    dve.wait_ge(soft_seq, 4 * upto(t, 0))
                    dve.tensor_tensor(prob[p][:], prob[p][:], ssum[:].unsqueeze(2).to_broadcast([SP_, HEADS, WIN]),
                                      ALU.mult).then_inc(prob_ready, 1)
                if live(i, 2):
                    t, p = i + 2, par
                    n = 5 * upto(t, -1)
                    h_t = h_all[:, bass.ds(t, 1), :].rearrange("p a c -> p (a c)")
                    dve.wait_ge(x_loaded[p], loaded_of(t, p))
                    dve.tensor_tensor(diff[:], xp_in[p][:, 0, :], xp_in[p][:, 1, :],
                                      ALU.subtract).then_inc(pool_seq, 1)
                    dve.wait_ge(pool_seq, n + 1)
                    dve.wait_ge(pool_tanh, upto(t, 0))
                    dve.scalar_tensor_tensor(out=diff[:], in0=tanh_d[p][:], scalar=1.0, in1=diff[:],
                                             op0=ALU.add, op1=ALU.mult).then_inc(pool_seq, 1)
                    dve.wait_ge(pool_seq, n + 2)
                    dve.scalar_tensor_tensor(out=h_t, in0=diff[:], scalar=0.5, in1=xp_in[p][:, 1, :],
                                             op0=ALU.mult, op1=ALU.add).then_inc(pool_seq, 1)
                    dve.wait_ge(pool_seq, n + 3)
                    count_ge(dve, hnT_mm, upto(t, -2))
                    normalise(t, p, h_t, hn[p][:], stats1, var1_ready, rstd1[p], rstd1_ready,
                              pool_seq, n + 3, None).then_inc(hn_ready, 1)
                if live(i, -1):
                    t, p = i - 1, (par + 1) % 2
                    n = 3 * upto(t, -1)
                    h_t = h_all[:, bass.ds(t, 1), :].rearrange("p a c -> p (a c)")
                    dve.wait_ge(r_mm, upto(t, 0))
                    dve.tensor_tensor(h_t, h_t, ps_r, ALU.add).then_inc(res_seq, 1)
                    dve.wait_ge(res_seq, n + 1)
                    count_ge(dve, hn2T_mm, upto(t, -2))
                    if not (isinstance(t, int) and t < 2):
                        dve.wait_ge(row_stored[p], stored_of(t, p, -2))
                    normalise(t, p, h_t, row[p][:, 0:C], stats2, var2_ready, rstd2[p], rstd2_ready,
                              res_seq, n + 1, None).then_inc(hn2_ready, 1)
                if live(i, 1):
                    t, p = i + 1, (par + 1) % 2
                    dve.wait_ge(v_ready, upto(t, 0))
                    count_ge(dve, o_mm, upto(t, -2))
                    scale_values(dve, p, 1)
                    dve.tensor_tensor(
                        vs[p][0:WIN, :, PAIRS, :].rearrange("p s (g d) -> p s g d", d=HD),
                        v_sb[p][0:WIN].rearrange("p s (g d) -> p s g d", d=HD),
                        mix_bias[:].unsqueeze(1).unsqueeze(3).to_broadcast([WIN, SEQS, HEADS, HD]),
                        ALU.mult).then_inc(vs1_ready, 1)
                if live(i, 3):
                    difference(i + 3, (par + 1) % 2)

            pipeline(dve, step)
            attention_over(dve)

            dve.memset(thr[:], 0).then_inc(find_seq, 1)
            dve.memset(bit[:], 1 << 30).then_inc(find_seq, 1)
            dve.wait_ge(find_seq, 2)
            dve.wait_ge(score_loaded, 16 * SPREAD)

            def try_bit(s):
                dve.tensor_tensor(cand[:], thr[:], bit[:], ALU.bitwise_or).then_inc(find_seq, 1)
                dve.wait_ge(find_seq, 5 * s + 3)
                dve.tensor_scalar(above[:], score[:], cand[:].bitcast(F32), 0.0, ALU.is_ge, ALU.add,
                                  accum_out=count[:]).then_inc(counted, 1)

            def keep_bit(s):
                dve.wait_ge(count_sum, s + 1)
                dve.tensor_scalar(enough[:], ps_x[0][:, 0:1], float(CAP), None, ALU.is_ge).then_inc(find_seq, 1)
                dve.wait_ge(find_seq, 5 * s + 4)
                dve.copy_predicated(thr[:], enough[:], cand[:]).then_inc(find_seq, 1)
                dve.tensor_scalar(bit[:], bit[:], 1, None, ALU.logical_shift_right).then_inc(find_seq, 1)
                dve.wait_ge(find_seq, 5 * s + 6)
                dve.engine_nop().then_inc(find_seq, 1)
                dve.wait_ge(find_seq, 5 * s + 7)

            def shared_act(n, b, p, f):
                dve.wait_ge(sh_silu, n + 1)
                dve.wait_ge(sh_u_mm, n + 1)
                dve.tensor_tensor(act_sh[p][:, f, :], silu[b][:], ps_u[b][:, 0:GT], ALU.mult).then_inc(sh_act, 1)

            def shared_out(g, p, half):
                dve.wait_ge(sh_y_mm, 2 * g + half + 1)
                dve.tensor_tensor(base[p][:, 2 * half:2 * half + 2, :],
                                  h_all[:, bass.ds(GROUP * g + 2 * half, 2), :],
                                  ps_y[half][0:TT, 0:2 * C].rearrange("p (j c) -> p j c", c=C),
                                  ALU.add).then_inc(sh_base, 1)

            def free_base(g, p):
                if g >= 2:
                    dve.wait_ge(base_stored[p], 16 * (g // 2))

            def shared_group(g, slot, out_first=0):
                n, p = FC_SH * g, g % 2
                b = n % 2
                if g >= 2:
                    dve.wait_ge(sh_y_mm, 2 * g - 2)
                slot(0)
                slot(1)
                shared_act(n, b, p, 0)
                slot(2)
                slot(3)
                if g > 0:
                    free_base(g - 1, 1 - p)
                    shared_out(g - 1, 1 - p, 0)
                    shared_out(g - 1, 1 - p, 1)
                slot(4)
                slot(5)
                shared_act(n + 1, 1 - b, p, 1)
                slot(6)
                slot(7)
                shared_act(n + 2, b, p, 2)

            for g in range(GROUPS // 2):
                def search(k):
                    try_bit(8 * g + k)
                    keep_bit(8 * g + k)
                shared_group(g, search)

            dve.wait_ge(const_pool, 7 + 3 * SPREAD)
            thr_f = thr[:].bitcast(F32)
            dve.tensor_scalar(above[:], score[:], thr_f, 0.0, ALU.is_gt, ALU.add,
                              accum_out=totals[:, 0:1]).then_inc(route_seq, 1)
            dve.tensor_scalar(equal[:], score[:], thr_f, 0.0, ALU.is_equal, ALU.add,
                              accum_out=totals[:, 1:2]).then_inc(totals_ready, 1)
            dve.wait_ge(totals_ready, 1)
            dve.tensor_tensor_scan(scan[:], equal[:], zeros[:], 0.0, ALU.add, ALU.add).then_inc(route_seq, 1)

            def route(k):
                if k == 1:
                    dve.wait_ge(eq_mm, 1)
                    dve.tensor_scalar(room[:, 0:1], ps_x[0][:, 1:2], -1.0, float(CAP), ALU.mult, ALU.add
                                      ).then_inc(route_seq, 1)
                    dve.wait_ge(route_seq, 3)
                    dve.tensor_tensor(room[:, 1:2], room[:, 0:1], ps_x[0][:, 3:4],
                                      ALU.subtract).then_inc(route_seq, 1)
                    dve.wait_ge(route_seq, 4)
                    dve.scalar_tensor_tensor(out=equal[:], in0=scan[:], scalar=room[:, 1:2], in1=equal[:],
                                             op0=ALU.is_le, op1=ALU.mult).then_inc(route_seq, 1)
                    dve.wait_ge(route_seq, 5)
                    dve.tensor_tensor(picked[:], above[:], equal[:], ALU.add).then_inc(route_seq, 1)
                    dve.wait_ge(route_seq, 6)
                    dve.tensor_tensor_scan(scan[:], picked[:], zeros[:], 0.0, ALU.add, ALU.add
                                           ).then_inc(route_seq, 1)
                    dve.wait_ge(route_seq, 7)
                    dve.tensor_copy(room[:, 2:3], scan[:, CAP - 1:CAP]).then_inc(sel_total, 1)
                if k == 4:
                    dve.wait_ge(sel_mm, 1)
                    dve.scalar_tensor_tensor(out=above[:], in0=scan[:], scalar=ps_x[0][:, 4:5], in1=picked[:],
                                             op0=ALU.add, op1=ALU.mult).then_inc(pos_ready, 1)
                if k == 6:
                    dve.wait_ge(posT_mm, 1)
                    dve.tensor_scalar(pos_i[:].rearrange("p (c j e) -> p j c e", j=GROUP, e=EXPERTS),
                                      ps_x[1][0:TT, :].rearrange("p (j c e) -> p j c e", j=GROUP, e=EXPERTS),
                                      -1.0, None, ALU.add).then_inc(route_seq, 1)
                    dve.wait_ge(route_seq, 8)
                    dve.tensor_scalar(pos_j[:], pos_i[:], 4, None, ALU.arith_shift_right).then_inc(route_seq, 1)
                    dve.tensor_scalar(pos_i[:], pos_i[:], LO - 1, None, ALU.bitwise_and).then_inc(route_seq, 1)
                if k == 7:
                    dve.wait_ge(route_seq, 10)
                    dve.tensor_copy(pos_hi[:], pos_j[:]).then_inc(route_seq, 1)
                    dve.tensor_copy(pos_lo[:], pos_i[:]).then_inc(route_seq, 1)

            shared_group(4, route)
            dve.wait_ge(route_seq, 12)

            def one_hot(k):
                for l in range(2 * k, 2 * k + 2):
                    dve.tensor_scalar(hot_id[:, 0, l, :], pos_lo[:], float(l), None,
                                      ALU.is_equal).then_inc(hot_lo_ready, 1)
                    dve.tensor_scalar(hot_id[:, 1, l, :], pos_lo[:], float(l), iota_p[:, 0:1],
                                      ALU.is_equal, ALU.mult)
                for h in range(4 * k, min(4 * k + 4, HI)):
                    ins = dve.tensor_scalar(hot_hi[:, h, :], pos_hi[:], float(h), None, ALU.is_equal)
                ins.then_inc(hot_ready, 1)

            shared_group(5, one_hot)
            dve.wait_ge(ids_mm, 1)
            ids_view = ps_x[0][0:HI, :].rearrange("p (e a l) -> p e a l", a=2, l=LO)
            dve.tensor_scalar(id_part[:], ids_view[:, :, 0, :], float(TT), None, ALU.mult).then_inc(route_seq, 1)
            dve.wait_ge(route_seq, 13)
            dve.tensor_tensor(ids[:], id_part[:], ids_view[:, :, 1, :], ALU.add).then_inc(ids_ready, 1)

            def split_low(e, p, piece):
                if piece < 4:
                    m, half = divmod(piece, 2)
                    dve.wait_ge(w_hi_ready, 2 * e + (m + 1))
                    count_ge(dve, u_mm, FC_EXP * (e - 1))
                    dve.tensor_tensor(w_lo[p][:, m, half, :], raw_in[:, m, half, :],
                                      w_hi[p][:, m, half, :].bitcast(F32), ALU.subtract).then_inc(w_lo_ready, 1)
                else:
                    rows = slice(3 * (piece - 4), 3 * (piece - 3))
                    dve.wait_ge(down_hi_ready, e + 1)
                    count_ge(dve, y_mm, GROUP * (e - 1))
                    dve.tensor_tensor(w_down[p][:, rows, 1, :], raw_down[:, rows, :],
                                      w_down[p][:, rows, 0, :].bitcast(F32), ALU.subtract
                                      ).then_inc(down_lo_ready, 1)

            def first_weights(k):
                if k % 2 == 1:
                    split_low(0, 0, k // 2)

            def nothing(k):
                pass

            shared_group(SPLIT_GROUP, first_weights)
            shared_group(7, nothing)
            free_base(7, 1)
            shared_out(7, 1, 0)
            shared_out(7, 1, 1)
            for piece in range(IN_PIECES, IN_PIECES + DOWN_PIECES):
                split_low(0, 0, piece)

            def x_low(e, p):
                dve.wait_ge(x_hi_ready, 2 * e + 2)
                count_ge(dve, u_mm, FC_EXP * (e - 1))
                dve.tensor_tensor(x_lo[p][:], ps_x[0][0:MAIN, 0:CAP], x_hi[p][:].bitcast(F32),
                                  ALU.subtract).then_inc(x_lo_ready, 1)
                dve.tensor_tensor(x_rem[p][REM:2 * REM], ps_x[1][0:REM, 0:CAP], x_rem[p][0:REM].bitcast(F32),
                                  ALU.subtract).then_inc(x_lo_ready, 1)

            def take_scores(e, p):
                dve.wait_ge(gathered[p], 32 * e - 32 * p + 64)
                count_ge(dve, yo_ready, GROUP * (e - 1))
                dve.tensor_copy(top[p][:], xg[p][:, :, bass.ds(e + C, 1)].rearrange("p j a -> p (j a)")
                                ).then_inc(top_ready, 1)

            def expert_out(e, p, j):
                if j == 0:
                    count_ge(dve, scattered, 64 * (e - 1))
                    dve.wait_ge(top_ready, e + 1)
                dve.wait_ge(y_mm, GROUP * e + (j + 1))
                count_ge(dve, yo_ready, GROUP * e + j)
                y = ps_y[j % 2][0:SLOTS]
                dve.tensor_scalar(scaled[:], y[:, 0:C], top[p][:, j:j + 1], None, ALU.mult).then_inc(scaled_ready, 1)
                dve.wait_ge(scaled_ready, GROUP * e + (j + 1))
                dve.scalar_tensor_tensor(out=yo[p][:, j, :], in0=y[:, C:2 * C], scalar=top[p][:, j:j + 1],
                                         in1=scaled[:], op0=ALU.mult, op1=ALU.add).then_inc(yo_ready, 1)

            def expert_act(e, f):
                dve.wait_ge(silu_ready, FC_EXP * e + (f + 1))
                dve.wait_ge(u_mm, FC_EXP * e + (f + 1))
                count_ge(dve, act_lo_ready, FC_EXP * e + (f - 1))
                dve.tensor_tensor(act_full[f % 2], silu[f % 2][:], ps_u[f % 2][:, 0:CAP],
                                  ALU.mult).then_inc(act_ready, 1)

            def act_low(e, p, f):
                dve.wait_ge(act_hi_ready, FC_EXP * e + (f + 1))
                if f == 0:
                    count_ge(dve, y_mm, GROUP * (e - 1))
                dve.tensor_tensor(act_lo[p][:, f, :], act_full[f % 2], act_hi[p][:, f, :].bitcast(F32),
                                  ALU.subtract).then_inc(act_lo_ready, 1)

            def expert(e, p, first=False, last=False):
                def weights(piece):
                    if not last:
                        split_low(e + 1, 1 - p, piece)

                def rows_out(j):
                    if not first:
                        expert_out(e - 1, 1 - p, j)
                take_scores(e, p)
                expert_act(e, 0)
                expert_act(e, 1)
                act_low(e, p, 0)
                act_low(e, p, 1)
                rows_out(0)
                weights(0)
                rows_out(1)
                weights(1)
                rows_out(2)
                weights(2)
                rows_out(3)
                weights(3)
                expert_act(e, 2)
                expert_act(e, 3)
                act_low(e, p, 2)
                weights(4)
                if not last:
                    x_low(e + 1, 1 - p)
                act_low(e, p, 3)
                expert_act(e, 4)
                weights(5)
                expert_act(e, 5)
                act_low(e, p, 4)
                act_low(e, p, 5)

            x_low(0, 0)
            expert(0, 0, first=True)
            expert(1, 1)
            with by_two(dve, 2, EXPERTS - 2) as e:
                expert(e, 0)
                expert(e + 1, 1)
            expert(EXPERTS - 2, 0)
            expert(EXPERTS - 1, 1, last=True)
            for j in range(GROUP):
                expert_out(EXPERTS - 1, 1, j)

        @block.tensor
        def _(pe):
            pe.wait_ge(const_pool, 4)
            pe.wait_ge(tok_loaded, 16)
            pe.wait_ge(const_dve, 8)

            def product(out, pairs, sync=None):
                for n, (lhsT, rhs) in enumerate(pairs):
                    ins = nc.tensor.matmul(out, lhsT, rhs, start=(n == 0), stop=(n == len(pairs) - 1))
                return ins

            def step(i, par):
                if live(i, 0):
                    t, p = i, par
                    pe.wait_ge(q_ready, upto(t, 0))
                    pe.wait_ge(ks0_ready, upto(t, 0))
                    pe.wait_ge(ks1_ready, upto(t, 0))
                    count_ge(pe, shifted, upto(t, -1))
                    count_ge(pe, gate_tanh, upto(t, -3))
                    for b in range(2):
                        g0 = HALF * b
                        for s in range(SEQS):
                            rows = slice(0, SECOND) if s == 0 else slice(WIN, TT)
                            keys = slice(s * WIN, (s + 1) * WIN)
                            at = slice(0, SECOND) if s == 0 else slice(SECOND, SP_)
                            ins = product(ps_s[b][at, 0:HALF * WIN].rearrange("p (g m) -> p g m", m=WIN), [
                                (qT[p][0:HC + 1, 0, rows], ks[p][0:HC + 1, 0, g0:g0 + HALF, keys]),
                                (qT[p][0:HC, 1, rows], ks[p][0:HC, 1, g0:g0 + HALF, keys])])
                    ins.then_inc(s_mm, 1)
                if live(i, -2):
                    t, p = i - 2, par
                    pe.wait_ge(hn2_ready, upto(t, 0))
                    count_ge(pe, hnT_ready, upto(t, 3))
                    count_ge(pe, hn2T_ready, upto(t, -1))
                    for k in range(KC):
                        ins = nc.tensor.transpose(ps_hT[:, k, :], row[p][:, k * HC:(k + 1) * HC], ident[0:TT, 0:TT])
                    ins.then_inc(hn2T_mm, 1)
                if live(i, 1):
                    t, p = i + 1, (par + 1) % 2
                    pe.wait_ge(hnT_ready, upto(t, 0))
                    if isinstance(t, int) and t == 0:
                        pe.wait_ge(qkv_loaded, 32)
                    count_ge(pe, q_ready, upto(t, -1))
                    count_ge(pe, k_ready, upto(t, -1))
                    for a in range(4):
                        cols = slice(a * HC, (a + 1) * HC)
                        ins = product(ps_qk[:, a, :], [
                            (w_qkv_sb[0:HC + 1, 0, cols], hnT[p][0:HC + 1, 0, :, 0, :]),
                            (w_qkv_sb[0:HC, 1, cols], hnT[p][0:HC, 1, :, 0, :])])
                    ins.then_inc(qk_mm, 1)
                if live(i, -3):
                    t, p = i - 3, (par + 1) % 2
                    pe.wait_ge(score_ready, upto(t, 0))
                    count_ge(pe, row_ready, upto(t, -1))
                    count_ge(pe, v_ready, upto(t, 3))
                    apart(pe)
                    nc.tensor.transpose(ps_sct, scoreT[p][:], ident[0:EXPERTS, 0:EXPERTS]).then_inc(sct_mm, 1)
                if live(i, 2):
                    t, p = i + 2, par
                    pe.wait_ge(dT_ready, upto(t, 0))
                    count_ge(pe, pool_tanh, upto(t, -1))
                    count_ge(pe, hnT_ready, upto(t, -1))
                    count_ge(pe, hn2T_ready, upto(t, -4))
                    product(ps_pool, [(dT[p][:, k, :], w_tok_sb[:, k, :]) for k in range(KC)]).then_inc(pool_mm, 1)
                if live(i, 1):
                    t, p = i + 1, (par + 1) % 2
                    count_ge(pe, v_ready, upto(t, -1))
                    count_ge(pe, row_ready, upto(t, -4))
                    for s in range(SEQS):
                        cols = slice(2 * C, 3 * C)
                        lhs = [hnT[p][0:n, k, s].rearrange("p a m -> p (a m)")
                               for k, n in ((0, HC + 1), (1, HC))]
                        ins = product(ps_v[:, s, :], [(lhs[0], w_qkv_sb[0:HC + 1, 0, cols]),
                                                      (lhs[1], w_qkv_sb[0:HC, 1, cols])])
                    ins.then_inc(v_mm, 1)
                if live(i, -1):
                    t, p = i - 1, (par + 1) % 2
                    pe.wait_ge(probT_ready, upto(t, 0))
                    pe.wait_ge(vs0_ready, upto(t, 0))
                    pe.wait_ge(vs1_ready, upto(t, 0))
                    count_ge(pe, oT_ready, upto(t, -1))
                    count_ge(pe, res_seq, 3 * upto(t, -1))
                    for k in range(KC):
                        c = slice(k * HC, (k + 1) * HC)
                        for s in range(SEQS):
                            at = s * SECOND
                            ins = product(ps_o[:, k, s * WIN:(s + 1) * WIN], [
                                (vs[p][:, s, j, c], probT[p][:, j, at:at + WIN]) for j in range(PAIRS)
                            ] + [(vs[p][0:WIN, s, PAIRS, c], ones_win[:])])
                    ins.then_inc(o_mm, 1)
                if live(i, -2):
                    t = i - 2
                    pe.wait_ge(hn2T_ready, upto(t, 0))
                    if isinstance(t, int) and t == 0:
                        pe.wait_ge(ffn_loaded, 64)
                    count_ge(pe, gate_tanh, upto(t, -1))
                    if live(i, 0):
                        pe.wait_ge(shifted, upto(i, 0))
                    product(ps_gate, [(w_gate_sb[:, k, :], hn2T[:, k, bass.ds(t * TT, TT)])
                                      for k in range(KC)]).then_inc(gate_mm, 1)
                if live(i, -1):
                    t, p = i - 1, (par + 1) % 2
                    pe.wait_ge(oT_ready, upto(t, 0))
                    if isinstance(t, int) and t == 0:
                        pe.wait_ge(proj_loaded, 32)
                    count_ge(pe, res_seq, 3 * upto(t, -1))
                    product(ps_r, [(oT[p][0:HC + 1, 0, :], w_proj_sb[0:HC + 1, 0, :]),
                                   (oT[p][0:HC, 1, :], w_proj_sb[0:HC, 1, :])]).then_inc(r_mm, 1)
                if live(i, 0):
                    t, p = i, par
                    pe.wait_ge(prob_ready, upto(t, 0))
                    count_ge(pe, probT_ready, upto(t, -1))
                    for j in range(PAIRS):
                        ins = nc.tensor.transpose(ps_pt[j // 3][0:2 * WIN, (j % 3) * SP_:(j % 3 + 1) * SP_],
                                                  prob[p][:, 2 * j:2 * j + 2, :].rearrange("p h m -> p (h m)"),
                                                  ident[0:SP_, 0:SP_])
                    ins.then_inc(pt_mm, 1)
                if live(i, 2):
                    t, p = i + 2, par
                    pe.wait_ge(hn_ready, upto(t, 0))
                    pe.wait_ge(pool_tanh, upto(t, 0))
                    for k in range(KC):
                        ins = nc.tensor.transpose(ps_hT[:, k, :], hn[p][:, k * HC:(k + 1) * HC], ident[0:TT, 0:TT])
                    ins.then_inc(hnT_mm, 1)

            pipeline(pe, step)
            attention_over(pe)
            pe.wait_ge(const_pool, 7 + 3 * SPREAD)

            def shared_in(g, n, b, f, w, banks, done):
                cols = slice(f * 128, (f + 1) * 128)
                count_ge(pe, sh_act, n - 1)
                product(banks[b][:, 0:GT], [(w[:, k, cols], hn2T[:, k, bass.ds(g * GT, GT)])
                                            for k in range(KC)]).then_inc(done, 1)

            def shared_down(g, p, half):
                pe.wait_ge(sh_act, FC_SH * g + FC_SH)
                count_ge(pe, sh_base, 2 * g + half - 1)
                for j in range(2 * half, 2 * half + 2):
                    ins = product(ps_y[half][0:TT, (j % 2) * C:(j % 2 + 1) * C],
                                  [(act_sh[p][:, f, j * TT:(j + 1) * TT], wsd_sb[:, f, :]) for f in range(FC_SH)])
                ins.then_inc(sh_y_mm, 1)

            def shared_group(g, slot):
                n, p = FC_SH * g, g % 2
                b = n % 2
                shared_in(g, n, b, 0, wsg_sb, ps_g, sh_g_mm)
                slot(0)
                shared_in(g, n, b, 0, wsu_sb, ps_u, sh_u_mm)
                slot(1)
                if g > 0:
                    shared_down(g - 1, 1 - p, 0)
                slot(2)
                if g > 0:
                    shared_down(g - 1, 1 - p, 1)
                slot(3)
                shared_in(g, n + 1, 1 - b, 1, wsg_sb, ps_g, sh_g_mm)
                slot(4)
                shared_in(g, n + 1, 1 - b, 1, wsu_sb, ps_u, sh_u_mm)
                slot(5)
                shared_in(g, n + 2, b, 2, wsg_sb, ps_g, sh_g_mm)
                slot(6)
                shared_in(g, n + 2, b, 2, wsu_sb, ps_u, sh_u_mm)
                slot(7)

            for g in range(GROUPS // 2):
                def search(k):
                    pe.wait_ge(counted, 8 * g + k + 1)
                    nc.tensor.matmul(ps_x[0][:, 0:1], onehot_sum[:], count[:], start=True,
                                     stop=True).then_inc(count_sum, 1)
                shared_group(g, search)

            def route(k):
                if k == 0:
                    pe.wait_ge(totals_ready, 1)
                    pe.wait_ge(route_seq, 1)
                    nc.tensor.matmul(ps_x[0][:, 1:3], onehot_sum[:], totals[:], start=True, stop=True)
                    nc.tensor.matmul(ps_x[0][:, 3:4], before[:], totals[:, 1:2], start=True,
                                     stop=True).then_inc(eq_mm, 1)
                if k == 2:
                    pe.wait_ge(sel_total, 1)
                    nc.tensor.matmul(ps_x[0][:, 4:5], before[:], room[:, 2:3], start=True,
                                     stop=True).then_inc(sel_mm, 1)
                if k == 4:
                    pe.wait_ge(pos_ready, 1)
                    for j in range(GROUP):
                        ins = nc.tensor.transpose(ps_x[1][0:TT, j * 128:(j + 1) * 128],
                                                  above[:, j * TT:(j + 1) * TT], ident[:])
                    ins.then_inc(posT_mm, 1)

            def nothing(k):
                pass

            shared_group(4, route)
            shared_group(5, nothing)
            pe.wait_ge(hot_ready, 8)
            pe.wait_ge(hot_tile_ready, LO)
            for e in range(EXPERTS):
                for t in range(TILES):
                    te = t * EXPERTS + e
                    ins = nc.tensor.matmul(ps_x[0][0:HI, e * 2 * LO:(e + 1) * 2 * LO], hot_hi[:, :, te],
                                           hot_id[:, :, :, te].rearrange("p a l -> p (a l)"),
                                           start=(t == 0), stop=(t == TILES - 1))
            ins.then_inc(ids_mm, 1)
            shared_group(6, nothing)
            shared_group(7, nothing)
            shared_down(7, 1, 0)
            shared_down(7, 1, 1)

            def turn_in(e, p):
                pe.wait_ge(gathered[p], 32 * e - 32 * p + 64)
                count_ge(pe, x_lo_ready, 2 * e)
                for k, cols in ((0, slice(0, MAIN)), (1, slice(MAIN, C))):
                    for j in range(GROUP):
                        ins = nc.tensor.transpose(ps_x[k][0:cols.stop - cols.start, j * SLOTS:(j + 1) * SLOTS],
                                                  xg[p][:, j, cols], ident[0:SLOTS, 0:SLOTS])
                ins.then_inc(xgT_mm, 1)

            def expert_in(e, p, f):
                cols = slice(f * 128, (f + 1) * 128)
                count_ge(pe, act_ready, FC_EXP * e + (f - 1))
                for m, (banks, done) in enumerate(((ps_g, g_mm), (ps_u, u_mm))):
                    if f == 0:
                        pe.wait_ge(w_lo_ready, IN_PIECES * e + 2 * (m + 1))
                    product(banks[f % 2][:, 0:CAP], [
                        (w_hi[p][:, m, 0, cols], x_hi[p][:]), (w_hi[p][:, m, 0, cols], x_lo[p][:]),
                        (w_lo[p][:, m, 0, cols], x_hi[p][:]), (w_hi[p][:, m, 1, cols], x_rem[p][:]),
                        (w_lo[p][:, m, 1, cols], x_rem[p][:])]).then_inc(done, 1)

            def expert_down(e, p):
                pe.wait_ge(act_lo_ready, FC_EXP * e + FC_EXP)
                pe.wait_ge(down_lo_ready, DOWN_PIECES * (e + 1))
                for j in range(GROUP):
                    count_ge(pe, yo_ready, GROUP * e + (j - 1))
                    slots = slice(j * SLOTS, (j + 1) * SLOTS)
                    for f in range(FC_EXP):
                        nc.tensor.matmul(ps_y[j % 2][0:SLOTS, 0:2 * C], act_hi[p][:, f, slots],
                                         w_down[p][:, f].rearrange("p a c -> p (a c)"), start=(f == 0), stop=False)
                        ins = nc.tensor.matmul(ps_y[j % 2][0:SLOTS, C:2 * C], act_lo[p][:, f, slots],
                                               w_down[p][:, f, 0, :], start=False, stop=(f == FC_EXP - 1))
                    ins.then_inc(y_mm, 1)

            def expert(e, p, first=False, last=False):
                pe.wait_ge(x_lo_ready, 2 * e + 2)
                expert_in(e, p, 0)
                expert_in(e, p, 1)
                if not first:
                    expert_down(e - 1, 1 - p)
                expert_in(e, p, 2)
                expert_in(e, p, 3)
                if not last:
                    turn_in(e + 1, 1 - p)
                expert_in(e, p, 4)
                expert_in(e, p, 5)

            pe.wait_ge(ids_ready, 1)
            turn_in(0, 0)
            pe.wait_ge(sh_base, 2 * GROUPS)
            pe.wait_ge(sh_act, FC_SH * GROUPS)
            expert(0, 0, first=True)
            expert(1, 1)
            with by_two(pe, 2, EXPERTS - 2) as e:
                expert(e, 0)
                expert(e + 1, 1)
            expert(EXPERTS - 2, 0)
            expert(EXPERTS - 1, 1, last=True)
            expert_down(EXPERTS - 1, 1)


def kernel(x, L0_tok_w, L0_attn_w_qkv, L0_attn_b_qkv, L0_attn_w_l, L0_attn_b_l, L0_attn_w_w, L0_attn_b_w,
           L0_attn_w_proj, L0_attn_b_proj, L0_ffn_gate_weight, L0_ffn_Wg, L0_ffn_Wu, L0_ffn_Wd,
           L0_ffn_Ws_g, L0_ffn_Ws_u, L0_ffn_Ws_d):
    import numpy as np
    import concourse.bacc as bacc
    from concourse.bass_utils import run_bass_kernel_spmd

    frames = np.asarray(x)[:, :POOL * WIN]
    halves = frames.reshape(TILES, SEQS, WIN, POOL, KC, HC)
    gate_up = np.stack([np.asarray(L0_ffn_Wg), np.asarray(L0_ffn_Wu)]).transpose(1, 3, 0, 2)
    arrays = {
        "xT": halves.transpose(0, 5, 4, 3, 1, 2).reshape(TILES, HC, KC, POOL, TT),
        "xp": frames.reshape(TILES, TT, POOL, C),
        "w_tok": np.asarray(L0_tok_w),
        "w_qkv": np.asarray(L0_attn_w_qkv),
        "b_qkv": np.asarray(L0_attn_b_qkv).reshape(1, -1),
        "w_l": np.asarray(L0_attn_w_l),
        "b_l": np.asarray(L0_attn_b_l).reshape(1, -1),
        "w_w": np.asarray(L0_attn_w_w),
        "b_w": np.asarray(L0_attn_b_w).reshape(1, -1),
        "w_proj": np.asarray(L0_attn_w_proj),
        "b_proj": np.asarray(L0_attn_b_proj).reshape(1, -1),
        "w_gate": np.asarray(L0_ffn_gate_weight).T,
        "w_main": gate_up[:, :MAIN],
        "w_rem": gate_up[:, MAIN:],
        "wd": np.asarray(L0_ffn_Wd).transpose(0, 2, 1).reshape(EXPERTS, FC_EXP, 128, C).transpose(0, 2, 1, 3),
        "wsg": np.asarray(L0_ffn_Ws_g).T,
        "wsu": np.asarray(L0_ffn_Ws_u).T,
        "wsd": np.asarray(L0_ffn_Ws_d).T,
    }
    nc = bacc.Bacc("TRN2", target_bir_lowering=False, num_devices=1)
    feeds, args = {}, []
    for name, a in arrays.items():
        feeds[f"in_{name}"] = np.ascontiguousarray(a)
        args.append(nc.dram_tensor(f"in_{name}", feeds[f"in_{name}"].shape, F32, kind="ExternalInput").ap())
    args.append(nc.dram_tensor("out_h", (BATCH, WIN, C), F32, kind="ExternalOutput").ap())
    audio_tower(nc, *args)
    r = run_bass_kernel_spmd(nc, [feeds], core_ids=[0])
    return r.results[0]["out_h"]
```

```python
from contextlib import ExitStack, contextmanager

import concourse.bass as bass
from concourse import mybir

ALU = mybir.AluOpType
ACT = mybir.ActivationFunctionType
AX = mybir.AxisListType
F32 = mybir.dt.float32
F32R = mybir.dt.float32r
BF16 = mybir.dt.bfloat16
I32 = mybir.dt.int32
U32 = mybir.dt.uint32

BATCH, FRAMES, C = 64, 125, 192
POOL = 2
WIN = (FRAMES - POOL) // POOL + 1
HEADS = 12
HD = C // HEADS
EXPERTS = 16
F_EXP = 4 * C
F_SH = F_EXP // 2
TOKENS = BATCH * WIN
TOP_K = 2
CAP = -(-TOKENS * TOP_K // EXPERTS)
LN_EPS = 1e-5

KC = 2
HC = C // KC
SEQS = 2
TT = SEQS * WIN
TILES = TOKENS // TT
HALF = HEADS // 2
PAIRS = HEADS // 2
SECOND = 64
SP_ = SECOND + WIN
ROW = C + EXPERTS
GROUP = 4
GT = GROUP * TT
GROUPS = TILES // GROUP
FC_SH = F_SH // 128
FC_EXP = F_EXP // 128
MAIN = 128
REM = C - MAIN
VR = 2 * WIN + 1
CONSTS = 4
IDS_GROUP = 6
LO_DVE = 4
SPLIT_GROUP = 7
IN_PIECES, DOWN_PIECES = 4, 2
SLOTS = CAP // GROUP
HI = CAP // 16
LO = 16
SEARCH = 15
PER_GROUP = 3
SEARCH_GROUPS = SEARCH // PER_GROUP
ROUTE_GROUP, HOT_GROUP = SEARCH_GROUPS, SEARCH_GROUPS + 1
SPREAD = GROUPS
TABLE_STEPS = 3 * SPREAD + 3

LEAD, LOOP_FROM, LOOP_TO, LAST = -3, 4, 28, TILES + 3


def count_ge(eng, sem, value):
    if isinstance(value, int) and value <= 0:
        return
    eng.wait_ge(sem, value)


def live(i, off):
    return not isinstance(i, int) or 0 <= i + off < TILES


def upto(t, off):
    if isinstance(t, int):
        return min(t + off + 1, TILES)
    return t + (off + 1)


@contextmanager
def by_two(eng, start, end):
    with eng.Fori(0, (end - start) // 2) as half:
        yield half * 2 + start


def pipeline(eng, body):
    for i in range(LEAD, LOOP_FROM):
        body(i, i % 2)
    with by_two(eng, LOOP_FROM, LOOP_TO) as r:
        body(r, 0)
        body(r + 1, 1)
    for i in range(LOOP_TO, LAST):
        body(i, i % 2)


def audio_tower(nc, xT, xp, w_tok, w_qkv, b_qkv, w_l, b_l, w_w, b_w, w_proj, b_proj,
                w_gate, w_main, w_rem, wd, wsg, wsu, wsd, out):
    out_rows = out.rearrange("b n c -> (b n) c")
    rows_dram = nc.dram_tensor("rows_scratch", (TOKENS, ROW), F32, kind="Internal").ap()
    score_dram = nc.dram_tensor("score_scratch", (EXPERTS, TOKENS), F32, kind="Internal").ap()
    ids_dram = nc.dram_tensor("ids_scratch", (EXPERTS, CAP), I32, kind="Internal").ap()

    with ExitStack() as ctx:
        ctx.enter_context(nc.allow_non_contiguous_dma(reason="layout of small tables"))

        def sb(name, shape, dt=F32, scope=ctx):
            return scope.enter_context(nc.sbuf_tensor(name, shape, dt))

        def sem(name):
            return ctx.enter_context(nc.semaphore(name))

        def sems(name, n=2):
            return [sem(f"{name}{i}") for i in range(n)]

        bank = [ctx.enter_context(nc.psum_tensor(f"bank{i}", [128, 512], F32)) for i in range(8)]

        ident = sb("ident", [128, 128])
        ffn_in = ExitStack()
        h_all = sb("h_all", [TT, TILES, C], F32, ffn_in)
        hn2T = sb("hn2T", [HC, KC, TOKENS], F32, ffn_in)
        ffn_in.close()
        x_hi = [sb(f"x_hi{p}", [MAIN, CAP], F32R) for p in range(2)]
        x_lo = [sb(f"x_lo{p}", [MAIN, CAP], F32R) for p in range(2)]
        x_rem = [sb(f"x_rem{p}", [2 * REM, CAP], F32R) for p in range(2)]
        act_hi = [sb(f"act_hi{p}", [128, FC_EXP, CAP], F32R) for p in range(2)]
        act_lo = [sb(f"act_lo{p}", [128, FC_EXP, CAP], F32R) for p in range(2)]
        w_gate_sb = sb("w_gate_sb", [HC, KC, EXPERTS])
        wsg_sb = sb("wsg_sb", [HC, KC, F_SH])
        wsu_sb = sb("wsu_sb", [HC, KC, F_SH])
        wsd_sb = sb("wsd_sb", [128, FC_SH, C])
        raw_in = sb("raw_in", [128, 2, 2, F_EXP])
        raw_down = sb("raw_down", [128, FC_EXP, C])
        onehot_sum = sb("onehot_sum", [128, 128])
        before = sb("before", [128, 128])
        zeros = sb("zeros", [128, CAP])
        iota_p = sb("iota_p", [TT, 1])
        iota_t = sb("iota_t", [TT, TILES, EXPERTS], BF16)
        score = sb("score", [128, CAP])
        idx_all = sb("idx_all", [SLOTS, EXPERTS, GROUP], I32)

        att = ExitStack()
        w_tok_sb = sb("w_tok_sb", [HC, KC, C], scope=att)
        w_qkv_sb = sb("w_qkv_sb", [HC + 1, KC, 3 * C], scope=att)
        w_proj_sb = sb("w_proj_sb", [HC + 1, KC, C], scope=att)
        mix_in = sb("mix_in", [HC, KC, HEADS], scope=att)
        mix_out = sb("mix_out", [VR, PAIRS, HEADS], scope=att)
        bl_row = sb("bl_row", [HC + 1, HEADS], scope=att)
        minus_half = sb("minus_half", [TT, 1], scope=att)
        xT_in = [sb(f"xT_in{p}", [HC, KC, POOL, TT], scope=att) for p in range(2)]
        xp_in = [sb(f"xp_in{p}", [TT, POOL, C], scope=att) for p in range(2)]
        dT = [sb(f"dT{p}", [HC, KC, TT], scope=att) for p in range(2)]
        tanh_d = [sb(f"tanh_d{p}", [TT, C], scope=att) for p in range(2)]
        diff = sb("diff", [TT, C], scope=att)
        stats1 = sb("stats1", [TT, 12], scope=att)
        stats2 = sb("stats2", [TT, 12], scope=att)
        rstd1 = [sb(f"rstd1_{p}", [TT, 1], scope=att) for p in range(2)]
        rstd2 = [sb(f"rstd2_{p}", [TT, 1], scope=att) for p in range(2)]
        hn = [sb(f"hn{p}", [TT, C], scope=att) for p in range(2)]
        hnT = [sb(f"hnT{p}", [HC + 1, KC, SEQS, VR], scope=att) for p in range(2)]
        qT = [sb(f"qT{p}", [HC + 1, KC, TT], scope=att) for p in range(2)]
        kT = [sb(f"kT{p}", [HC, KC, TT], scope=att) for p in range(2)]
        ks = [sb(f"ks{p}", [HC + 1, KC, HEADS, TT], scope=att) for p in range(2)]
        v_sb = [sb(f"v_sb{p}", [VR, SEQS, C], scope=att) for p in range(2)]
        vs = [sb(f"vs{p}", [VR, SEQS, PAIRS, C], scope=att) for p in range(2)]
        minus_max = [sb(f"minus_max{p}", [SP_, HEADS], scope=att) for p in range(2)]
        ssum = [sb(f"ssum{p}", [SP_, HEADS], scope=att) for p in range(2)]
        prob = [sb(f"prob{p}", [SP_, HEADS, WIN], scope=att) for p in range(2)]
        probT_both = sb("probT", [VR, 2, PAIRS, SP_], scope=att)
        probT = [probT_both[:, p] for p in range(2)]
        o_sb = [sb(f"o_sb{p}", [SP_, C], scope=att) for p in range(2)]
        oT = [sb(f"oT{p}", [HC + 1, KC, TT], scope=att) for p in range(2)]
        row = [sb(f"row{p}", [TT, ROW], scope=att) for p in range(2)]
        scoreT = [sb(f"scoreT{p}", [EXPERTS, TT], scope=att) for p in range(2)]
        att.close()

        cand = sb("cand", [128, 3], U32)
        thr = sb("thr", [128, 1], U32)
        bits = sb("bits", [128, 3], U32)
        enough = sb("enough", [128, 3], U32)
        count = sb("count", [128, 3])
        above = sb("above", [128, CAP])
        equal = sb("equal", [128, CAP])
        scan = sb("scan", [128, CAP])
        picked = sb("picked", [128, CAP])
        totals = sb("totals", [128, 2])
        room = sb("room", [128, 3])
        act_sh = [sb(f"act_sh{p}", [128, FC_SH, GT]) for p in range(2)]
        silu = [sb(f"silu{p}", [128, GT]) for p in range(2)]
        base = [sb(f"base{p}", [TT, GROUP, C]) for p in range(2)]
        ids = sb("ids", [HI, EXPERTS, LO], I32)
        id_part = sb("id_part", [HI, EXPERTS, LO])
        idx_g = [sb(f"idx_g{p}", [SLOTS, GROUP], I32) for p in range(2)]
        idx_s = [sb(f"idx_s{p}", [SLOTS, GROUP], I32) for p in range(2)]
        xg = [sb(f"xg{p}", [SLOTS, GROUP, ROW]) for p in range(2)]
        top = [sb(f"top{p}", [SLOTS, GROUP]) for p in range(2)]
        scaled = sb("scaled", [SLOTS, C])
        yo = base
        act_full = [act_sh[p][:, 0, :] for p in range(2)]
        TE = TILES * EXPERTS
        hot = ExitStack()
        pos_i = sb("pos_i", [TT, TE], I32, hot)
        pos_j = sb("pos_j", [TT, TE], I32, hot)
        pos_hi = sb("pos_hi", [TT, TE], BF16, hot)
        pos_lo = sb("pos_lo", [TT, TE], BF16, hot)
        hot_hi = sb("hot_hi", [TT, HI, TE], BF16, hot)
        hot_id = sb("hot_id", [TT, 2, LO, TE], BF16, hot)
        hot.close()
        w_hi = [sb(f"w_hi{p}", [128, 2, 2, F_EXP], F32R) for p in range(2)]
        w_lo = [sb(f"w_lo{p}", [128, 2, 2, F_EXP], F32R) for p in range(2)]
        w_down = [sb(f"w_down{p}", [128, FC_EXP, 2, C], F32R) for p in range(2)]
        ps_s = [bank[0], bank[1]]
        ps_gate = bank[0][0:EXPERTS, 372:372 + TT]
        ps_pt = [bank[2], bank[3]]
        ps_qk = bank[4][0:HC, 0:4 * TT].rearrange("p (a n) -> p a n", a=4)
        ps_v = bank[5][0:VR, 0:SEQS * C].rearrange("p (s c) -> p s c", s=SEQS)
        ps_sct = bank[7][0:TT, 448:448 + EXPERTS]
        ps_hT = bank[6][0:HC, 0:KC * TT].rearrange("p (k n) -> p k n", k=KC)
        ps_pool = bank[6][0:TT, 256:256 + C]
        ps_o = bank[7][0:SP_, 0:C]
        ps_oT = bank[7][0:HC, 0:KC * SP_].rearrange("p (k n) -> p k n", k=KC)
        ps_r = bank[7][0:TT, 256:256 + C]
        ps_g, ps_u, ps_y, ps_x = bank[0:2], bank[2:4], bank[4:6], bank[6:8]

        tok_loaded = sem("tok_loaded")
        qkv_loaded = sem("qkv_loaded")
        mix_in_loaded = sem("mix_in_loaded")
        mix_out_loaded = sem("mix_out_loaded")
        proj_loaded = sem("proj_loaded")
        ffn_loaded = sem("ffn_loaded")
        const_pool = sem("const_pool")
        const_dve = sem("const_dve")
        x_loaded = sems("x_loaded")
        dT_ready = sem("dT_ready")
        pool_mm = sem("pool_mm")
        pool_tanh = sem("pool_tanh")
        pool_seq = sem("pool_seq")
        var1_ready = sem("var1_ready")
        rstd1_ready = sem("rstd1_ready")
        hn_ready = sem("hn_ready")
        hnT_mm = sem("hnT_mm")
        hnT_ready = sem("hnT_ready")
        qk_mm = sem("qk_mm")
        v_mm = sem("v_mm")
        q_ready = sem("q_ready")
        k_ready = sem("k_ready")
        v_ready = sem("v_ready")
        ks0_ready = sem("ks0_ready")
        ks1_ready = sem("ks1_ready")
        vs0_ready = sem("vs0_ready")
        vs1_ready = sem("vs1_ready")
        s_mm = sem("s_mm")
        max_ready = sem("max_ready")
        recip_ready = sem("recip_ready")
        o_ready = sem("o_ready")
        oT_mm = sem("oT_mm")
        hsum_ready = sem("hsum_ready")
        exp_done = sem("exp_done")
        prob_ready = sem("prob_ready")
        pt_mm = sem("pt_mm")
        probT_ready = sem("probT_ready")
        o_mm = sem("o_mm")
        oT_ready = sem("oT_ready")
        r_mm = sem("r_mm")
        res_seq = sem("res_seq")
        var2_ready = sem("var2_ready")
        rstd2_ready = sem("rstd2_ready")
        hn2_ready = sem("hn2_ready")
        hn2T_mm = sem("hn2T_mm")
        hn2T_ready = sem("hn2T_ready")
        gate_mm = sem("gate_mm")
        gate_tanh = sem("gate_tanh")
        score_ready = sem("score_ready")
        sct_mm = sem("sct_mm")
        row_ready = sem("row_ready")
        row_stored = sems("row_stored")
        in_loaded = sem("in_loaded")
        down_loaded = sem("down_loaded")
        score_loaded = sem("score_loaded")
        counted = sem("counted")
        count_sum = sem("count_sum")
        find_seq = sem("find_seq")
        sh_g_mm = sem("sh_g_mm")
        sh_u_mm = sem("sh_u_mm")
        sh_silu = sem("sh_silu")
        sh_act = sem("sh_act")
        sh_y_mm = sem("sh_y_mm")
        sh_base = sem("sh_base")
        base_stored = sems("base_stored")
        route_seq = sem("route_seq")
        totals_ready = sem("totals_ready")
        eq_mm = sem("eq_mm")
        sel_total = sem("sel_total")
        sel_mm = sem("sel_mm")
        pos_ready = sem("pos_ready")
        posT_mm = sem("posT_mm")
        hot_lo_ready = sem("hot_lo_ready")
        hot_tile_ready = sem("hot_tile_ready")
        hot_ready = sem("hot_ready")
        ids_mm = sem("ids_mm")
        ids_ready = sem("ids_ready")
        ids_stored = sem("ids_stored")
        idx_loaded = sem("idx_loaded")
        idx_g_ready = sem("idx_g_ready")
        idx_s_ready = sem("idx_s_ready")
        gathered = sems("gathered")
        scattered = sem("scattered")
        top_ready = sem("top_ready")
        xgT_mm = sem("xgT_mm")
        x_hi_ready = sem("x_hi_ready")
        x_lo_ready = sem("x_lo_ready")
        w_hi_ready = sem("w_hi_ready")
        down_hi_ready = sem("down_hi_ready")
        w_lo_ready = sem("w_lo_ready")
        down_lo_ready = sem("down_lo_ready")
        g_mm = sem("g_mm")
        u_mm = sem("u_mm")
        silu_ready = sem("silu_ready")
        act_ready = sem("act_ready")
        act_hi_ready = sem("act_hi_ready")
        act_lo_ready = sem("act_lo_ready")
        y_mm = sem("y_mm")
        scaled_ready = sem("scaled_ready")
        yo_ready = sem("yo_ready")
        own_waits = {e.engine: sem(f"own_waits_{n}") for n, e in
                     (("sp", nc.sync), ("pool", nc.gpsimd), ("pe", nc.tensor), ("dve", nc.vector))}

        def attention_over(eng):
            for s in (hn2T_ready, row_ready, gate_tanh, score_ready, prob_ready, hn2_ready, oT_ready,
                      o_ready, oT_mm, o_mm, r_mm, sct_mm, gate_mm, pt_mm, v_mm, vs0_ready, vs1_ready, ks0_ready,
                      ks1_ready, probT_ready, rstd2_ready, exp_done, hn2T_mm):
                eng.wait_ge(s, TILES)
            for s in row_stored:
                eng.wait_ge(s, 32 * (TILES // 2))

        def scale_values(eng, p, s):
            shape = [VR, PAIRS, HEADS, HD]
            return eng.tensor_tensor(
                vs[p][:, s, 0:PAIRS, :].rearrange("p j (g d) -> p j g d", d=HD),
                v_sb[p][:, s, :].rearrange("p (g d) -> p g d", d=HD).unsqueeze(1).to_broadcast(shape),
                mix_out[:].unsqueeze(3).to_broadcast(shape), ALU.mult)

        def stored_of(t, p, off):
            if isinstance(t, int):
                return 32 * ((t + off - p) // 2 + 1)
            return 16 * t + 16 * (off - p + 2)

        def apart(eng):
            eng.sem_inc(own_waits[eng.engine], 1)

        block = ctx.enter_context(nc.Block())

        @block.sync
        def _(sp):
            def load_x(t, p):
                count_ge(sp, dT_ready, upto(t, -2))
                apart(sp)
                count_ge(sp, pool_seq, 5 * upto(t, -2))
                apart(sp)
                sp.dma_start(xT_in[p][:], xT[t]).then_inc(x_loaded[p], 16)
                sp.dma_start(xp_in[p][:], xp[t]).then_inc(x_loaded[p], 16)

            halves = "(k p) n -> p k n"
            load_x(0, 0)
            sp.dma_start(w_tok_sb[:], w_tok.rearrange(halves, k=KC)).then_inc(tok_loaded, 16)
            load_x(1, 1)
            sp.dma_start(w_qkv_sb[0:HC], w_qkv.rearrange(halves, k=KC)).then_inc(qkv_loaded, 16)
            sp.dma_start(w_qkv_sb[HC:HC + 1, 0, :], b_qkv).then_inc(qkv_loaded, 16)
            for half in range(2):
                sp.dma_start(mix_out[half * WIN:(half + 1) * WIN],
                             w_w.rearrange("(j a) g -> a j g", a=2)[half:half + 1].to_broadcast([WIN, PAIRS, HEADS])
                             ).then_inc(mix_out_loaded, 16)
            sp.dma_start(mix_out[VR - 1:VR], b_w.unsqueeze(1).to_broadcast([1, PAIRS, HEADS])
                         ).then_inc(mix_out_loaded, 16)
            sp.dma_start(w_proj_sb[0:HC], w_proj.rearrange(halves, k=KC)).then_inc(proj_loaded, 16)
            sp.dma_start(w_proj_sb[HC:HC + 1, 0, :], b_proj).then_inc(proj_loaded, 16)

            def load_ffn():
                sp.dma_start(w_gate_sb[:], w_gate.rearrange(halves, k=KC)).then_inc(ffn_loaded, 16)
                sp.dma_start(wsg_sb[:], wsg.rearrange(halves, k=KC)).then_inc(ffn_loaded, 16)
                sp.dma_start(wsu_sb[:], wsu.rearrange(halves, k=KC)).then_inc(ffn_loaded, 16)
                sp.dma_start(wsd_sb[:], wsd.rearrange("(f p) n -> p f n", p=128)).then_inc(ffn_loaded, 16)

            def load_in(e):
                sp.dma_start(raw_in[:, :, 0, :], w_main[e]).then_inc(in_loaded, 16)
                sp.dma_start(raw_in[0:REM, :, 1, :], w_rem[e]).then_inc(in_loaded, 16)
                sp.dma_start(raw_in[REM:2 * REM, :, 1, :], w_rem[e]).then_inc(in_loaded, 16)

            def load_down(e):
                sp.dma_start(raw_down[:], wd[e]).then_inc(down_loaded, 16)


            def load_scores(c):
                for p in range(2):
                    sp.wait_ge(row_stored[p], 32 * (GROUP * (c + 1) // 2))
                sp.dma_start(score[c * EXPERTS:(c + 1) * EXPERTS, :],
                             score_dram[:, c * CAP:(c + 1) * CAP]).then_inc(score_loaded, 16)

            def step(i, par):
                if live(i, -3):
                    t, p = i - 3, (par + 1) % 2
                    sp.wait_ge(row_ready, upto(t, 0))
                    apart(sp)
                    sp.dma_start(rows_dram[bass.ds(t * TT, TT), :], row[p][:]).then_inc(row_stored[p], 16)
                    sp.dma_start(score_dram[:, bass.ds(t * TT, TT)], scoreT[p][:]).then_inc(row_stored[p], 16)
                if live(i, 4) and not (isinstance(i, int) and i + 4 < 2):
                    load_x(i + 4, par)
                if isinstance(i, int) and i >= TILES:
                    for c in range(*((0, 3), (3, 6), (6, SPREAD - 1))[i - TILES]):
                        load_scores(c)
                if isinstance(i, int) and i == -1:
                    load_ffn()
                if isinstance(i, int) and i == 0:
                    load_in(0)
                    load_down(0)

            pipeline(sp, step)

            load_scores(SPREAD - 1)
            attention_over(sp)

            def store_base(g, p):
                sp.wait_ge(sh_base, 2 * g + 2)
                apart(sp)
                sp.dma_start(out_rows[bass.ds(g * GT, GT), :].rearrange("(j p) c -> p j c", p=TT),
                             base[p][:]).then_inc(base_stored[p], 16)

            with by_two(sp, 0, IDS_GROUP) as g:
                store_base(g, 0)
                store_base(g + 1, 1)
            sp.wait_ge(ids_ready, 1)
            sp.dma_start(ids_dram.rearrange("e (h l) -> h e l", l=LO), ids[:]).then_inc(ids_stored, 16)
            sp.wait_ge(ids_stored, 16)
            sp.dma_start(idx_all[:], ids_dram.rearrange("e (p j) -> p e j", j=GROUP)).then_inc(idx_loaded, 16)
            for g in range(IDS_GROUP, GROUPS):
                store_base(g, g % 2)

            def next_expert(e):
                sp.wait_ge(w_lo_ready, IN_PIECES * e)
                apart(sp)
                load_in(e)
                sp.wait_ge(down_lo_ready, DOWN_PIECES * e)
                apart(sp)
                load_down(e)

            with sp.Fori(1, EXPERTS) as e:
                next_expert(e)
            for s in base_stored:
                sp.wait_ge(s, 16 * (GROUPS // 2))
            sp.wait_ge(scattered, 64 * EXPERTS)

        @block.gpsimd
        def _(pool):
            def routing_tables(n):
                pool.wait_ge(const_pool, CONSTS + n)
                if n < 2:
                    pool.memset((onehot_sum, before)[n][:], 0.0).then_inc(const_pool, 1)
                elif n < 1 + 2 * SPREAD:
                    pool.affine_select(out=onehot_sum[:], in_=onehot_sum[:], compare_op=ALU.not_equal, fill=1.0,
                                       base=(n - 1 - SPREAD) * EXPERTS, pattern=[[-1, 128]],
                                       channel_multiplier=1).then_inc(const_pool, 1)
                elif n < 3 * SPREAD:
                    pool.affine_select(out=before[:], in_=before[:], compare_op=ALU.not_equal, fill=1.0,
                                       base=(n - 2 * SPREAD) * EXPERTS, pattern=[[-1, 128]],
                                       channel_multiplier=1).then_inc(const_pool, 1)
                elif n == 3 * SPREAD:
                    pool.memset(zeros[:], 0.0).then_inc(const_pool, 1)
                elif n == 3 * SPREAD + 1:
                    pool.iota(iota_p[:], [[0, 1]], base=0, channel_multiplier=1,
                              allow_small_or_imprecise_dtypes=True).then_inc(const_pool, 1)
                else:
                    pool.iota(iota_t[:], [[1, TILES], [0, EXPERTS]], base=0, channel_multiplier=0,
                              allow_small_or_imprecise_dtypes=True).then_inc(const_pool, 1)

            pool.memset(ident[:], 0.0).then_inc(const_pool, 1)
            pool.memset(minus_half[:], -0.5).then_inc(const_pool, 1)
            pool.memset(probT_both[:], 1.0).then_inc(const_pool, 1)
            pool.wait_ge(const_pool, 3)
            pool.affine_select(out=ident[:], in_=ident[:], compare_op=ALU.not_equal, fill=1.0,
                               base=0, pattern=[[-1, 128]], channel_multiplier=1).then_inc(const_pool, 1)

            def step(i, par):
                if live(i, -2):
                    t, p = i - 2, par
                    pool.wait_ge(var2_ready, upto(t, 0))
                    count_ge(pool, hn2_ready, upto(t, -2))
                    pool.tensor_tensor(rstd2[p][:], stats2[:, 8:9], minus_half[:], ALU.pow).then_inc(rstd2_ready, 1)
                if live(i, 0):
                    t, p = i, par
                    if isinstance(t, int) and t == 0:
                        pool.wait_ge(mix_out_loaded, 48)
                    pool.wait_ge(v_ready, upto(t, 0))
                    count_ge(pool, o_mm, upto(t, -2))
                    scale_values(pool, p, 0).then_inc(vs0_ready, 1)
                if live(i, 1):
                    t, p = i + 1, (par + 1) % 2
                    if isinstance(t, int) and t == 0:
                        pool.wait_ge(mix_in_loaded, 16 * (KC + 1))
                    pool.wait_ge(k_ready, upto(t, 0))
                    count_ge(pool, s_mm, 2 * upto(t, -2))
                    pool.tensor_tensor(ks[p][0:HC, 1], kT[p][:, 1, :].unsqueeze(1).to_broadcast([HC, HEADS, TT]),
                                       mix_in[:, 1, :].unsqueeze(2).to_broadcast([HC, HEADS, TT]),
                                       ALU.mult).then_inc(ks1_ready, 1)
                if live(i, 2):
                    t, p = i + 2, par
                    pool.wait_ge(var1_ready, upto(t, 0))
                    count_ge(pool, hn_ready, upto(t, -2))
                    pool.tensor_tensor(rstd1[p][:], stats1[:, 8:9], minus_half[:], ALU.pow).then_inc(rstd1_ready, 1)
                if isinstance(i, int) and i >= LOOP_TO:
                    each = -(-TABLE_STEPS // (TILES - LOOP_TO))
                    for n in range(each * (i - LOOP_TO), min(each * (i - LOOP_TO + 1), TABLE_STEPS)):
                        routing_tables(n)

            pipeline(pool, step)

            attention_over(pool)
            pool.wait_ge(const_pool, CONSTS + TABLE_STEPS)
            for l in range(LO - LO_DVE):
                pool.wait_ge(hot_lo_ready, l + 1)
                pool.tensor_tensor(hot_id[:, 0, l, :], hot_id[:, 0, l, :], iota_t[:].rearrange("p t e -> p (t e)"),
                                   ALU.mult).then_inc(hot_tile_ready, 1)

            def gather(e, p):
                count_ge(pool, gathered[p], 32 * e - 32 * p)
                apart(pool)
                pool.tensor_copy(idx_g[p][:], idx_all[:, bass.ds(e, 1), :].rearrange("p a j -> p (a j)")
                                 ).then_inc(idx_g_ready, 1)
                count_ge(pool, xgT_mm, e - 1)
                count_ge(pool, top_ready, e - 1)
                pool.wait_ge(idx_g_ready, e + 1)
                apart(pool)
                for j in range(GROUP):
                    pool.indirect_dma_start(out=xg[p][:, j, :], out_offset=None, in_=rows_dram,
                                            in_offset=bass.IndirectOffsetOnAxis(
                                                ap=idx_g[p][:, j:j + 1].bitcast(U32), axis=0)
                                            ).then_inc(gathered[p], 16)

            def scatter(e, p):
                count_ge(pool, scattered, 64 * e)
                apart(pool)
                pool.tensor_copy(idx_s[p][:], idx_all[:, bass.ds(e, 1), :].rearrange("p a j -> p (a j)")
                                 ).then_inc(idx_s_ready, 1)
                pool.wait_ge(yo_ready, GROUP * e + GROUP)
                pool.wait_ge(idx_s_ready, e + 1)
                apart(pool)
                for j in range(GROUP):
                    pool.indirect_dma_start(out=out_rows, out_offset=bass.IndirectOffsetOnAxis(
                        ap=idx_s[p][:, j:j + 1].bitcast(U32), axis=0),
                        in_=yo[p][:, j, :], in_offset=None, compute_op=ALU.add).then_inc(scattered, 16)

            pool.wait_ge(idx_loaded, 16)
            gather(0, 0)
            gather(1, 1)
            for s in base_stored:
                pool.wait_ge(s, 16 * (GROUPS // 2))

            def turn(e, p):
                gather(e + 1, 1 - p)
                scatter(e - 1, 1 - p)

            turn(1, 1)
            with by_two(pool, 2, EXPERTS - 2) as e:
                turn(e, 0)
                turn(e + 1, 1)
            turn(EXPERTS - 2, 0)
            scatter(EXPERTS - 2, 0)
            scatter(EXPERTS - 1, 1)

        @block.scalar
        def _(act):
            for k in range(KC):
                act.dma_start(mix_in[:, k, :], w_l[k * HALF:(k + 1) * HALF, :].unsqueeze(1)
                              .to_broadcast([HALF, HD, HEADS])).then_inc(mix_in_loaded, 16)
            act.dma_start(bl_row[HC:HC + 1, :], b_l).then_inc(mix_in_loaded, 16)
            act.wait_ge(const_pool, CONSTS)
            act.wait_ge(const_dve, 8)

            def exponentials(t, p, b):
                act.wait_ge(max_ready, 2 * upto(t, -1) + (b + 1))
                for g in range(HALF):
                    h = HALF * b + g
                    ins = nc.scalar.activation(prob[p][:, h, :], ps_s[b][0:SP_, g * WIN:(g + 1) * WIN], ACT.Exp,
                                               bias=minus_max[p][:, h:h + 1], accum_out=ssum[p][:, h:h + 1])
                return ins

            def step(i, par):
                if live(i, 1):
                    t, p = i + 1, (par + 1) % 2
                    act.wait_ge(hnT_mm, upto(t, 0))
                    count_ge(act, v_mm, upto(t, -2))
                    for k in range(KC):
                        ins = nc.scalar.copy(
                            hnT[p][0:HC, k, :, 0:2 * WIN].rearrange("p s (a m) -> p s a m", a=2),
                            ps_hT[:, k, :].rearrange("p (s m) -> p s m", s=SEQS)
                            .unsqueeze(2).to_broadcast([HC, SEQS, 2, WIN]))
                    ins.then_inc(hnT_ready, 1)
                if live(i, 0):
                    t, p = i, par
                    count_ge(act, pt_mm, upto(t, -2))
                    count_ge(act, recip_ready, upto(t, -2))
                    exponentials(t, p, 0)
                if live(i, 0):
                    exponentials(i, par, 1).then_inc(exp_done, 1)
                if live(i, -2):
                    t = i - 2
                    act.wait_ge(hn2T_mm, upto(t, 0))
                    nc.scalar.copy(hn2T[:, :, bass.ds(t * TT, TT)], ps_hT).then_inc(hn2T_ready, 1)
                if live(i, 1):
                    t, p = i + 1, (par + 1) % 2
                    act.wait_ge(qk_mm, upto(t, 0))
                    count_ge(act, ks0_ready, upto(t, -2))
                    count_ge(act, ks1_ready, upto(t, -2))
                    nc.scalar.copy(kT[p][:], ps_qk[:, 2:4, :]).then_inc(k_ready, 1)
                    count_ge(act, s_mm, 2 * upto(t, -2))
                    nc.scalar.mul(qT[p][0:HC], ps_qk[:, 0:2, :], float(HD) ** -0.5).then_inc(q_ready, 1)
                if live(i, -3):
                    t, p = i - 3, (par + 1) % 2
                    act.wait_ge(sct_mm, upto(t, 0))
                    nc.scalar.copy(row[p][:, C:ROW], ps_sct).then_inc(row_ready, 1)
                if live(i, 1):
                    t, p = i + 1, (par + 1) % 2
                    act.wait_ge(v_mm, upto(t, 0))
                    count_ge(act, vs0_ready, upto(t, -2))
                    count_ge(act, vs1_ready, upto(t, -2))
                    nc.scalar.copy(v_sb[p][:], ps_v).then_inc(v_ready, 1)
                if live(i, 2):
                    t, p = i + 2, par
                    act.wait_ge(pool_mm, upto(t, 0))
                    count_ge(act, pool_seq, 5 * upto(t, -2))
                    nc.scalar.activation(tanh_d[p][:], ps_pool, ACT.Tanh, scale=0.5).then_inc(pool_tanh, 1)
                if live(i, -1):
                    t, p = i - 1, (par + 1) % 2
                    act.wait_ge(o_mm, upto(t, 0))
                    count_ge(act, oT_mm, upto(t, -2))
                    nc.scalar.copy(o_sb[p][:], ps_o).then_inc(o_ready, 1)
                if live(i, -2):
                    t, p = i - 2, par
                    act.wait_ge(gate_mm, upto(t, 0))
                    count_ge(act, sct_mm, upto(t, -2))
                    if not (isinstance(t, int) and t < 2):
                        act.wait_ge(row_stored[p], stored_of(t, p, -2))
                    nc.scalar.activation(scoreT[p][:], ps_gate, ACT.Tanh, scale=0.5).then_inc(gate_tanh, 1)
                if live(i, -1):
                    t, p = i - 1, (par + 1) % 2
                    act.wait_ge(oT_mm, upto(t, 0))
                    count_ge(act, r_mm, upto(t, -2))
                    for s in range(SEQS):
                        ins = nc.scalar.copy(oT[p][0:HC, :, s * WIN:(s + 1) * WIN],
                                             ps_oT[:, :, s * SECOND:s * SECOND + WIN])
                    ins.then_inc(oT_ready, 1)
                if live(i, 0):
                    t, p = i, par
                    act.wait_ge(pt_mm, upto(t, 0))
                    count_ge(act, o_mm, upto(t, -2))
                    for b in range(2):
                        ins = nc.scalar.copy(probT[p][0:2 * WIN, 3 * b:3 * b + 3, :],
                                             ps_pt[b][0:2 * WIN, 0:3 * SP_].rearrange("p (a n) -> p a n", a=3))
                    ins.then_inc(probT_ready, 1)
                if live(i, -2):
                    t, p = i - 2, par
                    act.wait_ge(gate_tanh, upto(t, 0))
                    nc.scalar.activation(scoreT[p][:], scoreT[p][:], ACT.Copy, bias=0.5, scale=0.5
                                         ).then_inc(score_ready, 1)

            pipeline(act, step)
            attention_over(act)

            def shared_silu(n, b):
                act.wait_ge(sh_g_mm, n + 1)
                count_ge(act, sh_act, n - 1)
                nc.scalar.activation(silu[b][:], ps_g[b][:, 0:GT], ACT.Silu).then_inc(sh_silu, 1)

            for n in range(2):
                shared_silu(n, n)
            with by_two(act, 2, FC_SH * SPLIT_GROUP - 1) as n:
                shared_silu(n, 0)
                shared_silu(n + 1, 1)
            shared_silu(FC_SH * SPLIT_GROUP - 1, 0)

            def split_high(e, p, m):
                act.wait_ge(in_loaded, 48 * e + 48)
                count_ge(act, u_mm, FC_EXP * (e - 1))
                nc.scalar.copy(w_hi[p][:, m], raw_in[:, m]).then_inc(w_hi_ready, 1)

            act.wait_ge(ids_mm, 1)
            split_high(0, 0, 0)
            split_high(0, 0, 1)
            for n in range(FC_SH * SPLIT_GROUP, FC_SH * GROUPS):
                shared_silu(n, n % 2)

            def split_down(e, p):
                act.wait_ge(down_loaded, 16 * e + 16)
                count_ge(act, y_mm, GROUP * (e - 1))
                nc.scalar.copy(w_down[p][:, :, 0, :], raw_down[:]).then_inc(down_hi_ready, 1)

            def x_high(e, p):
                act.wait_ge(xgT_mm, e + 1)
                count_ge(act, u_mm, FC_EXP * (e - 1))
                nc.scalar.copy(x_hi[p][:], ps_x[0][0:MAIN, 0:CAP]).then_inc(x_hi_ready, 1)
                nc.scalar.copy(x_rem[p][0:REM], ps_x[1][0:REM, 0:CAP]).then_inc(x_hi_ready, 1)

            def expert_silu(e, f):
                act.wait_ge(g_mm, FC_EXP * e + (f + 1))
                count_ge(act, act_ready, FC_EXP * e + (f - 1))
                nc.scalar.activation(silu[f % 2][:], ps_g[f % 2][:, 0:CAP], ACT.Silu).then_inc(silu_ready, 1)

            def act_high(e, p, f):
                act.wait_ge(act_ready, FC_EXP * e + (f + 1))
                if f == 0:
                    count_ge(act, y_mm, GROUP * (e - 1))
                nc.scalar.copy(act_hi[p][:, f, :], act_full[f % 2]).then_inc(act_hi_ready, 1)

            def expert(e, p, last=False):
                expert_silu(e, 0)
                expert_silu(e, 1)
                act_high(e, p, 0)
                act_high(e, p, 1)
                if not last:
                    split_high(e + 1, 1 - p, 0)
                    split_high(e + 1, 1 - p, 1)
                expert_silu(e, 2)
                expert_silu(e, 3)
                act_high(e, p, 2)
                if not last:
                    split_down(e + 1, 1 - p)
                    x_high(e + 1, 1 - p)
                expert_silu(e, 4)
                act_high(e, p, 3)
                expert_silu(e, 5)
                act_high(e, p, 4)
                act_high(e, p, 5)

            split_down(0, 0)
            act.wait_ge(sh_base, 2 * GROUPS)
            act.wait_ge(sh_act, FC_SH * GROUPS)
            act.wait_ge(sh_y_mm, 2 * GROUPS)
            x_high(0, 0)
            expert(0, 0)
            expert(1, 1)
            with by_two(act, 2, EXPERTS - 2) as e:
                expert(e, 0)
                expert(e + 1, 1)
            expert(EXPERTS - 2, 0)
            expert(EXPERTS - 1, 1, last=True)

        @block.vector
        def _(dve):
            def loaded_of(t, p):
                return 32 * ((t - p) // 2 + 1) if isinstance(t, int) else 16 * t + 16 * (2 - p)

            def difference(t, p):
                dve.wait_ge(x_loaded[p], loaded_of(t, p))
                count_ge(dve, pool_mm, upto(t, -2))
                dve.tensor_tensor(dT[p][:], xT_in[p][:, :, 0, :], xT_in[p][:, :, 1, :],
                                  ALU.subtract).then_inc(dT_ready, 1)

            def variance(stats, seq, n, var_ready):
                dve.wait_ge(seq, n)
                apart(dve)
                dve.bn_aggr(stats[:, 6:8], stats[:, 0:6]).then_inc(seq, 1)
                dve.wait_ge(seq, n + 1)
                dve.tensor_scalar(stats[:, 8:9], stats[:, 7:8], LN_EPS, None, ALU.add).then_inc(var_ready, 1)

            def normalised(dst, src, stats, rstd):
                return dve.tensor_scalar(dst, src, stats[:, 6:7], rstd[:, 0:1], ALU.subtract, ALU.mult)

            def scaled_keys(t, p):
                if isinstance(t, int) and t < 2:
                    dve.wait_ge(mix_in_loaded, 16 * (KC + 1))
                    dve.tensor_copy(ks[p][HC:HC + 1, 0], bl_row[HC:HC + 1, :].unsqueeze(2)
                                    .to_broadcast([1, HEADS, TT]))
                dve.wait_ge(k_ready, upto(t, 0))
                count_ge(dve, s_mm, 2 * upto(t, -2))
                dve.tensor_tensor(ks[p][0:HC, 0], kT[p][:, 0, :].unsqueeze(1).to_broadcast([HC, HEADS, TT]),
                                  mix_in[:, 0, :].unsqueeze(2).to_broadcast([HC, HEADS, TT]),
                                  ALU.mult).then_inc(ks0_ready, 1)

            for p in range(2):
                dve.memset(hnT[p][HC:HC + 1, 0, :, 0:2 * WIN], 1.0).then_inc(const_dve, 1)
                dve.memset(hnT[p][HC:HC + 1, 0, :, 2 * WIN:VR], float(WIN)).then_inc(const_dve, 1)
                dve.memset(qT[p][HC:HC + 1, 0], 1.0).then_inc(const_dve, 1)
                dve.memset(oT[p][HC:HC + 1, 0], 1.0).then_inc(const_dve, 1)

            def greatest(p, b):
                dve.tensor_reduce(minus_max[p][:, HALF * b:HALF * (b + 1)],
                                  ps_s[b][0:SP_, 0:HALF * WIN].rearrange("p (g m) -> p g m", m=WIN),
                                  AX.X, ALU.max, negate=True).then_inc(max_ready, 1)

            def step(i, par):
                tr, m = i - 2, 3 * upto(i - 2, -1)
                h_out = h_all[:, bass.ds(tr, 1), :].rearrange("p a c -> p (a c)") if live(i, -2) else None
                if live(i, -2):
                    dve.wait_ge(r_mm, upto(tr, 0))
                    dve.tensor_tensor(h_out, h_out, ps_r, ALU.add).then_inc(res_seq, 1)
                    dve.wait_ge(res_seq, m + 1)
                    apart(dve)
                    dve.bn_stats(stats2[:, 0:6], h_out).then_inc(res_seq, 1)
                if live(i, 0):
                    t, p = i, par
                    dve.wait_ge(s_mm, 2 * upto(t, -1) + 1)
                    count_ge(dve, exp_done, upto(t, -2))
                    greatest(p, 0)
                if live(i, -2):
                    variance(stats2, res_seq, m + 2, var2_ready)
                if live(i, 3):
                    difference(i + 3, (par + 1) % 2)
                if live(i, 0):
                    dve.wait_ge(s_mm, 2 * upto(i, 0))
                    greatest(par, 1)
                if live(i, -2):
                    count_ge(dve, hn2T_mm, upto(tr, -2))
                    if not (isinstance(tr, int) and tr < 2):
                        dve.wait_ge(row_stored[par], stored_of(tr, par, -2))
                    dve.wait_ge(rstd2_ready, upto(tr, 0))
                    normalised(row[par][:, 0:C], h_out, stats2, rstd2[par]).then_inc(hn2_ready, 1)
                if live(i, 1):
                    t, p = i + 1, (par + 1) % 2
                    dve.wait_ge(hnT_ready, upto(t, 0))
                    dve.tensor_reduce(hnT[p][0:HC, :, :, VR - 1], hnT[p][0:HC, :, :, 0:WIN], AX.X,
                                      ALU.add).then_inc(hsum_ready, 1)
                tp, n = i + 2, 5 * upto(i + 2, -1)
                h_in = h_all[:, bass.ds(tp, 1), :].rearrange("p a c -> p (a c)") if live(i, 2) else None
                if live(i, 2):
                    dve.wait_ge(x_loaded[par], loaded_of(tp, par))
                    dve.tensor_tensor(diff[:], xp_in[par][:, 0, :], xp_in[par][:, 1, :],
                                      ALU.subtract).then_inc(pool_seq, 1)
                if live(i, 0):
                    dve.wait_ge(v_ready, upto(i, 0))
                    if isinstance(i, int) and i == 0:
                        dve.wait_ge(mix_out_loaded, 48)
                    count_ge(dve, o_mm, upto(i, -2))
                    scale_values(dve, par, 1).then_inc(vs1_ready, 1)
                if live(i, 0):
                    dve.wait_ge(exp_done, upto(i, 0))
                    dve.reciprocal(ssum[par][:], ssum[par][:]).then_inc(recip_ready, 1)
                    dve.wait_ge(recip_ready, upto(i, 0))
                    dve.tensor_tensor(prob[par][:], prob[par][:],
                                      ssum[par][:].unsqueeze(2).to_broadcast([SP_, HEADS, WIN]),
                                      ALU.mult).then_inc(prob_ready, 1)
                if live(i, 1):
                    scaled_keys(i + 1, (par + 1) % 2)
                if live(i, 2):
                    dve.wait_ge(pool_seq, n + 1)
                    dve.wait_ge(pool_tanh, upto(tp, 0))
                    dve.scalar_tensor_tensor(out=diff[:], in0=tanh_d[par][:], scalar=1.0, in1=diff[:],
                                             op0=ALU.add, op1=ALU.mult).then_inc(pool_seq, 1)
                    dve.wait_ge(pool_seq, n + 2)
                    dve.scalar_tensor_tensor(out=h_in, in0=diff[:], scalar=0.5, in1=xp_in[par][:, 1, :],
                                             op0=ALU.mult, op1=ALU.add).then_inc(pool_seq, 1)
                    dve.wait_ge(pool_seq, n + 3)
                    apart(dve)
                    dve.bn_stats(stats1[:, 0:6], h_in).then_inc(pool_seq, 1)
                    variance(stats1, pool_seq, n + 4, var1_ready)
                    count_ge(dve, hnT_mm, upto(tp, -2))
                    dve.wait_ge(rstd1_ready, upto(tp, 0))
                    normalised(hn[par][:], h_in, stats1, rstd1[par]).then_inc(hn_ready, 1)

            pipeline(dve, step)
            attention_over(dve)

            dve.memset(thr[:], 0).then_inc(find_seq, 1)
            for k in range(3):
                dve.memset(bits[:, k:k + 1], (k + 1) << (2 * SEARCH - 2)).then_inc(find_seq, 1)
            dve.wait_ge(find_seq, 4)
            dve.wait_ge(score_loaded, 16 * SPREAD)

            def try_bits(s):
                dve.tensor_tensor(cand[:], thr[:].to_broadcast([128, 3]), bits[:], ALU.bitwise_or
                                  ).then_inc(find_seq, 1)
                dve.wait_ge(find_seq, 7 * s + 5)
                for k, unused in enumerate((above, equal, picked)):
                    dve.tensor_scalar(unused[:], score[:], cand[:, k:k + 1].bitcast(F32), 0.0, ALU.is_ge, ALU.add,
                                      accum_out=count[:, k:k + 1]).then_inc(counted, 1)

            def keep_bits(s):
                dve.wait_ge(count_sum, s + 1)
                dve.tensor_scalar(enough[:], ps_x[0][:, 8:11], float(CAP), None, ALU.is_ge).then_inc(find_seq, 1)
                for k in range(3):
                    dve.wait_ge(find_seq, 7 * s + 6 + k)
                    dve.copy_predicated(thr[:], enough[:, k:k + 1], cand[:, k:k + 1]).then_inc(find_seq, 1)
                dve.tensor_scalar(bits[:], bits[:], 2, None, ALU.logical_shift_right).then_inc(find_seq, 1)
                dve.wait_ge(find_seq, 7 * s + 10)
                dve.engine_nop().then_inc(find_seq, 1)
                dve.wait_ge(find_seq, 7 * s + 11)

            def shared_act(n, b, p, f):
                dve.wait_ge(sh_silu, n + 1)
                dve.wait_ge(sh_u_mm, n + 1)
                dve.tensor_tensor(act_sh[p][:, f, :], silu[b][:], ps_u[b][:, 0:GT], ALU.mult).then_inc(sh_act, 1)

            def shared_out(g, p, half):
                dve.wait_ge(sh_y_mm, 2 * g + half + 1)
                dve.tensor_tensor(base[p][:, 2 * half:2 * half + 2, :],
                                  h_all[:, bass.ds(GROUP * g + 2 * half, 2), :],
                                  ps_y[half][0:TT, 0:2 * C].rearrange("p (j c) -> p j c", c=C),
                                  ALU.add).then_inc(sh_base, 1)

            def free_base(g, p):
                if g >= 2:
                    dve.wait_ge(base_stored[p], 16 * (g // 2))

            def shared_group(g, slot):
                n, p = FC_SH * g, g % 2
                b = n % 2
                if g >= 2:
                    dve.wait_ge(sh_y_mm, 2 * g - 2)
                slot(0)
                slot(1)
                shared_act(n, b, p, 0)
                slot(2)
                slot(3)
                if g > 0:
                    free_base(g - 1, 1 - p)
                    shared_out(g - 1, 1 - p, 0)
                    shared_out(g - 1, 1 - p, 1)
                slot(4)
                slot(5)
                shared_act(n + 1, 1 - b, p, 1)
                slot(6)
                slot(7)
                shared_act(n + 2, b, p, 2)

            for g in range(SEARCH_GROUPS):
                def search(k):
                    if k // 2 < PER_GROUP:
                        (try_bits, keep_bits)[k % 2](PER_GROUP * g + k // 2)
                shared_group(g, search)

            dve.wait_ge(const_pool, CONSTS + TABLE_STEPS)
            thr_f = thr[:].bitcast(F32)
            dve.tensor_scalar(above[:], score[:], thr_f, 0.0, ALU.is_gt, ALU.add,
                              accum_out=totals[:, 0:1]).then_inc(route_seq, 1)
            dve.tensor_scalar(equal[:], score[:], thr_f, 0.0, ALU.is_equal, ALU.add,
                              accum_out=totals[:, 1:2]).then_inc(totals_ready, 1)
            dve.wait_ge(totals_ready, 1)
            dve.tensor_tensor_scan(scan[:], equal[:], zeros[:], 0.0, ALU.add, ALU.add).then_inc(route_seq, 1)

            def route(k):
                if k == 1:
                    dve.wait_ge(eq_mm, 1)
                    dve.tensor_scalar(room[:, 0:1], ps_x[0][:, 1:2], -1.0, float(CAP), ALU.mult, ALU.add
                                      ).then_inc(route_seq, 1)
                    dve.wait_ge(route_seq, 3)
                    dve.tensor_tensor(room[:, 1:2], room[:, 0:1], ps_x[0][:, 3:4],
                                      ALU.subtract).then_inc(route_seq, 1)
                    dve.wait_ge(route_seq, 4)
                    dve.scalar_tensor_tensor(out=equal[:], in0=scan[:], scalar=room[:, 1:2], in1=equal[:],
                                             op0=ALU.is_le, op1=ALU.mult).then_inc(route_seq, 1)
                    dve.wait_ge(route_seq, 5)
                    dve.tensor_tensor(picked[:], above[:], equal[:], ALU.add).then_inc(route_seq, 1)
                    dve.wait_ge(route_seq, 6)
                    dve.tensor_tensor_scan(scan[:], picked[:], zeros[:], 0.0, ALU.add, ALU.add
                                           ).then_inc(route_seq, 1)
                    dve.wait_ge(route_seq, 7)
                    dve.tensor_copy(room[:, 2:3], scan[:, CAP - 1:CAP]).then_inc(sel_total, 1)
                if k == 4:
                    dve.wait_ge(sel_mm, 1)
                    dve.scalar_tensor_tensor(out=above[:], in0=scan[:], scalar=ps_x[0][:, 4:5], in1=picked[:],
                                             op0=ALU.add, op1=ALU.mult).then_inc(pos_ready, 1)
                if k == 6:
                    dve.wait_ge(posT_mm, 1)
                    dve.tensor_scalar(pos_i[:].rearrange("p (c j e) -> p j c e", j=GROUP, e=EXPERTS),
                                      ps_x[1][0:TT, :].rearrange("p (j c e) -> p j c e", j=GROUP, e=EXPERTS),
                                      -1.0, None, ALU.add).then_inc(route_seq, 1)
                    dve.wait_ge(route_seq, 8)
                    dve.tensor_scalar(pos_j[:], pos_i[:], 4, None, ALU.arith_shift_right).then_inc(route_seq, 1)
                    dve.tensor_scalar(pos_i[:], pos_i[:], LO - 1, None, ALU.bitwise_and).then_inc(route_seq, 1)
                if k == 7:
                    dve.wait_ge(route_seq, 10)
                    dve.tensor_copy(pos_hi[:], pos_j[:]).then_inc(route_seq, 1)
                    dve.tensor_copy(pos_lo[:], pos_i[:]).then_inc(route_seq, 1)

            shared_group(ROUTE_GROUP, route)
            dve.wait_ge(route_seq, 12)

            def one_hot(k):
                for l in range(2 * k, 2 * k + 2):
                    dve.tensor_scalar(hot_id[:, 0, l, :], pos_lo[:], float(l), None,
                                      ALU.is_equal).then_inc(hot_lo_ready, 1)
                    dve.tensor_scalar(hot_id[:, 1, l, :], pos_lo[:], float(l), iota_p[:, 0:1],
                                      ALU.is_equal, ALU.mult)
                for h in range(4 * k, min(4 * k + 4, HI)):
                    ins = dve.tensor_scalar(hot_hi[:, h, :], pos_hi[:], float(h), None, ALU.is_equal)
                ins.then_inc(hot_ready, 1)
                for l in range(max(2 * k, LO - LO_DVE), 2 * k + 2):
                    dve.wait_ge(hot_lo_ready, l + 1)
                    dve.tensor_tensor(hot_id[:, 0, l, :], hot_id[:, 0, l, :], iota_t[:].rearrange("p t e -> p (t e)"),
                                      ALU.mult).then_inc(hot_tile_ready, 1)

            shared_group(HOT_GROUP, one_hot)
            dve.wait_ge(ids_mm, 1)
            ids_view = ps_x[0][0:HI, :].rearrange("p (e a l) -> p e a l", a=2, l=LO)
            dve.tensor_scalar(id_part[:], ids_view[:, :, 0, :], float(TT), None, ALU.mult).then_inc(route_seq, 1)
            dve.wait_ge(route_seq, 13)
            dve.tensor_tensor(ids[:], id_part[:], ids_view[:, :, 1, :], ALU.add).then_inc(ids_ready, 1)

            def split_low(e, p, piece):
                if piece < 4:
                    m, half = divmod(piece, 2)
                    dve.wait_ge(w_hi_ready, 2 * e + (m + 1))
                    count_ge(dve, u_mm, FC_EXP * (e - 1))
                    dve.tensor_tensor(w_lo[p][:, m, half, :], raw_in[:, m, half, :],
                                      w_hi[p][:, m, half, :].bitcast(F32), ALU.subtract).then_inc(w_lo_ready, 1)
                else:
                    rows = slice(3 * (piece - 4), 3 * (piece - 3))
                    dve.wait_ge(down_hi_ready, e + 1)
                    count_ge(dve, y_mm, GROUP * (e - 1))
                    dve.tensor_tensor(w_down[p][:, rows, 1, :], raw_down[:, rows, :],
                                      w_down[p][:, rows, 0, :].bitcast(F32), ALU.subtract
                                      ).then_inc(down_lo_ready, 1)

            def first_weights(k):
                if k % 2 == 1:
                    split_low(0, 0, k // 2)

            def nothing(k):
                pass

            shared_group(SPLIT_GROUP, first_weights)
            free_base(7, 1)
            shared_out(7, 1, 0)
            shared_out(7, 1, 1)
            for piece in range(IN_PIECES, IN_PIECES + DOWN_PIECES):
                split_low(0, 0, piece)

            def x_low(e, p):
                dve.wait_ge(x_hi_ready, 2 * e + 2)
                count_ge(dve, u_mm, FC_EXP * (e - 1))
                dve.tensor_tensor(x_lo[p][:], ps_x[0][0:MAIN, 0:CAP], x_hi[p][:].bitcast(F32),
                                  ALU.subtract).then_inc(x_lo_ready, 1)
                dve.tensor_tensor(x_rem[p][REM:2 * REM], ps_x[1][0:REM, 0:CAP], x_rem[p][0:REM].bitcast(F32),
                                  ALU.subtract).then_inc(x_lo_ready, 1)

            def take_scores(e, p):
                dve.wait_ge(gathered[p], 32 * e - 32 * p + 64)
                count_ge(dve, yo_ready, GROUP * (e - 1))
                dve.tensor_copy(top[p][:], xg[p][:, :, bass.ds(e + C, 1)].rearrange("p j a -> p (j a)")
                                ).then_inc(top_ready, 1)

            def expert_out(e, p, j):
                if j == 0:
                    count_ge(dve, scattered, 64 * (e - 1))
                    dve.wait_ge(top_ready, e + 1)
                dve.wait_ge(y_mm, GROUP * e + (j + 1))
                count_ge(dve, yo_ready, GROUP * e + j)
                y = ps_y[j % 2][0:SLOTS]
                dve.tensor_scalar(scaled[:], y[:, 0:C], top[p][:, j:j + 1], None, ALU.mult).then_inc(scaled_ready, 1)
                dve.wait_ge(scaled_ready, GROUP * e + (j + 1))
                dve.scalar_tensor_tensor(out=yo[p][:, j, :], in0=y[:, C:2 * C], scalar=top[p][:, j:j + 1],
                                         in1=scaled[:], op0=ALU.mult, op1=ALU.add).then_inc(yo_ready, 1)

            def expert_act(e, f):
                dve.wait_ge(silu_ready, FC_EXP * e + (f + 1))
                dve.wait_ge(u_mm, FC_EXP * e + (f + 1))
                count_ge(dve, act_lo_ready, FC_EXP * e + (f - 1))
                dve.tensor_tensor(act_full[f % 2], silu[f % 2][:], ps_u[f % 2][:, 0:CAP],
                                  ALU.mult).then_inc(act_ready, 1)

            def act_low(e, p, f):
                dve.wait_ge(act_hi_ready, FC_EXP * e + (f + 1))
                if f == 0:
                    count_ge(dve, y_mm, GROUP * (e - 1))
                dve.tensor_tensor(act_lo[p][:, f, :], act_full[f % 2], act_hi[p][:, f, :].bitcast(F32),
                                  ALU.subtract).then_inc(act_lo_ready, 1)

            def expert(e, p, first=False, last=False):
                def weights(piece):
                    if not last:
                        split_low(e + 1, 1 - p, piece)

                def rows_out(j):
                    if not first:
                        expert_out(e - 1, 1 - p, j)
                take_scores(e, p)
                expert_act(e, 0)
                expert_act(e, 1)
                act_low(e, p, 0)
                act_low(e, p, 1)
                rows_out(0)
                weights(0)
                rows_out(1)
                weights(1)
                rows_out(2)
                weights(2)
                rows_out(3)
                weights(3)
                expert_act(e, 2)
                expert_act(e, 3)
                act_low(e, p, 2)
                weights(4)
                if not last:
                    x_low(e + 1, 1 - p)
                act_low(e, p, 3)
                expert_act(e, 4)
                weights(5)
                expert_act(e, 5)
                act_low(e, p, 4)
                act_low(e, p, 5)

            x_low(0, 0)
            expert(0, 0, first=True)
            expert(1, 1)
            with by_two(dve, 2, EXPERTS - 2) as e:
                expert(e, 0)
                expert(e + 1, 1)
            expert(EXPERTS - 2, 0)
            expert(EXPERTS - 1, 1, last=True)
            for j in range(GROUP):
                expert_out(EXPERTS - 1, 1, j)

        @block.tensor
        def _(pe):
            pe.wait_ge(tok_loaded, 16)
            pe.wait_ge(const_dve, 8)
            pe.wait_ge(const_pool, CONSTS)

            def product(out, pairs, sync=None):
                for n, (lhsT, rhs) in enumerate(pairs):
                    ins = nc.tensor.matmul(out, lhsT, rhs, start=(n == 0), stop=(n == len(pairs) - 1))
                return ins

            def mixed_scores(p, b):
                g0 = HALF * b
                for s in range(SEQS):
                    rows = slice(0, SECOND) if s == 0 else slice(WIN, TT)
                    keys = slice(s * WIN, (s + 1) * WIN)
                    at = slice(0, SECOND) if s == 0 else slice(SECOND, SP_)
                    ins = product(ps_s[b][at, 0:HALF * WIN].rearrange("p (g m) -> p g m", m=WIN), [
                        (qT[p][0:HC + 1, 0, rows], ks[p][0:HC + 1, 0, g0:g0 + HALF, keys]),
                        (qT[p][0:HC, 1, rows], ks[p][0:HC, 1, g0:g0 + HALF, keys])])
                ins.then_inc(s_mm, 1)

            def step(i, par):
                if live(i, 0):
                    t, p = i, par
                    pe.wait_ge(q_ready, upto(t, 0))
                    pe.wait_ge(ks0_ready, upto(t, 0))
                    pe.wait_ge(ks1_ready, upto(t, 0))
                    count_ge(pe, exp_done, upto(t, -1))
                    count_ge(pe, gate_tanh, upto(t, -3))
                    mixed_scores(p, 0)
                if live(i, 1):
                    t, p = i + 1, (par + 1) % 2
                    pe.wait_ge(hn_ready, upto(t, 0))
                    pe.wait_ge(pool_tanh, upto(t, 0))
                    for k in range(KC):
                        ins = nc.tensor.transpose(ps_hT[:, k, :], hn[p][:, k * HC:(k + 1) * HC], ident[0:TT, 0:TT])
                    ins.then_inc(hnT_mm, 1)
                if live(i, 0):
                    mixed_scores(par, 1)
                if live(i, 1):
                    t, p = i + 1, (par + 1) % 2
                    pe.wait_ge(hnT_ready, upto(t, 0))
                    if isinstance(t, int) and t == 0:
                        pe.wait_ge(qkv_loaded, 32)
                    count_ge(pe, q_ready, upto(t, -1))
                    count_ge(pe, k_ready, upto(t, -1))
                    for a in range(4):
                        cols = slice(a * HC, (a + 1) * HC)
                        ins = product(ps_qk[:, a, :], [
                            (w_qkv_sb[0:HC + 1, 0, cols], hnT[p][0:HC + 1, 0, :, 0:WIN]),
                            (w_qkv_sb[0:HC, 1, cols], hnT[p][0:HC, 1, :, 0:WIN])])
                    ins.then_inc(qk_mm, 1)
                if live(i, -2):
                    t, p = i - 2, par
                    pe.wait_ge(hn2_ready, upto(t, 0))
                    count_ge(pe, hnT_ready, upto(t, 3))
                    count_ge(pe, hn2T_ready, upto(t, -1))
                    for k in range(KC):
                        ins = nc.tensor.transpose(ps_hT[:, k, :], row[p][:, k * HC:(k + 1) * HC], ident[0:TT, 0:TT])
                    ins.then_inc(hn2T_mm, 1)
                if live(i, -3):
                    t, p = i - 3, (par + 1) % 2
                    pe.wait_ge(score_ready, upto(t, 0))
                    count_ge(pe, row_ready, upto(t, -1))
                    count_ge(pe, res_seq, 3 * upto(t, 1))
                    apart(pe)
                    nc.tensor.transpose(ps_sct, scoreT[p][:], ident[0:EXPERTS, 0:EXPERTS]).then_inc(sct_mm, 1)
                if live(i, 1):
                    t, p = i + 1, (par + 1) % 2
                    pe.wait_ge(hsum_ready, upto(t, 0))
                    count_ge(pe, v_ready, upto(t, -1))
                    for s in range(SEQS):
                        cols = slice(2 * C, 3 * C)
                        lhs = [hnT[p][0:n, k, s] for k, n in ((0, HC + 1), (1, HC))]
                        ins = product(ps_v[:, s, :], [(lhs[0], w_qkv_sb[0:HC + 1, 0, cols]),
                                                      (lhs[1], w_qkv_sb[0:HC, 1, cols])])
                    ins.then_inc(v_mm, 1)
                if live(i, 2):
                    t, p = i + 2, par
                    pe.wait_ge(dT_ready, upto(t, 0))
                    count_ge(pe, pool_tanh, upto(t, -1))
                    count_ge(pe, hnT_ready, upto(t, -1))
                    count_ge(pe, hn2T_ready, upto(t, -4))
                    product(ps_pool, [(dT[p][:, k, :], w_tok_sb[:, k, :]) for k in range(KC)]).then_inc(pool_mm, 1)
                if live(i, -1):
                    t, p = i - 1, (par + 1) % 2
                    pe.wait_ge(probT_ready, upto(t, 0))
                    pe.wait_ge(vs0_ready, upto(t, 0))
                    pe.wait_ge(vs1_ready, upto(t, 0))
                    count_ge(pe, oT_ready, upto(t, -1))
                    count_ge(pe, res_seq, 3 * upto(t, -1))
                    count_ge(pe, row_ready, upto(t, -2))
                    for j in range(PAIRS):
                        for s in range(SEQS):
                            n = VR if j == 0 else 2 * WIN
                            at = slice(s * SECOND, s * SECOND + (SECOND, WIN)[s])
                            ins = nc.tensor.matmul(ps_o[at, :], probT[p][0:n, j, at], vs[p][0:n, s, j, :],
                                                   start=(j == 0), stop=(j == PAIRS - 1))
                    ins.then_inc(o_mm, 1)
                if live(i, -2):
                    t = i - 2
                    pe.wait_ge(hn2T_ready, upto(t, 0))
                    if isinstance(t, int) and t == 0:
                        pe.wait_ge(ffn_loaded, 64)
                    count_ge(pe, gate_tanh, upto(t, -1))
                    if live(i, 0):
                        pe.wait_ge(exp_done, upto(i, 0))
                    product(ps_gate, [(w_gate_sb[:, k, :], hn2T[:, k, bass.ds(t * TT, TT)])
                                      for k in range(KC)]).then_inc(gate_mm, 1)
                if live(i, -1):
                    t, p = i - 1, (par + 1) % 2
                    pe.wait_ge(o_ready, upto(t, 0))
                    for k in range(KC):
                        ins = nc.tensor.transpose(ps_oT[:, k, :], o_sb[p][:, k * HC:(k + 1) * HC],
                                                  ident[0:SP_, 0:SP_])
                    ins.then_inc(oT_mm, 1)
                if live(i, 0):
                    t, p = i, par
                    pe.wait_ge(prob_ready, upto(t, 0))
                    count_ge(pe, probT_ready, upto(t, -1))
                    for j in range(PAIRS):
                        ins = nc.tensor.transpose(ps_pt[j // 3][0:2 * WIN, (j % 3) * SP_:(j % 3 + 1) * SP_],
                                                  prob[p][:, 2 * j:2 * j + 2, :].rearrange("p h m -> p (h m)"),
                                                  ident[0:SP_, 0:SP_])
                    ins.then_inc(pt_mm, 1)
                if live(i, -1):
                    t, p = i - 1, (par + 1) % 2
                    pe.wait_ge(oT_ready, upto(t, 0))
                    if isinstance(t, int) and t == 0:
                        pe.wait_ge(proj_loaded, 32)
                    count_ge(pe, res_seq, 3 * upto(t, -1))
                    product(ps_r, [(oT[p][0:HC + 1, 0, :], w_proj_sb[0:HC + 1, 0, :]),
                                   (oT[p][0:HC, 1, :], w_proj_sb[0:HC, 1, :])]).then_inc(r_mm, 1)

            pipeline(pe, step)
            for done in (exp_done, gate_tanh, probT_ready, q_ready, k_ready, v_ready, pool_tanh, hn2T_ready,
                         hnT_ready, o_ready, oT_ready, row_ready):
                pe.wait_ge(done, TILES)
            pe.wait_ge(res_seq, 3 * TILES)

            def shared_in(g, n, b, f, w, banks, done):
                cols = slice(f * 128, (f + 1) * 128)
                count_ge(pe, sh_act, n - 1)
                product(banks[b][:, 0:GT], [(w[:, k, cols], hn2T[:, k, bass.ds(g * GT, GT)])
                                            for k in range(KC)]).then_inc(done, 1)

            def shared_down(g, p, half):
                pe.wait_ge(sh_act, FC_SH * g + FC_SH)
                count_ge(pe, sh_base, 2 * g + half - 1)
                for j in range(2 * half, 2 * half + 2):
                    ins = product(ps_y[half][0:TT, (j % 2) * C:(j % 2 + 1) * C],
                                  [(act_sh[p][:, f, j * TT:(j + 1) * TT], wsd_sb[:, f, :]) for f in range(FC_SH)])
                ins.then_inc(sh_y_mm, 1)

            def shared_group(g, slot):
                n, p = FC_SH * g, g % 2
                b = n % 2
                shared_in(g, n, b, 0, wsg_sb, ps_g, sh_g_mm)
                slot(0)
                shared_in(g, n, b, 0, wsu_sb, ps_u, sh_u_mm)
                slot(1)
                if g > 0:
                    shared_down(g - 1, 1 - p, 0)
                slot(2)
                if g > 0:
                    shared_down(g - 1, 1 - p, 1)
                slot(3)
                shared_in(g, n + 1, 1 - b, 1, wsg_sb, ps_g, sh_g_mm)
                slot(4)
                shared_in(g, n + 1, 1 - b, 1, wsu_sb, ps_u, sh_u_mm)
                slot(5)
                shared_in(g, n + 2, b, 2, wsg_sb, ps_g, sh_g_mm)
                slot(6)
                shared_in(g, n + 2, b, 2, wsu_sb, ps_u, sh_u_mm)
                slot(7)

            for g in range(SEARCH_GROUPS):
                def search(k):
                    n = PER_GROUP * g + k // 2
                    if k % 2 == 1 and k // 2 < PER_GROUP:
                        if n == 0:
                            pe.wait_ge(const_pool, CONSTS + TABLE_STEPS)
                        pe.wait_ge(counted, 3 * n + 3)
                        nc.tensor.matmul(ps_x[0][:, 8:11], onehot_sum[:], count[:], start=True,
                                         stop=True).then_inc(count_sum, 1)
                shared_group(g, search)

            def route(k):
                if k == 0:
                    pe.wait_ge(totals_ready, 1)
                    pe.wait_ge(route_seq, 1)
                    nc.tensor.matmul(ps_x[0][:, 1:3], onehot_sum[:], totals[:], start=True, stop=True)
                    nc.tensor.matmul(ps_x[0][:, 3:4], before[:], totals[:, 1:2], start=True,
                                     stop=True).then_inc(eq_mm, 1)
                if k == 2:
                    pe.wait_ge(sel_total, 1)
                    nc.tensor.matmul(ps_x[0][:, 4:5], before[:], room[:, 2:3], start=True,
                                     stop=True).then_inc(sel_mm, 1)
                if k == 4:
                    pe.wait_ge(pos_ready, 1)
                    for j in range(GROUP):
                        ins = nc.tensor.transpose(ps_x[1][0:TT, j * 128:(j + 1) * 128],
                                                  above[:, j * TT:(j + 1) * TT], ident[:])
                    ins.then_inc(posT_mm, 1)

            def nothing(k):
                pass

            shared_group(ROUTE_GROUP, route)
            shared_group(HOT_GROUP, nothing)
            pe.wait_ge(hot_ready, 8)
            pe.wait_ge(hot_tile_ready, LO)
            for e in range(EXPERTS):
                for t in range(TILES):
                    te = t * EXPERTS + e
                    ins = nc.tensor.matmul(ps_x[0][0:HI, e * 2 * LO:(e + 1) * 2 * LO], hot_hi[:, :, te],
                                           hot_id[:, :, :, te].rearrange("p a l -> p (a l)"),
                                           start=(t == 0), stop=(t == TILES - 1))
            ins.then_inc(ids_mm, 1)
            shared_group(SPLIT_GROUP, nothing)
            shared_down(7, 1, 0)
            shared_down(7, 1, 1)

            def turn_in(e, p):
                pe.wait_ge(gathered[p], 32 * e - 32 * p + 64)
                count_ge(pe, x_lo_ready, 2 * e)
                for k, cols in ((0, slice(0, MAIN)), (1, slice(MAIN, C))):
                    for j in range(GROUP):
                        ins = nc.tensor.transpose(ps_x[k][0:cols.stop - cols.start, j * SLOTS:(j + 1) * SLOTS],
                                                  xg[p][:, j, cols], ident[0:SLOTS, 0:SLOTS])
                ins.then_inc(xgT_mm, 1)

            def expert_in(e, p, f):
                cols = slice(f * 128, (f + 1) * 128)
                count_ge(pe, act_ready, FC_EXP * e + (f - 1))
                for m, (banks, done) in enumerate(((ps_g, g_mm), (ps_u, u_mm))):
                    if f == 0:
                        pe.wait_ge(w_lo_ready, IN_PIECES * e + 2 * (m + 1))
                    product(banks[f % 2][:, 0:CAP], [
                        (w_hi[p][:, m, 0, cols], x_hi[p][:]), (w_hi[p][:, m, 0, cols], x_lo[p][:]),
                        (w_lo[p][:, m, 0, cols], x_hi[p][:]), (w_hi[p][:, m, 1, cols], x_rem[p][:]),
                        (w_lo[p][:, m, 1, cols], x_rem[p][:])]).then_inc(done, 1)

            def expert_down(e, p):
                pe.wait_ge(act_lo_ready, FC_EXP * e + FC_EXP)
                pe.wait_ge(down_lo_ready, DOWN_PIECES * (e + 1))
                for j in range(GROUP):
                    count_ge(pe, yo_ready, GROUP * e + (j - 1))
                    slots = slice(j * SLOTS, (j + 1) * SLOTS)
                    for f in range(FC_EXP):
                        nc.tensor.matmul(ps_y[j % 2][0:SLOTS, 0:2 * C], act_hi[p][:, f, slots],
                                         w_down[p][:, f].rearrange("p a c -> p (a c)"), start=(f == 0), stop=False)
                        ins = nc.tensor.matmul(ps_y[j % 2][0:SLOTS, C:2 * C], act_lo[p][:, f, slots],
                                               w_down[p][:, f, 0, :], start=False, stop=(f == FC_EXP - 1))
                    ins.then_inc(y_mm, 1)

            def expert(e, p, first=False, last=False):
                pe.wait_ge(x_lo_ready, 2 * e + 2)
                expert_in(e, p, 0)
                expert_in(e, p, 1)
                if not first:
                    expert_down(e - 1, 1 - p)
                expert_in(e, p, 2)
                expert_in(e, p, 3)
                if not last:
                    turn_in(e + 1, 1 - p)
                expert_in(e, p, 4)
                expert_in(e, p, 5)

            pe.wait_ge(ids_ready, 1)
            turn_in(0, 0)
            pe.wait_ge(sh_base, 2 * GROUPS)
            pe.wait_ge(sh_act, FC_SH * GROUPS)
            expert(0, 0, first=True)
            expert(1, 1)
            with by_two(pe, 2, EXPERTS - 2) as e:
                expert(e, 0)
                expert(e + 1, 1)
            expert(EXPERTS - 2, 0)
            expert(EXPERTS - 1, 1, last=True)
            expert_down(EXPERTS - 1, 1)


def kernel(x, L0_tok_w, L0_attn_w_qkv, L0_attn_b_qkv, L0_attn_w_l, L0_attn_b_l, L0_attn_w_w, L0_attn_b_w,
           L0_attn_w_proj, L0_attn_b_proj, L0_ffn_gate_weight, L0_ffn_Wg, L0_ffn_Wu, L0_ffn_Wd,
           L0_ffn_Ws_g, L0_ffn_Ws_u, L0_ffn_Ws_d):
    import numpy as np
    import concourse.bacc as bacc
    from concourse.bass_utils import run_bass_kernel_spmd

    frames = np.asarray(x)[:, :POOL * WIN]
    halves = frames.reshape(TILES, SEQS, WIN, POOL, KC, HC)
    gate_up = np.stack([np.asarray(L0_ffn_Wg), np.asarray(L0_ffn_Wu)]).transpose(1, 3, 0, 2)
    arrays = {
        "xT": halves.transpose(0, 5, 4, 3, 1, 2).reshape(TILES, HC, KC, POOL, TT),
        "xp": frames.reshape(TILES, TT, POOL, C),
        "w_tok": np.asarray(L0_tok_w),
        "w_qkv": np.asarray(L0_attn_w_qkv),
        "b_qkv": np.asarray(L0_attn_b_qkv).reshape(1, -1),
        "w_l": np.asarray(L0_attn_w_l),
        "b_l": np.asarray(L0_attn_b_l).reshape(1, -1),
        "w_w": np.asarray(L0_attn_w_w),
        "b_w": np.asarray(L0_attn_b_w).reshape(1, -1),
        "w_proj": np.asarray(L0_attn_w_proj),
        "b_proj": np.asarray(L0_attn_b_proj).reshape(1, -1),
        "w_gate": np.asarray(L0_ffn_gate_weight).T,
        "w_main": gate_up[:, :MAIN],
        "w_rem": gate_up[:, MAIN:],
        "wd": np.asarray(L0_ffn_Wd).transpose(0, 2, 1).reshape(EXPERTS, FC_EXP, 128, C).transpose(0, 2, 1, 3),
        "wsg": np.asarray(L0_ffn_Ws_g).T,
        "wsu": np.asarray(L0_ffn_Ws_u).T,
        "wsd": np.asarray(L0_ffn_Ws_d).T,
    }
    nc = bacc.Bacc("TRN2", target_bir_lowering=False, num_devices=1)
    feeds, args = {}, []
    for name, a in arrays.items():
        feeds[f"in_{name}"] = np.ascontiguousarray(a)
        args.append(nc.dram_tensor(f"in_{name}", feeds[f"in_{name}"].shape, F32, kind="ExternalInput").ap())
    args.append(nc.dram_tensor("out_h", (BATCH, WIN, C), F32, kind="ExternalOutput").ap())
    audio_tower(nc, *args)
    r = run_bass_kernel_spmd(nc, [feeds], core_ids=[0])
    return r.results[0]["out_h"]
```
